# Optimizing a Trainium2 kernel written in Bass

```python
import numpy as np
import jax
import jax.numpy as jnp

def _softmax(x, axis=-1):
    return jax.nn.softmax(x, axis=axis)

def _gelu(x):
    return jax.nn.gelu(x, approximate=True)

def _silu(x):
    return jax.nn.silu(x)

def _sigmoid(x):
    return jax.nn.sigmoid(x)

def _layernorm(x, axis=-1, eps=1e-05):
    m = jnp.mean(x, axis=axis, keepdims=True)
    v = jnp.var(x, axis=axis, keepdims=True)
    return (x - m) / jnp.sqrt(v + eps)

def _scatter_add(tgt, idx, src, axis=0):
    return tgt.at[idx].add(src)

def _segment_sum(src, seg, n):
    return jax.ops.segment_sum(src, seg, n)
kernel_name = 'mk_flamingo_gated_d2_seqx_r8_b286d2'

def setup_inputs(seed: int=0):
    np.random.seed(seed)
    _w = jnp.asarray

    def _rec_inputs():
        import jax
        import jax.numpy as jnp
        _rk = jax.random.key(seed)
        x = -0.0002928 + 1 * jax.random.normal(jax.random.fold_in(_rk, 1), (4, 256, 128), jnp.float32)
        _lenS = 256 - jax.random.randint(jax.random.fold_in(_rk, 7), (4,), 0, max(1, 256 // 4) + 1, jnp.int32)
        _lenS2 = 512 - jax.random.randint(jax.random.fold_in(_rk, 8), (4,), 0, max(1, 512 // 4) + 1, jnp.int32)
        _ctx_512P = jax.random.normal(jax.random.fold_in(_rk, 11), (4, 16, 64), jnp.float32)
        _ctx_512c = jax.random.dirichlet(jax.random.fold_in(_rk, 511), 0.3 * jnp.ones((16,), jnp.float32), (4, 512))
        _ctx_512t = jnp.einsum('bsk,bkd->bsd', _ctx_512c, _ctx_512P)
        _ctx_512t = _ctx_512t * jax.lax.rsqrt(jnp.mean(jnp.square(_ctx_512t)) + 1e-12) * 0.953939
        ctx_512 = 0.00222621 + 0.99962 * (_ctx_512t + 0.3 * jax.random.normal(jax.random.fold_in(_rk, 611), (4, 512, 64), jnp.float32))
        _g = jax.random.normal(jax.random.fold_in(_rk, 9001), (2, 2), jnp.float32)
        _g = jnp.sign(_g) * jnp.maximum(jnp.abs(_g), 1.0) + (_g == 0) * 1.0
        g_xattn = _g[0]
        g_ffn = _g[1]
        return (x, ctx_512, g_xattn, g_ffn)
    x, ctx_512, g_xattn, g_ffn = _rec_inputs()

    def _L0_xattn_setup():
        import jax, jax.numpy as jnp
        import numpy as np
        B, T, TC, C, CC, H = (2, 256, 64, 128, 64, 16)
        D = C // H

        def _heads(t):
            b, l, _ = t.shape
            return t.reshape(b, l, H, D).transpose(0, 2, 1, 3)
        key = jax.random.key(seed)
        ks = jax.random.split(key, 18)
        w = lambda k, i, o: jax.random.normal(k, (i, o), jnp.float32) / np.sqrt(i).astype(np.float32)
        return {'x': jax.random.normal(ks[0], (B, T, C), jnp.float32), 'cross_input': jax.random.normal(ks[1], (B, TC, CC), jnp.float32), 'Wk': w(ks[2], C, C), 'bk': jnp.zeros((C,), jnp.float32), 'Wq': w(ks[3], C, C), 'bq': jnp.zeros((C,), jnp.float32), 'Wv': w(ks[4], C, C), 'bv': jnp.zeros((C,), jnp.float32), 'Wck': w(ks[5], CC, C), 'bck': jnp.zeros((C,), jnp.float32), 'Wcq': w(ks[6], C, C), 'bcq': jnp.zeros((C,), jnp.float32), 'Wcv': w(ks[7], CC, C), 'bcv': jnp.zeros((C,), jnp.float32), 'Wp': w(ks[8], C, C), 'bp': jnp.zeros((C,), jnp.float32)}
    _L0_xattn_all = _L0_xattn_setup()
    _L0_xattn_in = {k: v for k, v in _L0_xattn_all.items() if k in ('Wk', 'bk', 'Wq', 'bq', 'Wv', 'bv', 'Wck', 'bck', 'Wcq', 'bcq', 'Wcv', 'bcv', 'Wp', 'bp')}
    del _L0_xattn_all

    def _L0_ffn_setup():
        import jax, jax.numpy as jnp
        import numpy as np
        TOP_K = 2
        CAPACITY_FACTOR = 1.25

        def _moe_forward(x, gate_w, wi_gate, wi_up, wo):
            B, S, D = x.shape
            E = wi_gate.shape[0]
            N = B * S
            capacity = max(int(N / E * CAPACITY_FACTOR), 1)
            x_flat = x.reshape(N, D)
            router_logits = x_flat @ gate_w.T
            router_probs = jax.nn.softmax(router_logits, axis=-1)
            top_k_probs, top_k_idx = jax.lax.top_k(router_probs, TOP_K)
            top_k_probs = top_k_probs / jnp.sum(top_k_probs, axis=-1, keepdims=True)
            out = jnp.zeros_like(x_flat)
            experts = jnp.arange(E, dtype=jnp.int32)
            for k in range(TOP_K):
                eid = top_k_idx[:, k]
                ew = top_k_probs[:, k]
                onehot = (eid[:, None] == experts[None, :]).astype(jnp.int32)
                pos_all = jnp.cumsum(onehot, axis=0) - 1
                pos = jnp.take_along_axis(pos_all, eid[:, None].astype(jnp.int32), axis=1)[:, 0]
                valid = pos < capacity
                pos_c = jnp.where(valid, pos, 0)
                disp = jnp.zeros((E, capacity, D), x_flat.dtype).at[eid, pos_c].add(jnp.where(valid[:, None], x_flat, 0.0))
                gate = jax.nn.silu(jnp.einsum('ecd,efd->ecf', disp, wi_gate))
                up = jnp.einsum('ecd,efd->ecf', disp, wi_up)
                expert_out = jnp.einsum('ecf,edf->ecd', gate * up, wo)
                tok_out = expert_out[eid, pos_c]
                out = out + jnp.where(valid[:, None], ew[:, None] * tok_out, 0.0)
            return out.reshape(B, S, D)
        key = jax.random.key(seed)
        k1, k2, k3, k4, k5 = jax.random.split(key, 5)
        B, S, D, F, E = (4, 256, 128, 512, 8)
        return {'x': jax.random.normal(k1, (B, S, D), dtype=jnp.float32), 'gate_w': jax.random.normal(k2, (E, D), dtype=jnp.float32) * 0.02, 'wi_gate': jax.random.normal(k3, (E, F, D), dtype=jnp.float32) * 0.02, 'wi_up': jax.random.normal(k4, (E, F, D), dtype=jnp.float32) * 0.02, 'wo': jax.random.normal(k5, (E, D, F), dtype=jnp.float32) * 0.02}
    _L0_ffn_all = _L0_ffn_setup()
    _L0_ffn_in = {k: v for k, v in _L0_ffn_all.items() if k in ('gate_w', 'wi_gate', 'wi_up', 'wo')}
    del _L0_ffn_all

    def _L1_xattn_setup():
        import jax, jax.numpy as jnp
        import numpy as np
        B, LQ, LK = (8, 256, 256)
        QD, KD, VD = (128, 64, 64)
        key = jax.random.key(seed)
        ks = jax.random.split(key, 9)
        s = 0.02
        return {'query': jax.random.normal(ks[0], (B, LQ, QD), jnp.float32), 'key': jax.random.normal(ks[1], (B, LK, KD), jnp.float32), 'value': jax.random.normal(ks[2], (B, LK, VD), jnp.float32), 'Wq': jax.random.normal(ks[3], (QD, QD), jnp.float32) * s, 'bq': jnp.zeros((QD,), jnp.float32), 'Wk': jax.random.normal(ks[4], (KD, QD), jnp.float32) * s, 'bk': jnp.zeros((QD,), jnp.float32), 'Wv': jax.random.normal(ks[5], (VD, QD), jnp.float32) * s, 'bv': jnp.zeros((QD,), jnp.float32)}
    _L1_xattn_all = _L1_xattn_setup()
    _L1_xattn_in = {k: v for k, v in _L1_xattn_all.items() if k in ('Wq', 'bq', 'Wk', 'bk', 'Wv', 'bv')}
    del _L1_xattn_all

    def _L1_ffn_setup():
        import jax, jax.numpy as jnp
        import numpy as np
        E = 8
        K = 2
        DIM = 128
        DFF = 256

        def _moe(x, Wg, bg, w1, w2):
            B, S, D = x.shape
            t = x.reshape(-1, D)
            logits = t @ Wg.T + bg
            probs = jax.nn.softmax(logits, axis=-1)
            topw, topi = jax.lax.top_k(probs, K)
            topw = topw / jnp.sum(topw, axis=-1, keepdims=True)
            combine = jnp.sum(jax.nn.one_hot(topi, E, dtype=t.dtype) * topw[..., None], axis=1)

            def body(acc, packed):
                w1e, w2e, ce = packed
                h = t @ w1e.T
                gate, up = jnp.split(h, 2, axis=-1)
                a = jax.nn.silu(gate) * up
                o = a @ w2e.T
                return (acc + ce[:, None] * o, None)
            out, _ = jax.lax.scan(body, jnp.zeros_like(t), (w1, w2, combine.T))
            return out.reshape(B, S, D)
        key = jax.random.key(seed)
        ks = jax.random.split(key, 5)
        B, S = (4, 256)
        x = jax.random.normal(ks[0], (B, S, DIM), dtype=jnp.float32)
        Wg = jax.random.normal(ks[1], (E, DIM), dtype=jnp.float32) * 0.02
        bg = jax.random.normal(ks[2], (E,), dtype=jnp.float32) * 0.02
        w1 = jax.random.normal(ks[3], (E, DFF, DIM), dtype=jnp.float32) * 0.02
        w2 = jax.random.normal(ks[4], (E, DIM, DFF // 2), dtype=jnp.float32) * 0.02
        return {'x': x, 'Wg': Wg, 'bg': bg, 'w1': w1, 'w2': w2}
    _L1_ffn_all = _L1_ffn_setup()
    _L1_ffn_in = {k: v for k, v in _L1_ffn_all.items() if k in ('Wg', 'bg', 'w1', 'w2')}
    del _L1_ffn_all
    return {'x': x, 'ctx_512': ctx_512, 'g_xattn': g_xattn, 'g_ffn': g_ffn, 'L0_xattn_Wk': _L0_xattn_in['Wk'], 'L0_xattn_bk': _L0_xattn_in['bk'], 'L0_xattn_Wq': _L0_xattn_in['Wq'], 'L0_xattn_bq': _L0_xattn_in['bq'], 'L0_xattn_Wv': _L0_xattn_in['Wv'], 'L0_xattn_bv': _L0_xattn_in['bv'], 'L0_xattn_Wck': _L0_xattn_in['Wck'], 'L0_xattn_bck': _L0_xattn_in['bck'], 'L0_xattn_Wcq': _L0_xattn_in['Wcq'], 'L0_xattn_bcq': _L0_xattn_in['bcq'], 'L0_xattn_Wcv': _L0_xattn_in['Wcv'], 'L0_xattn_bcv': _L0_xattn_in['bcv'], 'L0_xattn_Wp': _L0_xattn_in['Wp'], 'L0_xattn_bp': _L0_xattn_in['bp'], 'L0_ffn_gate_w': _L0_ffn_in['gate_w'], 'L0_ffn_wi_gate': _L0_ffn_in['wi_gate'], 'L0_ffn_wi_up': _L0_ffn_in['wi_up'], 'L0_ffn_wo': _L0_ffn_in['wo'], 'L1_xattn_Wq': _L1_xattn_in['Wq'], 'L1_xattn_bq': _L1_xattn_in['bq'], 'L1_xattn_Wk': _L1_xattn_in['Wk'], 'L1_xattn_bk': _L1_xattn_in['bk'], 'L1_xattn_Wv': _L1_xattn_in['Wv'], 'L1_xattn_bv': _L1_xattn_in['bv'], 'L1_ffn_Wg': _L1_ffn_in['Wg'], 'L1_ffn_bg': _L1_ffn_in['bg'], 'L1_ffn_w1': _L1_ffn_in['w1'], 'L1_ffn_w2': _L1_ffn_in['w2']}

def reference(x, ctx_512, g_xattn, g_ffn, L0_xattn_Wk, L0_xattn_bk, L0_xattn_Wq, L0_xattn_bq, L0_xattn_Wv, L0_xattn_bv, L0_xattn_Wck, L0_xattn_bck, L0_xattn_Wcq, L0_xattn_bcq, L0_xattn_Wcv, L0_xattn_bcv, L0_xattn_Wp, L0_xattn_bp, L0_ffn_gate_w, L0_ffn_wi_gate, L0_ffn_wi_up, L0_ffn_wo, L1_xattn_Wq, L1_xattn_bq, L1_xattn_Wk, L1_xattn_bk, L1_xattn_Wv, L1_xattn_bv, L1_ffn_Wg, L1_ffn_bg, L1_ffn_w1, L1_ffn_w2):
    import jax
    import jax.numpy as jnp

    def _L0_xattn_ref(x, cross_input, Wk, bk, Wq, bq, Wv, bv, Wck, bck, Wcq, bcq, Wcv, bcv, Wp, bp):
        import jax, jax.numpy as jnp
        import numpy as np
        B, T, TC, C, CC, H = (2, 256, 64, 128, 64, 16)
        D = C // H

        def _heads(t):
            b, l, _ = t.shape
            return t.reshape(b, l, H, D).transpose(0, 2, 1, 3)
        scale = np.float32(1.0 / np.sqrt(D))
        q = _heads(x @ Wq + bq)
        k = _heads(x @ Wk + bk)
        v = _heads(x @ Wv + bv)
        att = jnp.einsum('bhqd,bhkd->bhqk', q, k) * scale
        causal = jnp.tril(jnp.ones((T, T), bool))
        att = jnp.where(causal[None, None], att, -jnp.inf)
        y = jnp.einsum('bhqk,bhkd->bhqd', jax.nn.softmax(att, axis=-1), v)
        qc = _heads(x @ Wcq + bcq)
        kc = _heads(cross_input @ Wck + bck)
        vc = _heads(cross_input @ Wcv + bcv)
        attc = jnp.einsum('bhqd,bhkd->bhqk', qc, kc) * scale
        y = y + jnp.einsum('bhqk,bhkd->bhqd', jax.nn.softmax(attc, axis=-1), vc)
        y = y.transpose(0, 2, 1, 3).reshape(x.shape[0], T, C)
        return y @ Wp + bp

    def _L0_ffn_ref(x, gate_w, wi_gate, wi_up, wo):
        import jax, jax.numpy as jnp
        import numpy as np
        TOP_K = 2
        CAPACITY_FACTOR = 1.25

        def _moe_forward(x, gate_w, wi_gate, wi_up, wo):
            B, S, D = x.shape
            E = wi_gate.shape[0]
            N = B * S
            capacity = max(int(N / E * CAPACITY_FACTOR), 1)
            x_flat = x.reshape(N, D)
            router_logits = x_flat @ gate_w.T
            router_probs = jax.nn.softmax(router_logits, axis=-1)
            top_k_probs, top_k_idx = jax.lax.top_k(router_probs, TOP_K)
            top_k_probs = top_k_probs / jnp.sum(top_k_probs, axis=-1, keepdims=True)
            out = jnp.zeros_like(x_flat)
            experts = jnp.arange(E, dtype=jnp.int32)
            for k in range(TOP_K):
                eid = top_k_idx[:, k]
                ew = top_k_probs[:, k]
                onehot = (eid[:, None] == experts[None, :]).astype(jnp.int32)
                pos_all = jnp.cumsum(onehot, axis=0) - 1
                pos = jnp.take_along_axis(pos_all, eid[:, None].astype(jnp.int32), axis=1)[:, 0]
                valid = pos < capacity
                pos_c = jnp.where(valid, pos, 0)
                disp = jnp.zeros((E, capacity, D), x_flat.dtype).at[eid, pos_c].add(jnp.where(valid[:, None], x_flat, 0.0))
                gate = jax.nn.silu(jnp.einsum('ecd,efd->ecf', disp, wi_gate))
                up = jnp.einsum('ecd,efd->ecf', disp, wi_up)
                expert_out = jnp.einsum('ecf,edf->ecd', gate * up, wo)
                tok_out = expert_out[eid, pos_c]
                out = out + jnp.where(valid[:, None], ew[:, None] * tok_out, 0.0)
            return out.reshape(B, S, D)
        return _moe_forward(x, gate_w, wi_gate, wi_up, wo)

    def _L1_xattn_ref(query, key, value, Wq, bq, Wk, bk, Wv, bv):
        import jax, jax.numpy as jnp
        import numpy as np
        B, LQ, LK = (8, 256, 256)
        QD, KD, VD = (128, 64, 64)
        q = jnp.einsum('bld,de->ble', query, Wq) + bq
        k = jnp.einsum('bld,de->ble', key, Wk) + bk
        v = jnp.einsum('bld,de->ble', value, Wv) + bv
        scores = jnp.einsum('bqe,bke->bqk', q, k)
        attn = jax.nn.softmax(scores, axis=-1)
        out = jnp.einsum('bqk,bke->bqe', attn, v)
        return out

    def _L1_ffn_ref(x, Wg, bg, w1, w2):
        import jax, jax.numpy as jnp
        import numpy as np
        E = 8
        K = 2
        DIM = 128
        DFF = 256

        def _moe(x, Wg, bg, w1, w2):
            B, S, D = x.shape
            t = x.reshape(-1, D)
            logits = t @ Wg.T + bg
            probs = jax.nn.softmax(logits, axis=-1)
            topw, topi = jax.lax.top_k(probs, K)
            topw = topw / jnp.sum(topw, axis=-1, keepdims=True)
            combine = jnp.sum(jax.nn.one_hot(topi, E, dtype=t.dtype) * topw[..., None], axis=1)

            def body(acc, packed):
                w1e, w2e, ce = packed
                h = t @ w1e.T
                gate, up = jnp.split(h, 2, axis=-1)
                a = jax.nn.silu(gate) * up
                o = a @ w2e.T
                return (acc + ce[:, None] * o, None)
            out, _ = jax.lax.scan(body, jnp.zeros_like(t), (w1, w2, combine.T))
            return out.reshape(B, S, D)
        return _moe(x, Wg, bg, w1, w2)
    x = x + jnp.tanh(g_xattn[0]) * _L0_xattn_ref(_layernorm(x, axis=-1), ctx_512, L0_xattn_Wk, L0_xattn_bk, L0_xattn_Wq, L0_xattn_bq, L0_xattn_Wv, L0_xattn_bv, L0_xattn_Wck, L0_xattn_bck, L0_xattn_Wcq, L0_xattn_bcq, L0_xattn_Wcv, L0_xattn_bcv, L0_xattn_Wp, L0_xattn_bp)
    x = x + jnp.tanh(g_ffn[0]) * _L0_ffn_ref(_layernorm(x, axis=-1), L0_ffn_gate_w, L0_ffn_wi_gate, L0_ffn_wi_up, L0_ffn_wo)
    x = x + jnp.tanh(g_xattn[1]) * _L1_xattn_ref(_layernorm(x, axis=-1), ctx_512, ctx_512, L1_xattn_Wq, L1_xattn_bq, L1_xattn_Wk, L1_xattn_bk, L1_xattn_Wv, L1_xattn_bv)
    x = x + jnp.tanh(g_ffn[1]) * _L1_ffn_ref(_layernorm(x, axis=-1), L1_ffn_Wg, L1_ffn_bg, L1_ffn_w1, L1_ffn_w2)
    return x

_drawn_inputs = setup_inputs


def setup_inputs(seed=0):
    import zlib

    import numpy as np

    out = dict(_drawn_inputs(seed))
    spreads = {'g_ffn': (-1.0, 0.6),
     'L0_xattn_bk': (0.0, 0.8),
     'L0_xattn_bq': (0.0, 0.561),
     'L0_xattn_bv': (0.0, 0.1),
     'L0_xattn_bck': (0.0, 0.8),
     'L0_xattn_bcq': (0.0, 0.506),
     'L0_xattn_bcv': (0.0, 0.1),
     'L0_xattn_bp': (0.0, 0.1),
     'L1_xattn_bq': (0.0, 0.8),
     'L1_xattn_bk': (0.0, 0.8),
     'L1_xattn_bv': (0.0, 0.1)}
    factors = {'L0_ffn_gate_w': 8.0,
     'L0_ffn_wi_gate': 8.0,
     'L0_ffn_wi_up': 8.0,
     'L0_ffn_wo': 8.0,
     'L1_xattn_Wq': 4.823,
     'L1_xattn_Wk': 4.96,
     'L1_ffn_Wg': 8.0,
     'L1_ffn_bg': 8.0,
     'L1_ffn_w1': 8.0,
     'L1_ffn_w2': 8.0}
    for name, (base, spread) in spreads.items():
        noise = np.random.default_rng([zlib.crc32(name.encode()), seed]).standard_normal(out[name].shape)
        drawn = base * np.exp(spread * noise) if base else spread * noise
        out[name] = jnp.asarray(drawn.astype(out[name].dtype))
    for name, factor in factors.items():
        out[name] = (out[name] * factor).astype(out[name].dtype)
    return out
```

```python
from contextlib import ExitStack

import concourse.bass as bass
from concourse import mybir

F32 = mybir.dt.float32
BF16 = mybir.dt.bfloat16
U32 = mybir.dt.uint32
ALU = mybir.AluOpType
ACT = mybir.ActivationFunctionType
AX = mybir.AxisListType

P = 128
BANK = 512
EPS = 1e-5
CAPACITY_FACTOR = 1.25
NEG = -1.0e30

Q_PART = (0, 0, 0, 1, 1, 2)
K_PART = (0, 1, 2, 0, 1, 0)
B_Q, B_CQ, B_K, B_Q1 = range(4)


def flamingo_gated_kernel(nc, a, out):
    B, S, D = a["x"].shape
    SC, DC = a["ctx_512"].shape[1:]
    H = 16
    HD = D // H
    SCALE = float(HD) ** -0.5
    NT = B * S // P
    QT = S // P
    NC = B * SC // P
    CT = SC // P
    TOK = B * S
    E = a["L0_ffn_gate_w"].shape[0]
    NF0 = a["L0_ffn_wi_gate"].shape[1] // P
    NF1 = a["L1_ffn_w1"].shape[1] // 2 // P
    CAPACITY = max(int(TOK / E * CAPACITY_FACTOR), 1)
    assert D == P and QT == 2 and CT == 4 and NF1 == 1 and NF0 == 4 and E == 8 and HD == 8

    PAIR, PAR = H // 2, 2
    ROWS = HD * len(Q_PART)
    ROWS_M = ROWS + 3
    QW = 2 * S
    KW = S + SC
    XW = QW + KW
    HA = HD + 1
    HALF = H // 2
    OW = 2 * QT * HALF * HA

    ctx = ExitStack()
    with ctx:
        def sb(name, shape, dt=F32):
            return ctx.enter_context(nc.sbuf_tensor(name, shape, dt))

        def sem(name):
            return ctx.enter_context(nc.semaphore(name))

        x_sb = sb("x_sb", [P, NT, D])
        c_sb = sb("c_sb", [P, NC, DC])
        w_q = sb("w_q", [P, D])
        w_k = sb("w_k", [P, D])
        w_cq = sb("w_cq", [P, D])
        w_v = sb("w_v", [P, D])
        w_p = sb("w_p", [P, D])
        w_ck = sb("w_ck", [DC + 1, D])
        w_cv = sb("w_cv", [DC + 1, D])
        w1_q = sb("w1_q", [P, D])
        w1_k = sb("w1_k", [DC + 1, D])
        w1_v = sb("w1_v", [DC + 1, D])
        w_perm = sb("w_perm", [P, 4, D])
        b_perm = sb("b_perm", [3, D])
        b_rows = sb("b_rows", [3, D])
        b1_row = sb("b1_row", [1, D])
        b_col = sb("b_col", [P, 4])
        b_v = sb("b_v", [P, D])
        b_p = sb("b_p", [P, D])
        b_g = sb("b_g", [P, E])
        gates = sb("gates", [P, 4])
        tanh_g = sb("tanh_g", [P, 4])
        gw_rows = sb("gw_rows", [E, 2, D])
        gw_t = sb("gw_t", [P, 2, E])

        ident = sb("ident", [P, P])
        ident_b = sb("ident_b", [P, P], BF16)
        mask_b = sb("mask_b", [P, P], BF16)
        upto_b = sb("upto_b", [P, P], BF16)
        ones_b = sb("ones_b", [P, KW], BF16)
        iota_e = sb("iota_e", [P, E])
        half_neg = sb("half_neg", [P, NT])
        bp_g = sb("bp_g", [P, D])

        ln_stats = sb("ln_stats", [P, NT, 6])
        ln_mv = sb("ln_mv", [P, NT, 2])
        ln_rstd = sb("ln_rstd", [P, NT])
        h_sb = sb("h_sb", [P, NT, D])
        h_t = sb("h_t", [P, TOK])
        c_t = sb("c_t", [DC + 1, NC * P])

        qk = sb("qk", [P, 2, XW])
        qk_r = sb("qk_r", [P, 2, XW])
        parts = sb("parts", [P, 2, 3, XW], BF16)
        qcat = sb("qcat", [P, B, PAIR, QW], BF16)
        kcat = sb("kcat", [P, B, PAIR, KW], BF16)
        v_aug = sb("v_aug", [P, NT + NC, H, HA])

        nmax = sb("nmax", [P, 2, QT, 2, H])
        nmax_r = sb("nmax_r", [P, QT, 2 * PAR, PAIR])
        nmax_p = sb("nmax_p", [P, 2, QT, 2 * PAR, 3, PAIR], BF16)
        nmax_t = sb("nmax_t", [2 * PAR * 3 * PAIR, 2, S], BF16)
        NPT = 9
        p_t = sb("p_t", [P, NPT, BANK])
        o_sb = sb("o_sb", [P, 2, 2, QT, HALF, HA])
        o_rec = sb("o_rec", [P, 2, 2, QT, HALF])
        o_n = sb("o_n", [P, 2, 2, QT, HALF, HD])
        y_sb, y_t = h_sb, h_t
        x1_sb = sb("x1_sb", [P, NT, D])

        lg = sb("lg", [P, NT, E])
        top = sb("top", [P, NT, 8])
        top_i = sb("top_i", [P, NT, 8], U32)
        top_f = sb("top_f", [P, 2, NT])
        gap = sb("gap", [P, NT])
        e_gap = sb("e_gap", [P, NT])
        w_top = sb("w_top", [P, 2, NT])
        pick = sb("pick", [P, 2, NT, E])
        pick_b = sb("pick_b", [P, 2, NT, E], BF16)
        fits = sb("fits", [P, 2, NT, E])
        comb2 = sb("comb2", [P, 2, NT, E])
        comb = sb("comb", [P, NT, E])
        NRAW = 2
        raw = parts[:, :, :, :].rearrange("p s c n -> p (s c n)").bitcast(F32)[:, 0:NRAW * 3 * NF0 * P]\
            .rearrange("p (s m f d) -> p s m f d", s=NRAW, m=3, f=NF0)
        w_t = kcat[:, 3].rearrange("p a n -> p (a n)").bitcast(F32).rearrange("p (s m f) -> p s m f", s=2, m=3)
        hh = kcat[:, 1:3].rearrange("p b a n -> p (b a n)").bitcast(F32)[:, 0:2 * NF0 * BANK]\
            .rearrange("p (s f k) -> p s f k", s=2, f=NF0)
        sg = qcat[:, 3].rearrange("p a n -> p (a n)").bitcast(F32)[:, 0:2 * BANK].rearrange("p (s k) -> p s k", s=2)
        acc = qcat[:, 2].rearrange("p a n -> p (a n)").bitcast(F32)[:, 0:NT * D].rearrange("p (t d) -> p t d", t=NT)

        q1_t = h_sb[:, :, :].rearrange("p t d -> p (t d)")
        k1_t = kcat[:, 0, :, :].rearrange("p a n -> p (a n)").bitcast(F32)[:, 0:NC * P]
        v1 = qcat[:, 0:2, :, :].rearrange("p b a n -> p (b a n)").bitcast(F32)[:, 0:NC * D]\
            .rearrange("p (t d) -> p t d", t=NC)
        p1 = qk[:, :, 0:SC]
        p1_t = qk_r[:, :, 0:SC]
        s1_nmax = sb("s1_nmax", [P, NT])
        s1_sum = sb("s1_sum", [P, NT])
        s1_rec = sb("s1_rec", [P, NT])

        psum = ctx.enter_context(nc.psum_tensor("psum", [P, 8 * BANK], F32))

        def bank(i, n=1):
            return psum[:, i * BANK:(i + n) * BANK]

        in_x = sem("in_x")
        in_ctx = sem("in_ctx")
        in_w = sem("in_w")
        consts = sem("consts")
        ones_in = sem("ones_in")
        perm_in = sem("perm_in")
        tanh_in = sem("tanh_in")
        stats_in = [sem(f"stats_in{i}") for i in range(4)]
        rstd_in = [sem(f"rstd_in{i}") for i in range(4)]
        h_in = [sem(f"h_in{i}") for i in range(4)]
        job_done = sem("job_done")
        job_act = sem("job_act")
        job_dve = sem("job_dve")
        high_in = sem("high_in")
        parts_in = sem("parts_in")
        cat_in = [sem(f"cat_in{b}") for b in range(B)]
        s1_full = sem("s1_full")
        s1_free = sem("s1_free")
        split_in = sem("split_in")
        mrow_in = [sem(f"mrow_in{b}") for b in range(B)]
        s2_full = sem("s2_full")
        p_in = sem("p_in")
        masked = sem("masked")
        pv_done = sem("pv_done")
        o_taken = sem("o_taken")
        rec_in = sem("rec_in")
        y_in = sem("y_in")
        xb_in = sem("xb_in")
        yt_full = sem("yt_full")
        yt_act = sem("yt_act")
        yt_dve = sem("yt_dve")
        proj_full = sem("proj_full")
        x1_in = sem("x1_in")
        x2_in = sem("x2_in")
        x3_in = sem("x3_in")
        x4_in = sem("x4_in")
        ht_full = [sem(f"ht_full{i}") for i in range(4)]
        ht_act = [sem(f"ht_act{i}") for i in range(4)]
        ht_dve = [sem(f"ht_dve{i}") for i in range(4)]
        lg_full = [sem(f"lg_full{i}") for i in range(2)]
        gap_in = [sem(f"gap_in{i}") for i in range(2)]
        e_gap_in = [sem(f"e_gap_in{i}") for i in range(2)]
        pick_in = sem("pick_in")
        count_full = sem("count_full")
        raw_in = [[sem(f"raw_in{i}_{r}") for r in range(NRAW)] for i in range(2)]
        tr_full = [sem(f"tr_full{i}") for i in range(2)]
        wt_in = [sem(f"wt_in{i}") for i in range(2)]
        gu_full = [sem(f"gu_full{i}") for i in range(2)]
        sg_in = [sem(f"sg_in{i}") for i in range(2)]
        hh_in = [sem(f"hh_in{i}") for i in range(2)]
        dn_full = [sem(f"dn_full{i}") for i in range(2)]
        dn_taken = [sem(f"dn_taken{i}") for i in range(2)]
        kv1_full = sem("kv1_full")
        kv1_act = sem("kv1_act")
        q1_full = sem("q1_full")
        q1_act = sem("q1_act")
        sc1_full = sem("sc1_full")
        nm1_in = sem("nm1_in")
        p1_in = sem("p1_in")
        p1t_full = sem("p1t_full")
        p1t_in = sem("p1t_in")
        o1_full = sem("o1_full")
        stored = sem("stored")
        dve_step = sem("dve_step")
        act_step = sem("act_step")
        pool_step = sem("pool_step")

        def linker(eng, s):
            count = [0]

            def link(ins):
                count[0] += 1
                ins.then_inc(s, 1)
                eng.wait_ge(s, count[0])
            return link

        jobs = [("xt", i, "dve") for i in range(NT // 4)] + [("ct", i, "act") for i in range(NC // 4)]
        jobs += [("bias", 0, "act")]
        for b in range(B):
            jobs += [("q", b, "act"), ("k", b, "act"), ("ck", b, "act"), ("v", b, "dve"), ("cv", b, "dve")]
        jobs += [("gw", 0, "dve")]

        def job_at(kind, index):
            return [j for j, (k, i, _) in enumerate(jobs) if (k, i) == (kind, index)][0]

        def taken_count(j):
            return sum(e == jobs[j][2] for _, _, e in jobs[:j + 1])

        def wait_taken(eng, j):
            eng.wait_ge(job_dve if jobs[j][2] == "dve" else job_act, taken_count(j))

        def units_of(b):
            u = [("cross", b, t, pair) for t in range(QT) for pair in range(PAIR)]
            u += [("late", b, 1, g) for g in range(PAIR // 2)]
            return u + [("early", b, 0, g) for g in range(PAIR // 4)]

        TURN_LAG = 3
        N1 = len(units_of(0))
        pass1 = []
        for b in range(B):
            u = units_of(b)
            if b:
                u.insert(TURN_LAG, ("turn", b - 1))
            pass1 += u
        pass1.append(("turn", B - 1))
        turn_at = {u[1]: i for i, u in enumerate(pass1) if u[0] == "turn"}
        split_after = {b: max(i for i, u in enumerate(pass1) if u[0] != "turn" and u[1] == b) for b in range(B)}
        LEAD = N1 + 9

        def pass1_before(head):
            return min(len(pass1), LEAD + -(-head * (N1 + 1) // H))

        NHEAD = B * H

        def q_cols(kind):
            return kind * S

        def k_cols(kind):
            return kind * S

        NHT = TOK // BANK
        TPH = BANK // P

        def expert_weights(layer, e):
            if layer == 0:
                return [a["L0_ffn_wi_gate"][e].rearrange("(n f) d -> f n d", f=P),
                        a["L0_ffn_wi_up"][e].rearrange("(n f) d -> f n d", f=P),
                        a["L0_ffn_wo"][e].rearrange("d (n f) -> d n f", f=P)]
            return [a["L1_ffn_w1"][e, 0:P, :].unsqueeze(1), a["L1_ffn_w1"][e, P:2 * P, :].unsqueeze(1),
                    a["L1_ffn_w2"][e].unsqueeze(1)]

        def nf_of(layer):
            return NF0 if layer == 0 else NF1

        def tr_jobs(layer):
            if layer == 0:
                return [[(m, n) for n in range(NF0)] for m in range(3)]
            return [[(m, 0) for m in range(3)]]

        block = ctx.enter_context(nc.Block())

        def experts_of(layer):
            nf = nf_of(layer)
            units = [(e, s, f) for e in range(E) for s in range(NHT) for f in range(nf)]
            lag = 2 if layer == 0 else 1
            down_after = {}
            trans_after = {}
            per = NHT * nf
            nj = len(tr_jobs(layer))
            for n in range(E * NHT):
                down_after.setdefault(min((n + 1) * nf - 1 + lag, len(units) - 1), []).append(n)
            for e in range(1, E):
                for j in range(nj):
                    at = (e - 1) * per + (3 + j if layer == 0 else 1)
                    trans_after.setdefault(at, []).append((e, j))
            return units, down_after, trans_after, nj

        COUNT_AFTER = 1
        KV1_BANK = [2, 3, 4, 5, 6, 7, 2, 3]
        N_IN_W = 25

        ORDER = [experts_of(layer) for layer in range(2)]

        @block.sync
        def _(sp):
            sp.dma_start(x_sb[:, :, :], a["x"].rearrange("b (t p) d -> p (b t) d", p=P)).then_inc(in_x, 16)
            sp.dma_start(c_sb[:, :, :], a["ctx_512"].rearrange("b (t p) d -> p (b t) d", p=P)).then_inc(in_ctx, 16)
            sp.wait_ge(consts, 1)
            for b in range(B):
                for par in range(PAR):
                    r = 64 * par + ROWS
                    sp.dma_start(kcat[r:r + 3, b, :, :], ones_b[0:3 * PAIR, :]).then_inc(ones_in, 16)
            for b in range(B):
                sp.wait_ge(parts_in, b + 1)
                for r in range(len(Q_PART)):
                    for par in range(PAR):
                        rows = slice(64 * par + HD * r, 64 * par + HD * (r + 1))
                        half = slice(64 * par, 64 * par + 64)
                        sp.dma_start(qcat[rows, b, :, :], parts[half, b % 2, Q_PART[r], 0:QW]).then_inc(cat_in[b], 16)
                        sp.dma_start(kcat[rows, b, :, :], parts[half, b % 2, K_PART[r], QW:XW]).then_inc(cat_in[b], 16)
            for b in range(B - 2, B):
                sp.wait_ge(cat_in[b], 32 * PAR * len(Q_PART))
            for e in range(NRAW):
                for m, w in enumerate(expert_weights(0, e)):
                    sp.dma_start(raw[:, e, m, :, :], w).then_inc(raw_in[0][e], 16)
            for b in range(B):
                sp.wait_ge(s1_free, turn_at[b] + 1)
                for kind in range(2):
                    for par in range(PAR):
                        r = 3 * PAIR * (PAR * kind + par)
                        sp.dma_start(qcat[64 * par + ROWS:64 * par + ROWS_M, b, :, kind * S:kind * S + S],
                                     nmax_t[r:r + 3 * PAIR, b % 2, :]).then_inc(mrow_in[b], 16)
            for layer in range(2):
                nj = len(tr_jobs(layer))
                for e in range(NRAW if layer == 0 else 0, E):
                    if layer == 1 and e < NRAW:
                        sp.wait_ge(tr_full[0], len(tr_jobs(0)) * (E - NRAW + e + 1))
                    else:
                        sp.wait_ge(tr_full[layer], nj * (e - NRAW + 1))
                    for m, w in enumerate(expert_weights(layer, e)):
                        sp.dma_start(raw[:, e % NRAW, m, 0:nf_of(layer), :], w).then_inc(raw_in[layer][e % NRAW], 16)
            out_v = out.rearrange("b (t p) d -> p (b t) d", p=P)
            for s in range(NHT):
                sp.wait_ge(x4_in, s + 1)
                sp.dma_start(out_v[:, s * TPH:(s + 1) * TPH, :], x_sb[:, s * TPH:(s + 1) * TPH, :]).then_inc(stored, 16)
            sp.wait_ge(stored, 16 * NHT)

        @block.gpsimd
        def _(pool):
            link = linker(pool, pool_step)
            made = [0]

            def const(ins):
                made[0] += 1
                ins.then_inc(consts, 1)
                pool.wait_ge(consts, made[0])

            const(pool.memset(ones_b[:, :], 1.0))
            link(pool.memset(ident[:, :], 0.0))
            link(pool.affine_select(out=ident[:, :], in_=ident[:, :], pattern=[[-1, P]], compare_op=ALU.not_equal,
                                    fill=1.0, base=0, channel_multiplier=1))
            const(pool.memset(half_neg[:, :], -0.5))
            const(pool.memset(c_t[DC:DC + 1, :], 1.0))
            const(pool.tensor_copy(ident_b[:, :], ident[:, :]))

            def rstd(i):
                pool.wait_ge(stats_in[i], NT)
                link(pool.tensor_scalar(ln_rstd[:, :], ln_mv[:, :, 1], EPS, None, ALU.add))
                pool.tensor_tensor(ln_rstd[:, :], ln_rstd[:, :], half_neg[:, :], ALU.pow).then_inc(rstd_in[i], 1)

            rstd(0)
            pool.wait_ge(in_w, 16 * N_IN_W)
            for dst, src in ((w_perm[:, 0, :], w_q), (w_perm[:, 1, :], w_cq), (w_perm[:, 2, :], w_k),
                             (w_perm[0:DC + 1, 3, :], w_ck), (b_perm[:, :], b_rows)):
                pool.tensor_copy(dst.rearrange("k (par d pair) -> k par d pair", pair=PAIR, par=PAR),
                                 src[:, :].rearrange("k (pair par d) -> k par d pair", pair=PAIR, par=PAR))\
                    .then_inc(perm_in, 1)
            pool.wait_ge(perm_in, 5)
            link(pool.memset(mask_b[:, :], 0.0))
            const(pool.affine_select(out=mask_b[:, :], in_=mask_b[:, :], pattern=[[-1, P]], compare_op=ALU.is_ge,
                                     fill=NEG, base=0, channel_multiplier=1))
            const(pool.affine_select(out=upto_b[:, :], in_=ones_b[:, 0:P], pattern=[[1, P]], compare_op=ALU.is_ge,
                                     fill=0.0, base=0, channel_multiplier=-1))
            const(pool.iota(iota_e[:, :], pattern=[[1, E]], base=0, channel_multiplier=0,
                            allow_small_or_imprecise_dtypes=True))
            const(pool.memset(v_aug[:, :, :, HD:HA], 1.0))

            for b in range(B):
                pool.wait_ge(high_in, b + 1)
                link(pool.tensor_copy(parts[:, b % 2, 1, :], qk_r[:, b % 2, :]))
                pool.tensor_tensor(parts[:, b % 2, 2, :], qk_r[:, b % 2, :], parts[:, b % 2, 1, :],
                                   ALU.subtract).then_inc(parts_in, 1)

            pool.wait_ge(in_w, 16 * N_IN_W)
            pool.wait_ge(tanh_in, 1)
            link(pool.tensor_scalar(bp_g[:, :], b_p[:, :], tanh_g[:, 0:1], None, ALU.mult))
            pool.tensor_tensor(x1_sb[:, :, :], x_sb[:, :, :], bp_g[:, :].unsqueeze(1).to_broadcast([P, NT, D]),
                               ALU.add).then_inc(xb_in, 1)

            def normalise(n):
                pool.wait_ge(rec_in, n + 1)
                link(pool.tensor_tensor(o_n[:, n % 2].rearrange("p k t h d -> p (k t h) d"),
                                        o_sb[:, n % 2].rearrange("p k t h d -> p (k t h) d")[:, :, 0:HD],
                                        o_rec[:, n % 2].rearrange("p k t h -> p (k t h)").unsqueeze(2)
                                        .to_broadcast([P, 2 * QT * HALF, HD]), ALU.mult))
                b, half = n // 2, n % 2
                pool.tensor_tensor(y_sb[:, QT * b:QT * (b + 1), half * HALF * HD:(half + 1) * HALF * HD],
                                   o_n[:, n % 2, 0].rearrange("p t h d -> p t (h d)"),
                                   o_n[:, n % 2, 1].rearrange("p t h d -> p t (h d)"), ALU.add).then_inc(y_in, 1)

            for head in range(NHEAD):
                pool.wait_ge(p_in, 3 * head + 1)
                diag = p_t[:, (3 * head) % NPT, :].rearrange("p (c q) -> p c q", q=P)[:, 0:3:2, :]
                pool.affine_select(out=diag, in_=diag, pattern=[[0, 2], [1, P]], compare_op=ALU.is_ge, fill=0.0,
                                   base=0, channel_multiplier=-1).then_inc(masked, 1)
                if head % HALF == 2 and head > HALF:
                    normalise(head // HALF - 1)
            normalise(NHEAD // HALF - 1)
            for i in range(1, 4):
                rstd(i)

        @block.scalar
        def _(act):
            link = linker(act, act_step)
            count = [0]

            def load(dst, src):
                act.dma_start(dst, src).then_inc(in_w, 16)
                count[0] += 1

            load(gates[:, 0:2], a["g_xattn"].partition_broadcast(P))
            load(gates[:, 2:4], a["g_ffn"].partition_broadcast(P))
            load(w_q[:, :], a["L0_xattn_Wq"])
            load(w_cq[:, :], a["L0_xattn_Wcq"])
            load(w_k[:, :], a["L0_xattn_Wk"])
            load(w_ck[0:DC, :], a["L0_xattn_Wck"])
            load(w_ck[DC:DC + 1, :], a["L0_xattn_bck"].unsqueeze(0))
            for c, name in ((B_Q, "bq"), (B_CQ, "bcq"), (B_K, "bk")):
                load(b_rows[c:c + 1, :], a["L0_xattn_" + name].unsqueeze(0))
            load(w_v[:, :], a["L0_xattn_Wv"])
            load(w_cv[0:DC, :], a["L0_xattn_Wcv"])
            load(w_cv[DC:DC + 1, :], a["L0_xattn_bcv"].unsqueeze(0))
            load(b_v[:, :], a["L0_xattn_bv"].partition_broadcast(P))
            load(w_p[:, :], a["L0_xattn_Wp"])
            load(b_p[:, :], a["L0_xattn_bp"].partition_broadcast(P))
            load(gw_rows[:, 0, :], a["L0_ffn_gate_w"])
            load(gw_rows[:, 1, :], a["L1_ffn_Wg"])
            load(b_g[:, :], a["L1_ffn_bg"].partition_broadcast(P))
            load(w1_q[:, :], a["L1_xattn_Wq"])
            load(b1_row[:, :], a["L1_xattn_bq"].unsqueeze(0))
            for w, n in ((w1_k, "k"), (w1_v, "v")):
                load(w[0:DC, :], a["L1_xattn_W" + n])
                load(w[DC:DC + 1, :], a["L1_xattn_b" + n].unsqueeze(0))
            assert count[0] == N_IN_W, count[0]
            act.wait_ge(in_w, 16 * N_IN_W)
            act.activation(tanh_g[:, :], gates[:, :], ACT.Tanh).then_inc(tanh_in, 1)

            for j, (kind, i, engine) in enumerate(jobs):
                if engine != "act":
                    continue
                act.wait_ge(job_done, j + 1)
                if kind in ("q", "k", "ck") and i >= 2:
                    act.wait_ge(high_in, i - 1)
                src, dst = bank(j % 8), qk[:, i % 2, :]
                if kind == "ct":
                    act.activation(c_t[0:DC, i * BANK:(i + 1) * BANK], src[0:DC, :], ACT.Copy).then_inc(job_act, 1)
                elif kind == "bias":
                    act.activation(b_col[:, :], src[:, 0:4], ACT.Copy).then_inc(job_act, 1)
                elif kind == "q":
                    act.wait_ge(job_act, taken_count(job_at("bias", 0)))
                    act.activation(dst[:, 0:S], src[:, 0:S], ACT.Identity, bias=b_col[:, B_Q:B_Q + 1])
                    act.activation(dst[:, S:QW], src[:, S:QW], ACT.Identity,
                                   bias=b_col[:, B_CQ:B_CQ + 1]).then_inc(job_act, 1)
                elif kind == "k":
                    act.activation(dst[:, QW:QW + S], src[:, 0:S], ACT.Identity,
                                   bias=b_col[:, B_K:B_K + 1]).then_inc(job_act, 1)
                else:
                    act.activation(dst[:, QW + S:XW], src[:, :], ACT.Copy).then_inc(job_act, 1)

            for u in range(3 * NHEAD):
                head, w = u // 3, (S + P if u % 3 == 0 else BANK)
                act.wait_ge(s2_full, u + 1)
                if head >= NPT // 3:
                    act.wait_ge(pv_done, head - NPT // 3 + 1)
                act.activation(p_t[:, u % NPT, 0:w], bank(4 + u % 2)[:, 0:w], ACT.Exp, scale=SCALE).then_inc(p_in, 1)

            act.wait_ge(yt_full, 1)
            act.activation(y_t[:, 0:BANK], bank(0), ACT.Copy).then_inc(yt_act, 1)

            def take_ht(i):
                act.wait_ge(ht_full[i], 1)
                act.activation(h_t[:, 0:BANK], bank(0), ACT.Copy).then_inc(ht_act[i], 1)

            def experts(layer):
                units, _, trans_after, nj = ORDER[layer]
                take_ht(1 + 2 * layer)
                act.wait_ge(gap_in[layer], 1)
                act.activation(e_gap[:, :], gap[:, :], ACT.Exp).then_inc(e_gap_in[layer], 1)

                def take_weights(e, j):
                    k = nj * e + j
                    act.wait_ge(tr_full[layer], k + 1)
                    if e >= 2:
                        act.wait_ge(dn_full[layer], NHT * (e - 1))
                    w = tr_jobs(layer)[j]
                    if layer == 0:
                        dst = w_t[:, e % 2, w[0][0], :]
                        act.activation(dst, bank(k % 2), ACT.Copy).then_inc(wt_in[layer], 1)
                    else:
                        dst = w_t[:, e % 2, :, 0:P]
                        src = bank(k % 2)[:, 0:3 * P].rearrange("p (m f) -> p m f", m=3)
                        act.activation(dst, src, ACT.Copy).then_inc(wt_in[layer], 1)

                for j in range(nj):
                    take_weights(0, j)
                for i in range(len(units)):
                    act.wait_ge(gu_full[layer], i + 1)
                    if i >= 2:
                        act.wait_ge(hh_in[layer], i - 1)
                    act.activation(sg[:, i % 2, :], bank(2 + 2 * (i % 2)), ACT.Silu).then_inc(sg_in[layer], 1)
                    for e, j in trans_after.get(i, ()):
                        take_weights(e, j)

            experts(0)

            for j in range(2 * B):
                act.wait_ge(kv1_full, j + 1)
                src = bank(KV1_BANK[j])
                if j < B:
                    act.activation(k1_t[:, j * BANK:(j + 1) * BANK], src, ACT.Copy).then_inc(kv1_act, 1)
                else:
                    dst = v1[:, CT * (j - B):CT * (j - B + 1), :]
                    act.activation(dst, src.rearrange("p (t d) -> p t d", t=CT), ACT.Copy).then_inc(kv1_act, 1)
            take_ht(2)
            for s in range(NHT):
                act.wait_ge(q1_full, s + 1)
                act.activation(q1_t[:, s * BANK:(s + 1) * BANK], bank(4 + s), ACT.Identity,
                               bias=b_col[:, B_Q1:B_Q1 + 1]).then_inc(q1_act, 1)
            for t in range(NT):
                act.wait_ge(nm1_in, t + 1)
                if t >= 2:
                    act.wait_ge(p1t_full, t - 1)
                act.activation(p1[:, t % 2, :], bank(t % 2), ACT.Exp, bias=s1_nmax[:, t:t + 1],
                               accum_out=s1_sum[:, t:t + 1]).then_inc(p1_in, 1)
            experts(1)

        @block.vector
        def _(dve):
            link = linker(dve, dve_step)

            def norm(i, x, ready, counts):
                for t in range(NT):
                    if t in counts:
                        dve.wait_ge(ready, counts[t])
                    ins = dve.bn_stats(ln_stats[:, t, :], x[:, t, :])
                link(ins)
                for t in range(NT):
                    dve.bn_aggr(ln_mv[:, t, :], ln_stats[:, t, :]).then_inc(stats_in[i], 1)
                dve.wait_ge(rstd_in[i], 1)
                for t in range(NT):
                    dve.tensor_scalar(h_sb[:, t, :], x[:, t, :], ln_mv[:, t, 0:1], ln_rstd[:, t:t + 1],
                                      ALU.subtract, ALU.mult).then_inc(h_in[i], 1)

            norm(0, x_sb, in_x, {0: 16})

            for j, (kind, i, engine) in enumerate(jobs):
                if engine == "dve":
                    dve.wait_ge(job_done, j + 1)
                    src = bank(j % 8)
                    if kind == "xt":
                        dve.tensor_copy(h_t[:, i * BANK:(i + 1) * BANK], src).then_inc(job_dve, 1)
                    elif kind == "v":
                        if i == 0:
                            dve.wait_ge(in_w, 16 * N_IN_W)
                        dve.tensor_tensor(v_aug[:, QT * i:QT * (i + 1), :, 0:HD],
                                          src[:, 0:QT * D].rearrange("p (t h d) -> p t h d", t=QT, h=H),
                                          b_v[:, :].rearrange("p (h d) -> p h d", h=H).unsqueeze(1)
                                          .to_broadcast([P, QT, H, HD]), ALU.add).then_inc(job_dve, 1)
                    elif kind == "cv":
                        dve.tensor_copy(v_aug[:, NT + CT * i:NT + CT * (i + 1), :, 0:HD],
                                        src.rearrange("p (t h d) -> p t h d", t=CT, h=H)).then_inc(job_dve, 1)
                    else:
                        dve.tensor_copy(gw_t[:, :, :], src[:, 0:2 * E].rearrange("p (l e) -> p l e", l=2))\
                           .then_inc(job_dve, 1)
                if kind == "cv":
                    dve.wait_ge(job_act, taken_count(job_at("ck", i)))
                    if i >= 2:
                        dve.wait_ge(cat_in[i - 2], 32 * PAR * len(Q_PART))
                        dve.wait_ge(parts_in, i - 1)
                    link(dve.tensor_copy(parts[:, i % 2, 0, :], qk[:, i % 2, :]))
                    dve.tensor_tensor(qk_r[:, i % 2, :], qk[:, i % 2, :], parts[:, i % 2, 0, :],
                                      ALU.subtract).then_inc(high_in, 1)

            def split_max(b):
                dve.wait_ge(s1_free, split_after[b] + 1)
                whole = nmax[:, b % 2].rearrange("p t k (r q) -> p t (k r) q", q=PAIR)
                part = [nmax_p[:, b % 2, :, :, i, :] for i in range(3)]
                link(dve.tensor_copy(part[0], whole))
                link(dve.tensor_tensor(nmax_r[:, :, :, :], whole, part[0], ALU.subtract))
                link(dve.tensor_copy(part[1], nmax_r[:, :, :, :]))
                dve.tensor_tensor(part[2], nmax_r[:, :, :, :], part[1], ALU.subtract).then_inc(split_in, 1)

            def take_sums(n):
                dve.wait_ge(pv_done, HALF * (n + 1))
                if n >= 2:
                    dve.wait_ge(y_in, n - 1)
                flat = o_sb[:, n % 2].rearrange("p k t h d -> p (k t h d)")
                dve.tensor_copy(flat, bank(6 + n % 2)[:, 0:OW]).then_inc(o_taken, 1)
                dve.wait_ge(o_taken, n + 1)
                dve.reciprocal(o_rec[:, n % 2].rearrange("p k t h -> p (k t h)"),
                               o_sb[:, n % 2].rearrange("p k t h d -> p (k t h) d")[:, :, HD]).then_inc(rec_in, 1)

            sums_after = {}
            for n in range(NHEAD // HALF):
                sums_after.setdefault(min(pass1_before(HALF * (n + 1)) + 1, len(pass1) - 1), []).append(n)
            for i, u in enumerate(pass1):
                dve.wait_ge(s1_full, i + 1)
                src = bank(2 * (i % 2), 2)
                if u[0] == "turn":
                    if u[1] >= 2:
                        dve.wait_ge(mrow_in[u[1] - 2], 16 * 2 * PAR)
                    dve.tensor_copy(nmax_t[:, u[1] % 2, :],
                                    src[0:2 * PAR * 3 * PAIR, 0:S // 2].bitcast(BF16)).then_inc(s1_free, 1)
                else:
                    kind, b, t, g = u
                    n = {"cross": 1, "late": 2, "early": 4}[kind]
                    dst = nmax[:, b % 2, t, int(kind == "cross"), :].rearrange("p (r q) -> p r q", r=PAR)
                    dve.tensor_reduce(dst[:, :, n * g:n * (g + 1)],
                                      src.rearrange("p (r q k) -> p r q k", r=PAR, q=n),
                                      AX.X, ALU.max, negate=True).then_inc(s1_free, 1)
                    if i == split_after[b]:
                        split_max(b)
                for n in sums_after.get(i, ()):
                    take_sums(n)

            dve.wait_ge(yt_full, 2)
            dve.tensor_copy(y_t[:, BANK:TOK], bank(1)).then_inc(yt_dve, 1)
            dve.wait_ge(xb_in, 1)
            for s in range(NHT):
                half = x1_sb[:, s * TPH:(s + 1) * TPH, :].rearrange("p t d -> p (t d)")
                dve.wait_ge(proj_full, s + 1)
                dve.scalar_tensor_tensor(out=half, in0=bank(2 + s), scalar=tanh_g[:, 0:1], in1=half,
                                         op0=ALU.mult, op1=ALU.add).then_inc(x1_in, 1)

            def take_ht(i):
                dve.wait_ge(ht_full[i], 2)
                dve.tensor_copy(h_t[:, BANK:TOK], bank(1)).then_inc(ht_dve[i], 1)

            def choose(layer):
                dve.wait_ge(lg_full[layer], 1)
                src = bank(6)[:, 0:NT * E].rearrange("p (t e) -> p t e", t=NT)
                if layer == 0:
                    link(dve.tensor_copy(lg[:, :, :], src))
                else:
                    link(dve.tensor_tensor(lg[:, :, :], src, b_g[:, :].unsqueeze(1).to_broadcast([P, NT, E]), ALU.add))
                for t in range(NT):
                    ins = dve.max(top[:, t, :], lg[:, t, :])
                link(ins)
                dve.tensor_tensor(gap[:, :], top[:, :, 1], top[:, :, 0], ALU.subtract).then_inc(gap_in[layer], 1)
                for t in range(NT):
                    ins = dve.max_index(top_i[:, t, :], top[:, t, :], lg[:, t, :])
                link(ins)
                link(dve.tensor_copy(top_f[:, :, :], top_i[:, :, 0:2].rearrange("p t k -> p k t")))
                link(dve.tensor_tensor(pick[:, :, :, :].rearrange("p k t e -> p (k t) e"),
                                       iota_e[:, :].unsqueeze(1).to_broadcast([P, 2 * NT, E]),
                                       top_f[:, :, :].rearrange("p k t -> p (k t)").unsqueeze(2)
                                       .to_broadcast([P, 2 * NT, E]), ALU.is_equal))
                if layer == 0:
                    dve.tensor_copy(pick_b[:, :, :, :], pick[:, :, :, :]).then_inc(pick_in, 1)
                dve.wait_ge(e_gap_in[layer], 1)
                link(dve.tensor_scalar(w_top[:, 1, :], e_gap[:, :], 1.0, None, ALU.add))
                link(dve.reciprocal(w_top[:, 0, :], w_top[:, 1, :]))
                link(dve.tensor_tensor(w_top[:, 1, :], w_top[:, 0, :], e_gap[:, :], ALU.mult))
                link(dve.tensor_tensor(pick[:, :, :, :].rearrange("p k t e -> p (k t) e"),
                                       pick[:, :, :, :].rearrange("p k t e -> p (k t) e"),
                                       w_top[:, :, :].rearrange("p k t -> p (k t)").unsqueeze(2)
                                       .to_broadcast([P, 2 * NT, E]), ALU.mult))

            def combine(layer):
                if layer == 0:
                    dve.wait_ge(count_full, 1)
                    flat = "p k t e -> p (k t e)"
                    link(dve.tensor_scalar(fits[:, :, :, :].rearrange(flat), bank(7)[:, 0:2 * NT * E],
                                           float(CAPACITY) + 0.5, None, ALU.is_le))
                    link(dve.tensor_tensor(pick[:, :, :, :].rearrange(flat), pick[:, :, :, :].rearrange(flat),
                                           fits[:, :, :, :].rearrange(flat), ALU.mult))
                link(dve.tensor_tensor(comb[:, :, :], pick[:, 0, :, :], pick[:, 1, :, :], ALU.add))

            def experts(layer, x, x_out, x_out_in):
                units, down_after, _, _ = ORDER[layer]
                nf = nf_of(layer)
                choose(layer)

                def take_down(n):
                    e, s = n // NHT, n % NHT
                    dve.wait_ge(dn_full[layer], n + 1)
                    if e > 0:
                        dve.wait_ge(dn_taken[layer], n - 1)
                    for t in range(TPH):
                        src, dst = bank(6 + n % 2)[:, t * P:(t + 1) * P], acc[:, s * TPH + t, :]
                        weight = comb[:, s * TPH + t, e:e + 1]
                        if e == 0:
                            ins = dve.tensor_scalar(dst, src, weight, None, ALU.mult)
                        else:
                            ins = dve.scalar_tensor_tensor(out=dst, in0=src, scalar=weight, in1=dst,
                                                           op0=ALU.mult, op1=ALU.add)
                    ins.then_inc(dn_taken[layer], 1)

                for i, (e, s, f) in enumerate(units):
                    n = NHT * e + s
                    dve.wait_ge(sg_in[layer], i + 1)
                    if f == 0 and n >= 2:
                        dve.wait_ge(dn_full[layer], n - 1)
                    dve.tensor_tensor(hh[:, n % 2, f, :], bank(3 + 2 * (i % 2)), sg[:, i % 2, :],
                                      ALU.mult).then_inc(hh_in[layer], 1)
                    if i == COUNT_AFTER:
                        combine(layer)
                    for m in down_after.get(i, ()):
                        take_down(m)
                for s in range(NHT):
                    flat = "p t d -> p (t d)"
                    dve.wait_ge(dn_taken[layer], NHT * (E - 1) + s + 1)
                    half = slice(s * TPH, (s + 1) * TPH)
                    dve.scalar_tensor_tensor(out=x_out[:, half, :].rearrange(flat), in0=acc[:, half, :].rearrange(flat),
                                             scalar=tanh_g[:, 2 + layer:3 + layer], in1=x[:, half, :].rearrange(flat),
                                             op0=ALU.mult, op1=ALU.add).then_inc(x_out_in, 1)

            norm(1, x1_sb, x1_in, {0: 1, TPH: 2})
            take_ht(1)
            experts(0, x1_sb, x_sb, x2_in)

            norm(2, x_sb, x2_in, {0: 1, TPH: 2})
            take_ht(2)

            def max1(t):
                dve.wait_ge(sc1_full, t + 1)
                dve.tensor_reduce(s1_nmax[:, t:t + 1], bank(t % 2), AX.X, ALU.max, negate=True).then_inc(nm1_in, 1)

            max1(0)
            for t in range(NT):
                if t + 1 < NT:
                    max1(t + 1)
                dve.wait_ge(p1t_full, t + 1)
                if t >= 2:
                    dve.wait_ge(o1_full, t - 1)
                dve.tensor_copy(p1_t[:, t % 2, :], bank(2 + t % 2)).then_inc(p1t_in, 1)
                link(dve.reciprocal(s1_rec[:, t:t + 1], s1_sum[:, t:t + 1]))
                link(dve.tensor_tensor(s1_rec[:, t:t + 1], s1_rec[:, t:t + 1], tanh_g[:, 1:2], ALU.mult))
                dve.wait_ge(o1_full, t + 1)
                dve.scalar_tensor_tensor(out=x1_sb[:, t, :], in0=bank(4 + t % 2)[:, 0:D], scalar=s1_rec[:, t:t + 1],
                                         in1=x_sb[:, t, :], op0=ALU.mult, op1=ALU.add).then_inc(x3_in, 1)

            norm(3, x1_sb, x3_in, {t: t + 1 for t in range(NT)})
            take_ht(3)
            experts(1, x1_sb, x_sb, x4_in)

        @block.tensor
        def _(pe):
            pe.wait_ge(consts, 8)
            for j, (kind, i, engine) in enumerate(jobs):
                if j >= 8:
                    wait_taken(pe, j - 8)
                dst = bank(j % 8)
                if kind == "xt":
                    for t in range(4 * i, 4 * i + 4):
                        pe.wait_ge(h_in[0], t + 1)
                        ins = pe.transpose(dst[:, (t % 4) * P:(t % 4 + 1) * P], h_sb[:, t, :], ident[:, :])
                elif kind == "ct":
                    pe.wait_ge(in_ctx, 16)
                    for t in range(4 * i, 4 * i + 4):
                        ins = pe.transpose(dst[0:DC, (t % 4) * P:(t % 4 + 1) * P], c_sb[:, t, :], ident[:, :])
                elif kind == "bias":
                    pe.wait_ge(in_w, 16 * N_IN_W)
                    pe.wait_ge(perm_in, 5)
                    pe.transpose(dst[:, 0:3], b_perm[:, :], ident[0:3, 0:3])
                    ins = pe.transpose(dst[:, 3:4], b1_row[:, :], ident[0:1, 0:1])
                elif kind == "q":
                    if i == 0:
                        pe.wait_ge(in_w, 16 * N_IN_W)
                        for k in range(NT // 4):
                            wait_taken(pe, job_at("xt", k))
                        for k in range(NC // 4):
                            wait_taken(pe, job_at("ct", k))
                    for c in range(2):
                        ins = pe.matmul(dst[:, c * S:(c + 1) * S], w_perm[:, c, :],
                                        h_t[:, i * S:(i + 1) * S], start=True, stop=True)
                elif kind == "k":
                    ins = pe.matmul(dst[:, 0:S], w_perm[:, 2, :],
                                    h_t[:, i * S:(i + 1) * S], start=True, stop=True)
                elif kind == "ck":
                    ins = pe.matmul(dst, w_perm[0:DC + 1, 3, :],
                                    c_t[:, i * SC:(i + 1) * SC], start=True, stop=True)
                elif kind == "v":
                    for t in range(QT):
                        tok = (QT * i + t) * P
                        ins = pe.matmul(dst[:, t * P:(t + 1) * P], h_t[:, tok:tok + P], w_v[:, :],
                                        start=True, stop=True)
                elif kind == "cv":
                    for t in range(CT):
                        tok = (CT * i + t) * P
                        ins = pe.matmul(dst[:, t * P:(t + 1) * P], c_t[:, tok:tok + P], w_cv[:, :],
                                        start=True, stop=True)
                else:
                    for layer in range(2):
                        ins = pe.transpose(dst[:, layer * E:(layer + 1) * E], gw_rows[:, layer, :], ident[0:E, 0:E])
                ins.then_inc(job_done, 1)
            for j in range(len(jobs) - 8, len(jobs)):
                wait_taken(pe, j)

            def masked_scores(dst, q, k, width):
                pe.matmul(dst, q, k, start=True, stop=False, skip_group_check=True)
                return pe.matmul(dst[:, width - P:width], ident_b[:, :], mask_b[:, :], start=False, stop=True,
                                 skip_group_check=True)

            def pass1_unit(i):
                u = pass1[i]
                if i >= 2:
                    pe.wait_ge(s1_free, i - 1)
                first = 2 * (i % 2)
                if u[0] == "turn":
                    pe.wait_ge(split_in, u[1] + 1)
                    for t in range(QT):
                        dst = bank(first)[0:2 * PAR * 3 * PAIR, t * P // 2:(t + 1) * P // 2].bitcast(BF16)
                        src = nmax_p[:, u[1] % 2, t].rearrange("p k c q -> p (k c q)")
                        ins = pe.transpose(dst, src, ident_b[:, :])
                    ins.then_inc(s1_full, 1)
                    return
                kind, b, t, g = u
                if b == 0 or kind == "cross" and t == 0 and g == 0:
                    pe.wait_ge(cat_in[b], 32 * PAR * len(Q_PART))
                for par in range(PAR):
                    rows = slice(64 * par, 64 * par + ROWS)
                    dst = bank(first + par)
                    if kind == "cross":
                        ins = pe.matmul(dst, qcat[rows, b, g, S + t * P:S + (t + 1) * P], kcat[rows, b, g, S:KW],
                                        start=True, stop=True)
                    elif kind == "late":
                        for n in range(2):
                            ins = masked_scores(dst[:, n * S:(n + 1) * S], qcat[rows, b, 2 * g + n, P:S],
                                                kcat[rows, b, 2 * g + n, 0:S], S)
                    else:
                        for n in range(4):
                            ins = masked_scores(dst[:, n * P:(n + 1) * P], qcat[rows, b, 4 * g + n, 0:P],
                                                kcat[rows, b, 4 * g + n, 0:P], P)
                ins.then_inc(s1_full, 1)

            def scores2(head, part):
                b, h = head // H, head % H
                rows = slice(64 * (h % 2), 64 * (h % 2) + ROWS_M)
                u = 3 * head + part
                if u >= 2:
                    pe.wait_ge(p_in, u - 1)
                if head % H == 0 and part == 0:
                    pe.wait_ge(mrow_in[b], 16 * 2 * PAR)
                dst, q, k = bank(4 + u % 2), qcat[rows, b, h // 2, :], kcat[rows, b, h // 2, :]
                if part == 0:
                    pe.matmul(dst[:, 0:S], k[:, 0:P], q[:, 0:S], start=True, stop=True)
                    ins = pe.matmul(dst[:, S:S + P], k[:, P:S], q[:, P:S], start=True, stop=True)
                else:
                    for c in range(2):
                        key = S + (2 * (part - 1) + c) * P
                        ins = pe.matmul(dst[:, c * S:(c + 1) * S], k[:, key:key + P], q[:, S:QW],
                                        start=True, stop=True)
                ins.then_inc(s2_full, 1)

            def values(head, kind):
                b, h = head // H, head % H
                n = head // HALF
                slot = (3 * head) % NPT
                if kind == 0:
                    if head % HALF == 0 and n >= 2:
                        pe.wait_ge(o_taken, n - 1)
                    pe.wait_ge(masked, head + 1)
                else:
                    pe.wait_ge(p_in, 3 * head + 3)
                for t in range(QT):
                    col = ((kind * QT + t) * HALF + h % HALF) * HA
                    dst = bank(6 + n % 2)[:, col:col + HA]
                    if kind == 0:
                        blocks = [(p_t[:, slot, t * P:(t + 1) * P], QT * b)]
                        if t == 1:
                            blocks.append((p_t[:, slot, S:S + P], QT * b + 1))
                    else:
                        blocks = [(p_t[:, slot + 1 + c // 2, (c % 2) * S + t * P:(c % 2) * S + (t + 1) * P],
                                   NT + CT * b + c) for c in range(CT)]
                    for c, (p, v) in enumerate(blocks):
                        ins = pe.matmul(dst, p, v_aug[:, v, h, :], start=(c == 0), stop=(c == len(blocks) - 1))
                if kind == 1:
                    ins.then_inc(pv_done, 1)

            pe.wait_ge(ones_in, 16 * B * PAR)
            done = 0
            for head in range(NHEAD + 1):
                while done < pass1_before(head):
                    pass1_unit(done)
                    done += 1
                if head < NHEAD:
                    scores2(head, 0)
                    scores2(head, 1)
                if head > 0:
                    values(head - 1, 0)
                if head < NHEAD:
                    scores2(head, 2)
                if head > 0:
                    values(head - 1, 1)

            pe.wait_ge(s1_free, len(pass1))
            for s in range(NHT):
                for t in range(TPH):
                    pe.wait_ge(y_in, 2 * ((s * TPH + t) // QT + 1))
                    ins = pe.transpose(bank(s)[:, t * P:(t + 1) * P], y_sb[:, s * TPH + t, :], ident[:, :])
                ins.then_inc(yt_full, 1)
            for s in range(NHT):
                pe.wait_ge([yt_act, yt_dve][s], 1)
                for t in range(TPH):
                    tok = (s * TPH + t) * P
                    ins = pe.matmul(bank(2 + s)[:, t * P:(t + 1) * P], y_t[:, tok:tok + P], w_p[:, :],
                                    start=True, stop=True)
                ins.then_inc(proj_full, 1)

            def transpose_h(i):
                for s in range(NHT):
                    for t in range(TPH):
                        pe.wait_ge(h_in[i], s * TPH + t + 1)
                        ins = pe.transpose(bank(s)[:, t * P:(t + 1) * P], h_sb[:, s * TPH + t, :], ident[:, :])
                    ins.then_inc(ht_full[i], 1)
                pe.wait_ge(ht_act[i], 1)
                pe.wait_ge(ht_dve[i], 1)

            def experts(layer):
                units, down_after, trans_after, nj = ORDER[layer]
                nf = nf_of(layer)
                transpose_h(1 + 2 * layer)
                for t in range(NT):
                    ins = pe.matmul(bank(6)[:, t * E:(t + 1) * E], h_t[:, t * P:(t + 1) * P], gw_t[:, layer, :],
                                    start=True, stop=True)
                ins.then_inc(lg_full[layer], 1)

                def transpose_weights(e, j):
                    k = nj * e + j
                    if j == 0:
                        pe.wait_ge(raw_in[layer][e % NRAW], 48 * (e // NRAW + 1))
                    if k >= 2:
                        pe.wait_ge(wt_in[layer], k - 1)
                    for c, (m, f) in enumerate(tr_jobs(layer)[j]):
                        ins = pe.transpose(bank(k % 2)[:, c * P:(c + 1) * P], raw[:, e % NRAW, m, f, :], ident[:, :])
                    ins.then_inc(tr_full[layer], 1)

                def go_down(n):
                    e, s = n // NHT, n % NHT
                    pe.wait_ge(wt_in[layer], nj * (e + 1))
                    pe.wait_ge(hh_in[layer], nf * (n + 1))
                    if n >= 2:
                        pe.wait_ge(dn_taken[layer], n - 1)
                    for t in range(TPH):
                        for f in range(nf):
                            ins = pe.matmul(bank(6 + n % 2)[:, t * P:(t + 1) * P], hh[:, n % 2, f, t * P:(t + 1) * P],
                                            w_t[:, e % 2, 2, f * P:(f + 1) * P], start=(f == 0), stop=(f == nf - 1))
                    ins.then_inc(dn_full[layer], 1)

                for j in range(nj):
                    transpose_weights(0, j)
                for i, (e, s, f) in enumerate(units):
                    if s == 0 and f == 0:
                        pe.wait_ge(wt_in[layer], nj * e + (2 if layer == 0 else 1))
                    if i >= 2:
                        pe.wait_ge(hh_in[layer], i - 1)
                    for m in range(2):
                        ins = pe.matmul(bank(2 + 2 * (i % 2) + m), w_t[:, e % 2, m, f * P:(f + 1) * P],
                                        h_t[:, s * BANK:(s + 1) * BANK], start=True, stop=True)
                    ins.then_inc(gu_full[layer], 1)
                    if i == COUNT_AFTER and layer == 0:
                        pe.wait_ge(pick_in, 1)
                        dst = bank(7)[:, 0:2 * NT * E].rearrange("p (k t e) -> p k t e", k=2, t=NT)
                        pe.matmul(dst, upto_b[:, :], pick_b[:, :, :, :], start=True, stop=False, skip_group_check=True)
                        for d in range(1, NT):
                            ins = pe.matmul(dst[:, :, d:NT, :], ones_b[:, 0:P], pick_b[:, :, 0:NT - d, :],
                                            start=False, stop=(d == NT - 1), skip_group_check=True)
                        ins.then_inc(count_full, 1)
                    for n in down_after.get(i, ()):
                        go_down(n)
                    for w in trans_after.get(i, ()):
                        transpose_weights(*w)

            experts(0)

            for j in range(2 * B):
                if KV1_BANK[j] in (6, 7):
                    pe.wait_ge(dn_taken[0], NHT * E)
                if j in (6, 7):
                    pe.wait_ge(kv1_act, j - 5)
                if j == 0:
                    pe.wait_ge(hh_in[0], len(ORDER[0][0]))
                dst = bank(KV1_BANK[j])
                if j < B:
                    ins = pe.matmul(dst, w1_k[:, :], c_t[:, j * SC:(j + 1) * SC], start=True, stop=True)
                else:
                    for c in range(CT):
                        tok = (CT * (j - B) + c) * P
                        ins = pe.matmul(dst[:, c * P:(c + 1) * P], c_t[:, tok:tok + P], w1_v[:, :],
                                        start=True, stop=True)
                ins.then_inc(kv1_full, 1)
            transpose_h(2)
            pe.wait_ge(kv1_act, 2 * B)
            for s in range(NHT):
                pe.matmul(bank(4 + s), w1_q[:, :], h_t[:, s * BANK:(s + 1) * BANK],
                          start=True, stop=True).then_inc(q1_full, 1)
            pe.wait_ge(q1_act, NHT)

            def scores1(t):
                if t >= 2:
                    pe.wait_ge(p1_in, t - 1)
                b = t // QT
                pe.matmul(bank(t % 2), q1_t[:, t * P:(t + 1) * P], k1_t[:, b * SC:(b + 1) * SC],
                          start=True, stop=True).then_inc(sc1_full, 1)

            scores1(0)
            for t in range(NT):
                if t + 1 < NT:
                    scores1(t + 1)
                pe.wait_ge(p1_in, t + 1)
                if t >= 2:
                    pe.wait_ge(p1t_in, t - 1)
                for c in range(CT):
                    ins = pe.transpose(bank(2 + t % 2)[:, c * P:(c + 1) * P], p1[:, t % 2, c * P:(c + 1) * P], ident[:, :])
                ins.then_inc(p1t_full, 1)
                pe.wait_ge(p1t_in, t + 1)
                if t >= 2:
                    pe.wait_ge(x3_in, t - 1)
                for c in range(CT):
                    ins = pe.matmul(bank(4 + t % 2)[:, 0:D], p1_t[:, t % 2, c * P:(c + 1) * P], v1[:, CT * (t // QT) + c, :],
                                    start=(c == 0), stop=(c == CT - 1))
                ins.then_inc(o1_full, 1)
            experts(1)


_INS = ['x', 'ctx_512', 'g_xattn', 'g_ffn', 'L0_xattn_Wk', 'L0_xattn_bk', 'L0_xattn_Wq', 'L0_xattn_bq', 'L0_xattn_Wv',
        'L0_xattn_bv', 'L0_xattn_Wck', 'L0_xattn_bck', 'L0_xattn_Wcq', 'L0_xattn_bcq', 'L0_xattn_Wcv', 'L0_xattn_bcv',
        'L0_xattn_Wp', 'L0_xattn_bp', 'L0_ffn_gate_w', 'L0_ffn_wi_gate', 'L0_ffn_wi_up', 'L0_ffn_wo', 'L1_xattn_Wq',
        'L1_xattn_bq', 'L1_xattn_Wk', 'L1_xattn_bk', 'L1_xattn_Wv', 'L1_xattn_bv', 'L1_ffn_Wg', 'L1_ffn_bg',
        'L1_ffn_w1', 'L1_ffn_w2']


def kernel(**inputs):
    import numpy as _np
    import concourse.bacc as _bacc
    from concourse import mybir as _mybir
    from concourse.bass_utils import run_bass_kernel_spmd as _run

    nc = _bacc.Bacc("TRN2", target_bir_lowering=False, num_devices=1)
    arrays, aps = {}, {}
    for name in _INS:
        arr = _np.ascontiguousarray(inputs[name])
        arrays[f"in_{name}_dram"] = arr
        aps[name] = nc.dram_tensor(f"in_{name}_dram", arr.shape, _mybir.dt.from_np(arr.dtype),
                                   kind="ExternalInput").ap()
    out = nc.dram_tensor("out_0_dram", inputs["x"].shape, _mybir.dt.float32, kind="ExternalOutput").ap()
    flamingo_gated_kernel(nc, aps, out)
    r = _run(nc, [arrays], core_ids=[0])
    return r.results[0]["out_0_dram"]
```

```python
from contextlib import ExitStack

import concourse.bass as bass
from concourse import mybir

F32 = mybir.dt.float32
BF16 = mybir.dt.bfloat16
U32 = mybir.dt.uint32
ALU = mybir.AluOpType
ACT = mybir.ActivationFunctionType
AX = mybir.AxisListType

P = 128
BANK = 512
EPS = 1e-5
CAPACITY_FACTOR = 1.25
NEG = -1.0e30

Q_PART = (0, 0, 0, 1, 1, 2)
K_PART = (0, 1, 2, 0, 1, 0)
B_Q, B_CQ, B_K, B_Q1 = range(4)


def flamingo_gated_kernel(nc, a, out):
    B, S, D = a["x"].shape
    SC, DC = a["ctx_512"].shape[1:]
    H = 16
    HD = D // H
    SCALE = float(HD) ** -0.5
    NT = B * S // P
    QT = S // P
    NC = B * SC // P
    CT = SC // P
    TOK = B * S
    E = a["L0_ffn_gate_w"].shape[0]
    NF0 = a["L0_ffn_wi_gate"].shape[1] // P
    NF1 = a["L1_ffn_w1"].shape[1] // 2 // P
    CAPACITY = max(int(TOK / E * CAPACITY_FACTOR), 1)
    assert D == P and QT == 2 and CT == 4 and NF1 == 1 and NF0 == 4 and E == 8 and HD == 8

    PAIR, PAR = H // 2, 2
    ROWS = HD * len(Q_PART)
    ROWS_M = ROWS + 3
    QW = 2 * S
    KW = S + SC
    XW = QW + KW
    HA = HD + 1
    QUAD = 4
    NPT = 2 * 3 * QUAD

    ctx = ExitStack()
    with ctx:
        def sb(name, shape, dt=F32):
            return ctx.enter_context(nc.sbuf_tensor(name, shape, dt))

        def sem(name):
            return ctx.enter_context(nc.semaphore(name))

        x_sb = sb("x_sb", [P, NT, D])
        w_q = sb("w_q", [P, D])
        w_k = sb("w_k", [P, D])
        w_cq = sb("w_cq", [P, D])
        w_v = sb("w_v", [P, D])
        w_p = sb("w_p", [P, D])
        w_ck = sb("w_ck", [DC + 1, D])
        w_cv = sb("w_cv", [DC + 1, D])
        w1_q = sb("w1_q", [P, D])
        w1_k = sb("w1_k", [DC + 1, D])
        w1_v = sb("w1_v", [DC + 1, D])
        w_perm = sb("w_perm", [P, 4, D])
        b_perm = sb("b_perm", [3, D])
        b_rows = sb("b_rows", [3, D])
        b1_row = sb("b1_row", [1, D])
        b_col = sb("b_col", [P, 4])
        b_v = sb("b_v", [P, D])
        b_p = sb("b_p", [P, D])
        b_g = sb("b_g", [P, E])
        gates = sb("gates", [P, 4])
        tanh_g = sb("tanh_g", [P, 4])
        gw_rows = sb("gw_rows", [E, 2, D])
        gw_t = sb("gw_t", [P, 2, E])

        ident = sb("ident", [P, P])
        ident_b = sb("ident_b", [P, P], BF16)
        mask_b = sb("mask_b", [P, P], BF16)
        upto_b = sb("upto_b", [P, P], BF16)
        ones_b = sb("ones_b", [P, KW], BF16)
        iota_e = sb("iota_e", [P, E])
        half_neg = sb("half_neg", [P, NT])
        bp_g = sb("bp_g", [P, D])

        ln_stats = sb("ln_stats", [P, NT, 6])
        ln_mv = sb("ln_mv", [P, NT, 2])
        ln_rstd = sb("ln_rstd", [P, NT])
        h_sb = sb("h_sb", [P, NT, D])
        h_t = sb("h_t", [P, TOK])
        c_t = sb("c_t", [DC + 1, NC * P])

        qk = sb("qk", [P, 2, XW])
        qk_r = sb("qk_r", [P, 2, XW])
        parts = sb("parts", [P, 3, B, XW], BF16)
        qcat = sb("qcat", [P, PAIR, B, QW], BF16)
        kcat = sb("kcat", [P, PAIR, B, KW], BF16)
        c_sb = qcat[:, 0].rearrange("p b n -> p (b n)").bitcast(F32).rearrange("p (t d) -> p t d", t=NC)
        v_aug = sb("v_aug", [P, NT + NC, H, HA])

        p_slots = [x.rearrange("p (s n) -> p s n", n=BANK)[:, i, :]
                   for x, m in ((qk[:, :, :].rearrange("p s n -> p (s n)"), 2 * XW // BANK),
                                (qk_r[:, :, :].rearrange("p s n -> p (s n)"), 2 * XW // BANK),
                                (parts[:, :, :, :].rearrange("p c b n -> p (c b n)").bitcast(F32),
                                 3 * B * XW // 2 // BANK)) for i in range(m)][0:NPT]
        ot_sb = sb("ot_sb", [P, BANK])
        nmax = sb("nmax", [P, 2, QT, 2, H])
        nmax_r = sb("nmax_r", [P, QT, 2 * PAR, PAIR])
        nmax_p = sb("nmax_p", [P, 2, QT, 2 * PAR, 3, PAIR], BF16)
        nmax_t = sb("nmax_t", [2 * PAR * 3 * PAIR, 2, S], BF16)
        o_sb = sb("o_sb", [P, 2, 2 * QT, QUAD, HA])
        o_rec = sb("o_rec", [P, 2, 2 * QT, QUAD])
        o_n = sb("o_n", [P, 2, 2 * QT, QUAD, HD])
        y_sb, y_t = h_sb, h_t
        x1_sb = sb("x1_sb", [P, NT, D])

        lg = sb("lg", [P, NT, E])
        top = sb("top", [P, NT, 8])
        top_i = sb("top_i", [P, NT, 8], U32)
        top_f = sb("top_f", [P, 2, NT])
        gap = sb("gap", [P, NT])
        e_gap = sb("e_gap", [P, NT])
        w_top = sb("w_top", [P, 2, NT])
        pick = sb("pick", [P, 2, NT, E])
        pick_b = sb("pick_b", [P, 2, NT, E], BF16)
        fits = sb("fits", [P, 2, NT, E])
        comb2 = sb("comb2", [P, 2, NT, E])
        comb = sb("comb", [P, NT, E])
        NRAW = 2
        raw = sb("raw", [P, NRAW, 3, NF0, P])

        def region(x, first, n):
            return x[:, :, :, :].rearrange("p a b n -> p (a b n)").bitcast(F32)[:, first:first + n]

        n_wt, n_hh = 2 * 3 * NF0 * P, 2 * NF0 * BANK
        w_t = region(kcat, 0, n_wt).rearrange("p (s m f) -> p s m f", s=2, m=3)
        hh = region(kcat, n_wt, n_hh).rearrange("p (s f k) -> p s f k", s=2, f=NF0)
        k1_t = region(kcat, n_wt + n_hh, NC * P)
        sg = region(qcat, 0, 2 * BANK).rearrange("p (s k) -> p s k", s=2)
        acc = region(qcat, 2 * BANK, NT * D).rearrange("p (t d) -> p t d", t=NT)
        v1 = region(qcat, 2 * BANK + NT * D, NC * D).rearrange("p (t d) -> p t d", t=NC)

        q1_t = h_sb[:, :, :].rearrange("p t d -> p (t d)")
        p1 = qk[:, :, 0:SC]
        p1_t = qk_r[:, :, 0:SC]
        s1_nmax = sb("s1_nmax", [P, NT])
        s1_sum = sb("s1_sum", [P, NT])
        s1_rec = sb("s1_rec", [P, NT])

        psum = ctx.enter_context(nc.psum_tensor("psum", [P, 8 * BANK], F32))

        def bank(i, n=1):
            return psum[:, i * BANK:(i + n) * BANK]

        in_x = sem("in_x")
        in_ctx = sem("in_ctx")
        in_w = sem("in_w")
        in_late = sem("in_late")
        consts = sem("consts")
        ones_in = sem("ones_in")
        perm_in = sem("perm_in")
        tanh_in = sem("tanh_in")
        stats_in = [sem(f"stats_in{i}") for i in range(4)]
        rstd_in = [sem(f"rstd_in{i}") for i in range(4)]
        h_in = [sem(f"h_in{i}") for i in range(4)]
        job_done = sem("job_done")
        job_act = sem("job_act")
        job_dve = sem("job_dve")
        high_in = sem("high_in")
        parts_in = sem("parts_in")
        cat_in = [sem(f"cat_in{n}") for n in range(B)]
        cat_pool = [sem(f"cat_pool{n}") for n in range(2)]
        s1_full = sem("s1_full")
        s1_free = sem("s1_free")
        split_in = sem("split_in")
        mrow_in = [sem(f"mrow_in{b}") for b in range(B)]
        s2_full = sem("s2_full")
        p_in = sem("p_in")
        masked = sem("masked")
        pv_done = sem("pv_done")
        ot_in = sem("ot_in")
        o_full = sem("o_full")
        o_clear = sem("o_clear")
        o_taken = sem("o_taken")
        rec_in = sem("rec_in")
        y_in = sem("y_in")
        xb_in = sem("xb_in")
        yt_full = sem("yt_full")
        yt_act = sem("yt_act")
        yt_dve = sem("yt_dve")
        proj_full = sem("proj_full")
        x1_in = sem("x1_in")
        x2_in = sem("x2_in")
        x3_in = sem("x3_in")
        x4_in = sem("x4_in")
        ht_full = [sem(f"ht_full{i}") for i in range(4)]
        ht_act = [sem(f"ht_act{i}") for i in range(4)]
        ht_dve = [sem(f"ht_dve{i}") for i in range(4)]
        lg_full = [sem(f"lg_full{i}") for i in range(2)]
        gap_in = [sem(f"gap_in{i}") for i in range(2)]
        e_gap_in = [sem(f"e_gap_in{i}") for i in range(2)]
        pick_in = sem("pick_in")
        count_full = sem("count_full")
        raw_in = [[sem(f"raw_in{i}_{r}") for r in range(NRAW)] for i in range(2)]
        tr_full = [sem(f"tr_full{i}") for i in range(2)]
        wt_in = [sem(f"wt_in{i}") for i in range(2)]
        gu_full = [sem(f"gu_full{i}") for i in range(2)]
        sg_in = [sem(f"sg_in{i}") for i in range(2)]
        hh_in = [sem(f"hh_in{i}") for i in range(2)]
        dn_full = [sem(f"dn_full{i}") for i in range(2)]
        dn_taken = [sem(f"dn_taken{i}") for i in range(2)]
        kv1_full = sem("kv1_full")
        kv1_act = sem("kv1_act")
        q1_full = sem("q1_full")
        q1_act = sem("q1_act")
        sc1_full = sem("sc1_full")
        nm1_in = sem("nm1_in")
        p1_in = sem("p1_in")
        p1t_full = sem("p1t_full")
        p1t_in = sem("p1t_in")
        o1_full = sem("o1_full")
        stored = sem("stored")
        dve_step = sem("dve_step")
        act_step = sem("act_step")
        pool_step = sem("pool_step")

        def linker(eng, s):
            count = [0]

            def link(ins):
                count[0] += 1
                ins.then_inc(s, 1)
                eng.wait_ge(s, count[0])
            return link

        jobs = [("ct", i, "act") for i in range(NC // 4)] + [("bias", 0, "act")]
        jobs += [("ck", 0, "act"), ("cv", 0, "dve"), ("cv", 1, "dve")] + [("xt", i, "dve") for i in range(NT // 4)]
        for b in range(B):
            jobs += [("ck", b, "act")] * (b > 0) + [("q", b, "act"), ("k", b, "act"), ("v", b, "dve")]
            jobs += [("cv", b, "dve")] * (b > 1)
        jobs += [("gw", 0, "dve")]

        def job_at(kind, index):
            return [j for j, (k, i, _) in enumerate(jobs) if (k, i) == (kind, index)][0]

        def taken_count(j):
            return sum(e == jobs[j][2] for _, _, e in jobs[:j + 1])

        def wait_taken(eng, j):
            eng.wait_ge(job_dve if jobs[j][2] == "dve" else job_act, taken_count(j))

        POOL_LAYS = 2

        def units_of(b):
            u = [("cross", b, t, pair) for t in range(QT) for pair in range(PAIR)]
            u += [("late", b, 1, g) for g in range(PAIR // 2)]
            return u + [("early", b, 0, g) for g in range(PAIR // 4)]

        TURN_LAG = 3
        N1 = len(units_of(0))
        pass1 = []
        for b in range(B):
            u = units_of(b)
            if b:
                u.insert(TURN_LAG, ("turn", b - 1))
            pass1 += u
        pass1.append(("turn", B - 1))
        turn_at = {u[1]: i for i, u in enumerate(pass1) if u[0] == "turn"}
        split_after = {b: max(i for i, u in enumerate(pass1) if u[0] != "turn" and u[1] == b) for b in range(B)}
        LEAD = N1 + 9

        def pass1_before(head):
            return min(len(pass1), LEAD + -(-head * (N1 + 1) // H))

        NHEAD = B * H

        def q_cols(kind):
            return kind * S

        def k_cols(kind):
            return kind * S

        NHT = TOK // BANK
        TPH = BANK // P

        def expert_weights(layer, e):
            if layer == 0:
                return [a["L0_ffn_wi_gate"][e].rearrange("(n f) d -> f n d", f=P),
                        a["L0_ffn_wi_up"][e].rearrange("(n f) d -> f n d", f=P),
                        a["L0_ffn_wo"][e].rearrange("d (n f) -> d n f", f=P)]
            return [a["L1_ffn_w1"][e, 0:P, :].unsqueeze(1), a["L1_ffn_w1"][e, P:2 * P, :].unsqueeze(1),
                    a["L1_ffn_w2"][e].unsqueeze(1)]

        def nf_of(layer):
            return NF0 if layer == 0 else NF1

        def tr_jobs(layer):
            if layer == 0:
                return [[(m, n) for n in range(NF0)] for m in range(3)]
            return [[(m, 0) for m in range(3)]]

        block = ctx.enter_context(nc.Block())

        def experts_of(layer):
            nf = nf_of(layer)
            units = [(e, s, f) for e in range(E) for s in range(NHT) for f in range(nf)]
            lag = 2 if layer == 0 else 1
            down_after = {}
            trans_after = {}
            per = NHT * nf
            nj = len(tr_jobs(layer))
            for n in range(E * NHT):
                down_after.setdefault(min((n + 1) * nf - 1 + lag, len(units) - 1), []).append(n)
            for e in range(1, E):
                for j in range(nj):
                    at = (e - 1) * per + (3 + j if layer == 0 else 1)
                    trans_after.setdefault(at, []).append((e, j))
            return units, down_after, trans_after, nj

        O_BANK, OT_BANK = 6, 7
        TAKE_AT = 1
        N_CONSTS = 8
        COUNT_AFTER = 1
        KV1_BANK = [2, 3, 4, 5, 6, 7, 2, 3]
        N_CAT = 16 * 2 * PAR * len(Q_PART)
        N_IN_LATE = 11
        N_IN_W = 14

        ORDER = [experts_of(layer) for layer in range(2)]

        def lay_out(eng, b, par, laid):
            half = slice(64 * par, 64 * par + 64)
            for r in range(len(Q_PART)):
                rows = slice(64 * par + HD * r, 64 * par + HD * (r + 1))
                eng.dma_start(qcat[rows, :, b, :], parts[half, Q_PART[r], b, 0:QW]).then_inc(laid, 16)
                eng.dma_start(kcat[rows, :, b, :], parts[half, K_PART[r], b, QW:XW]).then_inc(laid, 16)

        def wait_laid(eng, b):
            if b < POOL_LAYS:
                eng.wait_ge(cat_in[b], N_CAT // 2)
                eng.wait_ge(cat_pool[b], N_CAT // 2)
            else:
                eng.wait_ge(cat_in[b], N_CAT)

        @block.sync
        def _(sp):
            sp.dma_start(x_sb[:, :, :], a["x"].rearrange("b (t p) d -> p (b t) d", p=P)).then_inc(in_x, 16)
            sp.dma_start(c_sb[:, :, :], a["ctx_512"].rearrange("b (t p) d -> p (b t) d", p=P)).then_inc(in_ctx, 16)
            for b in range(B):
                sp.wait_ge(parts_in, b + 1)
                for par in range(1 if b < POOL_LAYS else PAR):
                    lay_out(sp, b, par, cat_in[b])
                if b == 0:
                    for e in range(NRAW):
                        for m, w in enumerate(expert_weights(0, e)):
                            sp.dma_start(raw[:, e, m, :, :], w).then_inc(raw_in[0][e], 16)
            for b in range(B):
                sp.wait_ge(s1_free, turn_at[b] + 1)
                for kind in range(2):
                    for par in range(PAR):
                        r = 3 * PAIR * (PAR * kind + par)
                        sp.dma_start(qcat[64 * par + ROWS:64 * par + ROWS_M, :, b, kind * S:kind * S + S],
                                     nmax_t[r:r + 3 * PAIR, b % 2, :]).then_inc(mrow_in[b], 16)
            for layer in range(2):
                nj = len(tr_jobs(layer))
                for e in range(NRAW if layer == 0 else 0, E):
                    if layer == 1 and e < NRAW:
                        sp.wait_ge(tr_full[0], len(tr_jobs(0)) * (E - NRAW + e + 1))
                    else:
                        sp.wait_ge(tr_full[layer], nj * (e - NRAW + 1))
                    for m, w in enumerate(expert_weights(layer, e)):
                        sp.dma_start(raw[:, e % NRAW, m, 0:nf_of(layer), :], w).then_inc(raw_in[layer][e % NRAW], 16)
            out_v = out.rearrange("b (t p) d -> p (b t) d", p=P)
            for s in range(NHT):
                sp.wait_ge(x4_in, s + 1)
                sp.dma_start(out_v[:, s * TPH:(s + 1) * TPH, :], x_sb[:, s * TPH:(s + 1) * TPH, :]).then_inc(stored, 16)
            sp.wait_ge(stored, 16 * NHT)

        @block.gpsimd
        def _(pool):
            link = linker(pool, pool_step)
            count = [0]

            def load(dst, src):
                pool.dma_start(dst, src).then_inc(in_late, 16)
                count[0] += 1

            made = [0]

            def const(ins):
                made[0] += 1
                ins.then_inc(consts, 1)
                pool.wait_ge(consts, made[0])

            const(pool.memset(ones_b[:, :], 1.0))
            for par in range(PAR):
                r = 64 * par + ROWS
                pool.dma_start(kcat[r:r + 3, :, :, :], ones_b[0:3 * PAIR * B, :]).then_inc(ones_in, 16)
            link(pool.memset(ident[:, :], 0.0))
            link(pool.affine_select(out=ident[:, :], in_=ident[:, :], pattern=[[-1, P]], compare_op=ALU.not_equal,
                                    fill=1.0, base=0, channel_multiplier=1))
            const(pool.memset(half_neg[:, :], -0.5))
            const(pool.memset(c_t[DC:DC + 1, :], 1.0))
            const(pool.tensor_copy(ident_b[:, :], ident[:, :]))

            def rstd(i):
                pool.wait_ge(stats_in[i], NT)
                link(pool.tensor_scalar(ln_rstd[:, :], ln_mv[:, :, 1], EPS, None, ALU.add))
                pool.tensor_tensor(ln_rstd[:, :], ln_rstd[:, :], half_neg[:, :], ALU.pow).then_inc(rstd_in[i], 1)

            rstd(0)
            pool.wait_ge(in_w, 16 * N_IN_W)
            for dst, src in ((w_perm[:, 0, :], w_q), (w_perm[:, 1, :], w_cq), (w_perm[:, 2, :], w_k),
                             (w_perm[0:DC + 1, 3, :], w_ck), (b_perm[:, :], b_rows)):
                pool.tensor_copy(dst.rearrange("k (par d pair) -> k par d pair", pair=PAIR, par=PAR),
                                 src[:, :].rearrange("k (pair par d) -> k par d pair", pair=PAIR, par=PAR))\
                    .then_inc(perm_in, 1)
            pool.wait_ge(perm_in, 5)
            link(pool.memset(mask_b[:, :], 0.0))
            const(pool.affine_select(out=mask_b[:, :], in_=mask_b[:, :], pattern=[[-1, P]], compare_op=ALU.is_ge,
                                     fill=NEG, base=0, channel_multiplier=1))
            const(pool.affine_select(out=upto_b[:, :], in_=ones_b[:, 0:P], pattern=[[1, P]], compare_op=ALU.is_ge,
                                     fill=0.0, base=0, channel_multiplier=-1))
            const(pool.iota(iota_e[:, :], pattern=[[1, E]], base=0, channel_multiplier=0,
                            allow_small_or_imprecise_dtypes=True))
            const(pool.memset(v_aug[:, :, :, HD:HA], 1.0))

            load(w_p[:, :], a["L0_xattn_Wp"])
            load(b_p[:, :], a["L0_xattn_bp"].partition_broadcast(P))
            load(gw_rows[:, 0, :], a["L0_ffn_gate_w"])
            load(gw_rows[:, 1, :], a["L1_ffn_Wg"])
            load(b_g[:, :], a["L1_ffn_bg"].partition_broadcast(P))
            load(w1_q[:, :], a["L1_xattn_Wq"])
            load(b1_row[:, :], a["L1_xattn_bq"].unsqueeze(0))
            for w, n in ((w1_k, "k"), (w1_v, "v")):
                load(w[0:DC, :], a["L1_xattn_W" + n])
                load(w[DC:DC + 1, :], a["L1_xattn_b" + n].unsqueeze(0))
            assert count[0] == N_IN_LATE, count[0]
            for b in range(B):
                pool.wait_ge(high_in, b + 1)
                link(pool.tensor_copy(parts[:, 1, b, :], qk_r[:, b % 2, :]))
                pool.tensor_tensor(parts[:, 2, b, :], qk_r[:, b % 2, :], parts[:, 1, b, :],
                                   ALU.subtract).then_inc(parts_in, 1)
                if b < POOL_LAYS:
                    pool.wait_ge(parts_in, b + 1)
                    lay_out(pool, b, 1, cat_pool[b])

            pool.wait_ge(in_late, 16 * N_IN_LATE)
            pool.wait_ge(tanh_in, 1)
            link(pool.tensor_scalar(bp_g[:, :], b_p[:, :], tanh_g[:, 0:1], None, ALU.mult))
            pool.tensor_tensor(x1_sb[:, :, :], x_sb[:, :, :], bp_g[:, :].unsqueeze(1).to_broadcast([P, NT, D]),
                               ALU.add).then_inc(xb_in, 1)

            def normalise(n):
                pool.wait_ge(rec_in, n + 1)
                link(pool.tensor_tensor(o_n[:, n % 2].rearrange("p k h d -> p (k h) d"),
                                        o_sb[:, n % 2].rearrange("p k h d -> p (k h) d")[:, :, 0:HD],
                                        o_rec[:, n % 2].rearrange("p k h -> p (k h)").unsqueeze(2)
                                        .to_broadcast([P, 2 * QT * QUAD, HD]), ALU.mult))
                b, at = n // (H // QUAD), n % (H // QUAD) * QUAD * HD
                pool.tensor_tensor(y_sb[:, QT * b:QT * (b + 1), at:at + QUAD * HD],
                                   o_n[:, n % 2, 0:QT].rearrange("p t h d -> p t (h d)"),
                                   o_n[:, n % 2, QT:2 * QT].rearrange("p t h d -> p t (h d)"),
                                   ALU.add).then_inc(y_in, 1)

            for head in range(NHEAD):
                pool.wait_ge(p_in, 3 * head + 1)
                diag = p_slots[(3 * head) % NPT].rearrange("p (c q) -> p c q", q=P)[:, 0:3:2, :]
                pool.affine_select(out=diag, in_=diag, pattern=[[0, 2], [1, P]], compare_op=ALU.is_ge, fill=0.0,
                                   base=0, channel_multiplier=-1).then_inc(masked, 1)
                if head % QUAD == QUAD - 1 and head >= 3 * QUAD:
                    normalise(head // QUAD - 3)
            normalise(NHEAD // QUAD - 3)
            normalise(NHEAD // QUAD - 2)
            normalise(NHEAD // QUAD - 1)
            for i in range(1, 4):
                rstd(i)

        @block.scalar
        def _(act):
            link = linker(act, act_step)
            count = [0]

            def load(dst, src):
                act.dma_start(dst, src).then_inc(in_w, 16)
                count[0] += 1

            load(w_ck[0:DC, :], a["L0_xattn_Wck"])
            load(w_ck[DC:DC + 1, :], a["L0_xattn_bck"].unsqueeze(0))
            load(w_cv[0:DC, :], a["L0_xattn_Wcv"])
            load(w_cv[DC:DC + 1, :], a["L0_xattn_bcv"].unsqueeze(0))
            load(w_q[:, :], a["L0_xattn_Wq"])
            load(w_cq[:, :], a["L0_xattn_Wcq"])
            load(w_k[:, :], a["L0_xattn_Wk"])
            for c, name in ((B_Q, "bq"), (B_CQ, "bcq"), (B_K, "bk")):
                load(b_rows[c:c + 1, :], a["L0_xattn_" + name].unsqueeze(0))
            load(w_v[:, :], a["L0_xattn_Wv"])
            load(b_v[:, :], a["L0_xattn_bv"].partition_broadcast(P))
            load(gates[:, 0:2], a["g_xattn"].partition_broadcast(P))
            load(gates[:, 2:4], a["g_ffn"].partition_broadcast(P))
            assert count[0] == N_IN_W, count[0]
            act.wait_ge(in_w, 16 * N_IN_W)
            act.activation(tanh_g[:, :], gates[:, :], ACT.Tanh).then_inc(tanh_in, 1)

            for j, (kind, i, engine) in enumerate(jobs):
                if engine != "act":
                    continue
                act.wait_ge(job_done, j + 1)
                if kind in ("q", "k", "ck") and i >= 2:
                    act.wait_ge(high_in, i - 1)
                src, dst = bank(j % 8), qk[:, i % 2, :]
                if kind == "ct":
                    act.activation(c_t[0:DC, i * BANK:(i + 1) * BANK], src[0:DC, :], ACT.Copy).then_inc(job_act, 1)
                elif kind == "bias":
                    act.activation(b_col[:, :], src[:, 0:4], ACT.Copy).then_inc(job_act, 1)
                elif kind == "q":
                    act.wait_ge(job_act, taken_count(job_at("bias", 0)))
                    act.activation(dst[:, 0:S], src[:, 0:S], ACT.Identity, bias=b_col[:, B_Q:B_Q + 1])
                    act.activation(dst[:, S:QW], src[:, S:QW], ACT.Identity,
                                   bias=b_col[:, B_CQ:B_CQ + 1]).then_inc(job_act, 1)
                elif kind == "k":
                    act.activation(dst[:, QW:QW + S], src[:, 0:S], ACT.Identity,
                                   bias=b_col[:, B_K:B_K + 1]).then_inc(job_act, 1)
                else:
                    act.activation(dst[:, QW + S:XW], src[:, :], ACT.Copy).then_inc(job_act, 1)

            def take_values(n):
                act.wait_ge(pv_done, n + 1)
                if n >= 1:
                    act.wait_ge(o_full, n)
                act.activation(ot_sb[:, :], bank(O_BANK), ACT.Copy).then_inc(ot_in, 1)

            act.wait_ge(parts_in, B)
            for u in range(3 * NHEAD):
                head, w = u // 3, (S + P if u % 3 == 0 else BANK)
                if u == 2 * (2 * XW // BANK):
                    for n in range(B):
                        wait_laid(act, n)
                act.wait_ge(s2_full, u + 1)
                if u >= NPT and u % (3 * QUAD) == 0:
                    act.wait_ge(pv_done, u // (3 * QUAD) - 1)
                act.activation(p_slots[u % NPT][:, 0:w], bank(4 + u % 2)[:, 0:w], ACT.Exp,
                               scale=SCALE).then_inc(p_in, 1)
                if u % (3 * QUAD) == TAKE_AT and u > 2 * 3 * QUAD:
                    take_values(u // (3 * QUAD) - 2)
            take_values(NHEAD // QUAD - 2)
            take_values(NHEAD // QUAD - 1)

            act.wait_ge(yt_full, 1)
            act.activation(y_t[:, 0:BANK], bank(0), ACT.Copy).then_inc(yt_act, 1)

            def take_ht(i):
                act.wait_ge(ht_full[i], 1)
                act.activation(h_t[:, 0:BANK], bank(0), ACT.Copy).then_inc(ht_act[i], 1)

            def experts(layer):
                units, _, trans_after, nj = ORDER[layer]
                take_ht(1 + 2 * layer)
                act.wait_ge(gap_in[layer], 1)
                act.activation(e_gap[:, :], gap[:, :], ACT.Exp).then_inc(e_gap_in[layer], 1)

                def take_weights(e, j):
                    k = nj * e + j
                    act.wait_ge(tr_full[layer], k + 1)
                    if e >= 2:
                        act.wait_ge(dn_full[layer], NHT * (e - 1))
                    w = tr_jobs(layer)[j]
                    if layer == 0:
                        dst = w_t[:, e % 2, w[0][0], :]
                        act.activation(dst, bank(k % 2), ACT.Copy).then_inc(wt_in[layer], 1)
                    else:
                        dst = w_t[:, e % 2, :, 0:P]
                        src = bank(k % 2)[:, 0:3 * P].rearrange("p (m f) -> p m f", m=3)
                        act.activation(dst, src, ACT.Copy).then_inc(wt_in[layer], 1)

                for j in range(nj):
                    take_weights(0, j)
                for i in range(len(units)):
                    act.wait_ge(gu_full[layer], i + 1)
                    if i >= 2:
                        act.wait_ge(hh_in[layer], i - 1)
                    act.activation(sg[:, i % 2, :], bank(2 + 2 * (i % 2)), ACT.Silu).then_inc(sg_in[layer], 1)
                    for e, j in trans_after.get(i, ()):
                        take_weights(e, j)

            experts(0)

            for j in range(2 * B):
                act.wait_ge(kv1_full, j + 1)
                src = bank(KV1_BANK[j])
                if j < B:
                    act.activation(k1_t[:, j * BANK:(j + 1) * BANK], src, ACT.Copy).then_inc(kv1_act, 1)
                else:
                    dst = v1[:, CT * (j - B):CT * (j - B + 1), :]
                    act.activation(dst, src.rearrange("p (t d) -> p t d", t=CT), ACT.Copy).then_inc(kv1_act, 1)
            take_ht(2)
            for s in range(NHT):
                act.wait_ge(q1_full, s + 1)
                act.activation(q1_t[:, s * BANK:(s + 1) * BANK], bank(4 + s), ACT.Identity,
                               bias=b_col[:, B_Q1:B_Q1 + 1]).then_inc(q1_act, 1)
            for t in range(NT):
                act.wait_ge(nm1_in, t + 1)
                if t >= 2:
                    act.wait_ge(p1t_full, t - 1)
                act.activation(p1[:, t % 2, :], bank(t % 2), ACT.Exp, bias=s1_nmax[:, t:t + 1],
                               accum_out=s1_sum[:, t:t + 1]).then_inc(p1_in, 1)
            experts(1)

        @block.vector
        def _(dve):
            link = linker(dve, dve_step)

            def norm(i, x, ready, counts):
                for t in range(NT):
                    if t in counts:
                        dve.wait_ge(ready, counts[t])
                    ins = dve.bn_stats(ln_stats[:, t, :], x[:, t, :])
                link(ins)
                for t in range(NT):
                    dve.bn_aggr(ln_mv[:, t, :], ln_stats[:, t, :]).then_inc(stats_in[i], 1)
                dve.wait_ge(rstd_in[i], 1)
                for t in range(NT):
                    dve.tensor_scalar(h_sb[:, t, :], x[:, t, :], ln_mv[:, t, 0:1], ln_rstd[:, t:t + 1],
                                      ALU.subtract, ALU.mult).then_inc(h_in[i], 1)

            norm(0, x_sb, in_x, {0: 16})

            for j, (kind, i, engine) in enumerate(jobs):
                if engine == "dve":
                    dve.wait_ge(job_done, j + 1)
                    src = bank(j % 8)
                    if kind == "xt":
                        dve.tensor_copy(h_t[:, i * BANK:(i + 1) * BANK], src).then_inc(job_dve, 1)
                    elif kind == "v":
                        if i == 0:
                            dve.wait_ge(in_w, 16 * N_IN_W)
                        dve.tensor_tensor(v_aug[:, QT * i:QT * (i + 1), :, 0:HD],
                                          src[:, 0:QT * D].rearrange("p (t h d) -> p t h d", t=QT, h=H),
                                          b_v[:, :].rearrange("p (h d) -> p h d", h=H).unsqueeze(1)
                                          .to_broadcast([P, QT, H, HD]), ALU.add).then_inc(job_dve, 1)
                    elif kind == "cv":
                        dve.tensor_copy(v_aug[:, NT + CT * i:NT + CT * (i + 1), :, 0:HD],
                                        src.rearrange("p (t h d) -> p t h d", t=CT, h=H)).then_inc(job_dve, 1)
                    else:
                        dve.tensor_copy(gw_t[:, :, :], src[:, 0:2 * E].rearrange("p (l e) -> p l e", l=2))\
                           .then_inc(job_dve, 1)
                if kind == "v":
                    dve.wait_ge(job_act, taken_count(job_at("k", i)))
                    if i >= 2:
                        dve.wait_ge(parts_in, i - 1)
                    link(dve.tensor_copy(parts[:, 0, i, :], qk[:, i % 2, :]))
                    dve.tensor_tensor(qk_r[:, i % 2, :], qk[:, i % 2, :], parts[:, 0, i, :],
                                      ALU.subtract).then_inc(high_in, 1)

            def split_max(b):
                dve.wait_ge(s1_free, split_after[b] + 1)
                whole = nmax[:, b % 2].rearrange("p t k (r q) -> p t (k r) q", q=PAIR)
                part = [nmax_p[:, b % 2, :, :, i, :] for i in range(3)]
                link(dve.tensor_copy(part[0], whole))
                link(dve.tensor_tensor(nmax_r[:, :, :, :], whole, part[0], ALU.subtract))
                link(dve.tensor_copy(part[1], nmax_r[:, :, :, :]))
                dve.tensor_tensor(part[2], nmax_r[:, :, :, :], part[1], ALU.subtract).then_inc(split_in, 1)

            def take_sums(n):
                dve.wait_ge(o_full, n + 1)
                if n >= 2:
                    dve.wait_ge(y_in, n - 1)
                dve.tensor_copy(o_sb[:, n % 2], bank(OT_BANK).rearrange("p (k h c) -> p k h c", k=2 * QT, h=QUAD)
                                [:, :, :, 0:HA]).then_inc(o_taken, 1)
                dve.wait_ge(o_taken, n + 1)
                dve.reciprocal(o_rec[:, n % 2].rearrange("p k h -> p (k h)"),
                               o_sb[:, n % 2].rearrange("p k h d -> p (k h) d")[:, :, HD]).then_inc(rec_in, 1)

            dve.wait_ge(job_done, len(jobs))
            for j in range(len(jobs) - 8, len(jobs)):
                wait_taken(dve, j)
            dve.memset(bank(O_BANK), 0.0).then_inc(o_clear, 1)

            sums_after = {}
            for n in range(NHEAD // QUAD):
                at = min(pass1_before(QUAD * (n + 2) + 1) + 1, len(pass1) - 1)
                sums_after.setdefault(at, []).append(n)
            for i, u in enumerate(pass1):
                dve.wait_ge(s1_full, i + 1)
                src = bank(2 * (i % 2), 2)
                if u[0] == "turn":
                    if u[1] >= 2:
                        dve.wait_ge(mrow_in[u[1] - 2], 16 * 2 * PAR)
                    dve.tensor_copy(nmax_t[:, u[1] % 2, :],
                                    src[0:2 * PAR * 3 * PAIR, 0:S // 2].bitcast(BF16)).then_inc(s1_free, 1)
                else:
                    kind, b, t, g = u
                    n = {"cross": 1, "late": 2, "early": 4}[kind]
                    dst = nmax[:, b % 2, t, int(kind == "cross"), :].rearrange("p (r q) -> p r q", r=PAR)
                    dve.tensor_reduce(dst[:, :, n * g:n * (g + 1)],
                                      src.rearrange("p (r q k) -> p r q k", r=PAR, q=n),
                                      AX.X, ALU.max, negate=True).then_inc(s1_free, 1)
                    if i == split_after[b]:
                        split_max(b)
                for n in sums_after.get(i, ()):
                    take_sums(n)

            dve.wait_ge(yt_full, 2)
            dve.tensor_copy(y_t[:, BANK:TOK], bank(1)).then_inc(yt_dve, 1)
            dve.wait_ge(xb_in, 1)
            for s in range(NHT):
                half = x1_sb[:, s * TPH:(s + 1) * TPH, :].rearrange("p t d -> p (t d)")
                dve.wait_ge(proj_full, s + 1)
                dve.scalar_tensor_tensor(out=half, in0=bank(2 + s), scalar=tanh_g[:, 0:1], in1=half,
                                         op0=ALU.mult, op1=ALU.add).then_inc(x1_in, 1)

            def take_ht(i):
                dve.wait_ge(ht_full[i], 2)
                dve.tensor_copy(h_t[:, BANK:TOK], bank(1)).then_inc(ht_dve[i], 1)

            def choose(layer):
                dve.wait_ge(lg_full[layer], 1)
                src = bank(6)[:, 0:NT * E].rearrange("p (t e) -> p t e", t=NT)
                if layer == 0:
                    link(dve.tensor_copy(lg[:, :, :], src))
                else:
                    link(dve.tensor_tensor(lg[:, :, :], src, b_g[:, :].unsqueeze(1).to_broadcast([P, NT, E]), ALU.add))
                for t in range(NT):
                    ins = dve.max(top[:, t, :], lg[:, t, :])
                link(ins)
                dve.tensor_tensor(gap[:, :], top[:, :, 1], top[:, :, 0], ALU.subtract).then_inc(gap_in[layer], 1)
                for t in range(NT):
                    ins = dve.max_index(top_i[:, t, :], top[:, t, :], lg[:, t, :])
                link(ins)
                link(dve.tensor_copy(top_f[:, :, :], top_i[:, :, 0:2].rearrange("p t k -> p k t")))
                link(dve.tensor_tensor(pick[:, :, :, :].rearrange("p k t e -> p (k t) e"),
                                       iota_e[:, :].unsqueeze(1).to_broadcast([P, 2 * NT, E]),
                                       top_f[:, :, :].rearrange("p k t -> p (k t)").unsqueeze(2)
                                       .to_broadcast([P, 2 * NT, E]), ALU.is_equal))
                if layer == 0:
                    dve.tensor_copy(pick_b[:, :, :, :], pick[:, :, :, :]).then_inc(pick_in, 1)
                dve.wait_ge(e_gap_in[layer], 1)
                link(dve.tensor_scalar(w_top[:, 1, :], e_gap[:, :], 1.0, None, ALU.add))
                link(dve.reciprocal(w_top[:, 0, :], w_top[:, 1, :]))
                link(dve.tensor_tensor(w_top[:, 1, :], w_top[:, 0, :], e_gap[:, :], ALU.mult))
                link(dve.tensor_tensor(pick[:, :, :, :].rearrange("p k t e -> p (k t) e"),
                                       pick[:, :, :, :].rearrange("p k t e -> p (k t) e"),
                                       w_top[:, :, :].rearrange("p k t -> p (k t)").unsqueeze(2)
                                       .to_broadcast([P, 2 * NT, E]), ALU.mult))

            def combine(layer):
                if layer == 0:
                    dve.wait_ge(count_full, 1)
                    flat = "p k t e -> p (k t e)"
                    link(dve.tensor_scalar(fits[:, :, :, :].rearrange(flat), bank(7)[:, 0:2 * NT * E],
                                           float(CAPACITY) + 0.5, None, ALU.is_le))
                    link(dve.tensor_tensor(pick[:, :, :, :].rearrange(flat), pick[:, :, :, :].rearrange(flat),
                                           fits[:, :, :, :].rearrange(flat), ALU.mult))
                link(dve.tensor_tensor(comb[:, :, :], pick[:, 0, :, :], pick[:, 1, :, :], ALU.add))

            def experts(layer, x, x_out, x_out_in):
                units, down_after, _, _ = ORDER[layer]
                nf = nf_of(layer)
                choose(layer)

                def take_down(n):
                    e, s = n // NHT, n % NHT
                    dve.wait_ge(dn_full[layer], n + 1)
                    if e > 0:
                        dve.wait_ge(dn_taken[layer], n - 1)
                    for t in range(TPH):
                        src, dst = bank(6 + n % 2)[:, t * P:(t + 1) * P], acc[:, s * TPH + t, :]
                        weight = comb[:, s * TPH + t, e:e + 1]
                        if e == 0:
                            ins = dve.tensor_scalar(dst, src, weight, None, ALU.mult)
                        else:
                            ins = dve.scalar_tensor_tensor(out=dst, in0=src, scalar=weight, in1=dst,
                                                           op0=ALU.mult, op1=ALU.add)
                    ins.then_inc(dn_taken[layer], 1)

                for i, (e, s, f) in enumerate(units):
                    n = NHT * e + s
                    dve.wait_ge(sg_in[layer], i + 1)
                    if f == 0 and n >= 2:
                        dve.wait_ge(dn_full[layer], n - 1)
                    dve.tensor_tensor(hh[:, n % 2, f, :], bank(3 + 2 * (i % 2)), sg[:, i % 2, :],
                                      ALU.mult).then_inc(hh_in[layer], 1)
                    if i == COUNT_AFTER:
                        combine(layer)
                    for m in down_after.get(i, ()):
                        take_down(m)
                for s in range(NHT):
                    flat = "p t d -> p (t d)"
                    dve.wait_ge(dn_taken[layer], NHT * (E - 1) + s + 1)
                    half = slice(s * TPH, (s + 1) * TPH)
                    dve.scalar_tensor_tensor(out=x_out[:, half, :].rearrange(flat), in0=acc[:, half, :].rearrange(flat),
                                             scalar=tanh_g[:, 2 + layer:3 + layer], in1=x[:, half, :].rearrange(flat),
                                             op0=ALU.mult, op1=ALU.add).then_inc(x_out_in, 1)

            norm(1, x1_sb, x1_in, {0: 1, TPH: 2})
            take_ht(1)
            experts(0, x1_sb, x_sb, x2_in)

            norm(2, x_sb, x2_in, {0: 1, TPH: 2})
            take_ht(2)

            def max1(t):
                dve.wait_ge(sc1_full, t + 1)
                dve.tensor_reduce(s1_nmax[:, t:t + 1], bank(t % 2), AX.X, ALU.max, negate=True).then_inc(nm1_in, 1)

            max1(0)
            for t in range(NT):
                if t + 1 < NT:
                    max1(t + 1)
                dve.wait_ge(p1t_full, t + 1)
                if t >= 2:
                    dve.wait_ge(o1_full, t - 1)
                dve.tensor_copy(p1_t[:, t % 2, :], bank(2 + t % 2)).then_inc(p1t_in, 1)
                link(dve.reciprocal(s1_rec[:, t:t + 1], s1_sum[:, t:t + 1]))
                link(dve.tensor_tensor(s1_rec[:, t:t + 1], s1_rec[:, t:t + 1], tanh_g[:, 1:2], ALU.mult))
                dve.wait_ge(o1_full, t + 1)
                dve.scalar_tensor_tensor(out=x1_sb[:, t, :], in0=bank(4 + t % 2)[:, 0:D], scalar=s1_rec[:, t:t + 1],
                                         in1=x_sb[:, t, :], op0=ALU.mult, op1=ALU.add).then_inc(x3_in, 1)

            norm(3, x1_sb, x3_in, {t: t + 1 for t in range(NT)})
            take_ht(3)
            experts(1, x1_sb, x_sb, x4_in)

        @block.tensor
        def _(pe):
            pe.wait_ge(consts, 4)
            for j, (kind, i, engine) in enumerate(jobs):
                if j >= 8:
                    wait_taken(pe, j - 8)
                dst = bank(j % 8)
                if kind == "xt":
                    for t in range(4 * i, 4 * i + 4):
                        pe.wait_ge(h_in[0], t + 1)
                        ins = pe.transpose(dst[:, (t % 4) * P:(t % 4 + 1) * P], h_sb[:, t, :], ident[:, :])
                elif kind == "ct":
                    pe.wait_ge(in_ctx, 16)
                    for t in range(4 * i, 4 * i + 4):
                        ins = pe.transpose(dst[0:DC, (t % 4) * P:(t % 4 + 1) * P], c_sb[:, t, :], ident[:, :])
                elif kind == "bias":
                    pe.wait_ge(in_w, 16 * N_IN_W)
                    pe.wait_ge(in_late, 16 * N_IN_LATE)
                    pe.wait_ge(perm_in, 5)
                    pe.transpose(dst[:, 0:3], b_perm[:, :], ident[0:3, 0:3])
                    ins = pe.transpose(dst[:, 3:4], b1_row[:, :], ident[0:1, 0:1])
                elif kind == "q":
                    if i == 0:
                        for k in range(NT // 4):
                            wait_taken(pe, job_at("xt", k))
                    for c in range(2):
                        ins = pe.matmul(dst[:, c * S:(c + 1) * S], w_perm[:, c, :],
                                        h_t[:, i * S:(i + 1) * S], start=True, stop=True)
                elif kind == "k":
                    ins = pe.matmul(dst[:, 0:S], w_perm[:, 2, :],
                                    h_t[:, i * S:(i + 1) * S], start=True, stop=True)
                elif kind == "ck":
                    if i == 0:
                        for k in range(NC // 4):
                            wait_taken(pe, job_at("ct", k))
                    ins = pe.matmul(dst, w_perm[0:DC + 1, 3, :],
                                    c_t[:, i * SC:(i + 1) * SC], start=True, stop=True)
                elif kind == "v":
                    for t in range(QT):
                        tok = (QT * i + t) * P
                        ins = pe.matmul(dst[:, t * P:(t + 1) * P], h_t[:, tok:tok + P], w_v[:, :],
                                        start=True, stop=True)
                elif kind == "cv":
                    for t in range(CT):
                        tok = (CT * i + t) * P
                        ins = pe.matmul(dst[:, t * P:(t + 1) * P], c_t[:, tok:tok + P], w_cv[:, :],
                                        start=True, stop=True)
                else:
                    for layer in range(2):
                        ins = pe.transpose(dst[:, layer * E:(layer + 1) * E], gw_rows[:, layer, :], ident[0:E, 0:E])
                ins.then_inc(job_done, 1)
            for j in range(len(jobs) - 8, len(jobs)):
                wait_taken(pe, j)

            def masked_scores(dst, q, k, width):
                pe.matmul(dst, q, k, start=True, stop=False, skip_group_check=True)
                return pe.matmul(dst[:, width - P:width], ident_b[:, :], mask_b[:, :], start=False, stop=True,
                                 skip_group_check=True)

            def pass1_unit(i):
                u = pass1[i]
                if i >= 2:
                    pe.wait_ge(s1_free, i - 1)
                first = 2 * (i % 2)
                if u[0] == "turn":
                    pe.wait_ge(split_in, u[1] + 1)
                    for t in range(QT):
                        dst = bank(first)[0:2 * PAR * 3 * PAIR, t * P // 2:(t + 1) * P // 2].bitcast(BF16)
                        src = nmax_p[:, u[1] % 2, t].rearrange("p k c q -> p (k c q)")
                        ins = pe.transpose(dst, src, ident_b[:, :])
                    ins.then_inc(s1_full, 1)
                    return
                kind, b, t, g = u
                if kind == "cross" and t == 0 and g == 0:
                    wait_laid(pe, b)
                for par in range(PAR):
                    rows = slice(64 * par, 64 * par + ROWS)
                    dst = bank(first + par)
                    if kind == "cross":
                        ins = pe.matmul(dst, qcat[rows, g, b, S + t * P:S + (t + 1) * P], kcat[rows, g, b, S:KW],
                                        start=True, stop=True)
                    elif kind == "late":
                        for n in range(2):
                            ins = masked_scores(dst[:, n * S:(n + 1) * S], qcat[rows, 2 * g + n, b, P:S],
                                                kcat[rows, 2 * g + n, b, 0:S], S)
                    else:
                        for n in range(4):
                            ins = masked_scores(dst[:, n * P:(n + 1) * P], qcat[rows, 4 * g + n, b, 0:P],
                                                kcat[rows, 4 * g + n, b, 0:P], P)
                ins.then_inc(s1_full, 1)

            def scores2(head, part):
                b, h = head // H, head % H
                rows = slice(64 * (h % 2), 64 * (h % 2) + ROWS_M)
                u = 3 * head + part
                if u >= 2:
                    pe.wait_ge(p_in, u - 1)
                if head % H == 0 and part == 0:
                    pe.wait_ge(mrow_in[b], 16 * 2 * PAR)
                dst, q, k = bank(4 + u % 2), qcat[rows, h // 2, b, :], kcat[rows, h // 2, b, :]
                if part == 0:
                    pe.matmul(dst[:, 0:S], k[:, 0:P], q[:, 0:S], start=True, stop=True)
                    ins = pe.matmul(dst[:, S:S + P], k[:, P:S], q[:, P:S], start=True, stop=True)
                else:
                    for c in range(2):
                        key = S + (2 * (part - 1) + c) * P
                        ins = pe.matmul(dst[:, c * S:(c + 1) * S], k[:, key:key + P], q[:, S:QW],
                                        start=True, stop=True)
                ins.then_inc(s2_full, 1)

            def values(n, r):
                if r == 0:
                    if n >= 1:
                        pe.wait_ge(ot_in, n)
                    pe.wait_ge(masked, QUAD * (n + 1))
                if r == 2:
                    pe.wait_ge(p_in, 3 * QUAD * (n + 1))
                for j in range(QUAD):
                    head = QUAD * n + j
                    b, h = head // H, head % H
                    if r < 2:
                        p = p_slots[(3 * head) % NPT][:, (0 if r == 0 else S):(S if r == 0 else S + P)]
                        cols, v = slice(r * P, S), QT * b + r
                    else:
                        c = r - 2
                        p = p_slots[(3 * head + 1 + c // 2) % NPT][:, (c % 2) * S:(c % 2 + 1) * S]
                        cols, v = slice(S, 2 * S), NT + CT * b + c
                    ins = pe.matmul(bank(O_BANK)[32 * j:32 * j + HA, cols], v_aug[:, v, h, :], p,
                                    start=r in (0, 2), stop=r in (1, ROUNDS - 1), skip_group_check=True)
                if r == ROUNDS - 1:
                    ins.then_inc(pv_done, 1)

            def turn_values(n):
                pe.wait_ge(ot_in, n + 1)
                if n >= 1:
                    pe.wait_ge(o_taken, n)
                for k in range(2 * QT):
                    ins = pe.transpose(bank(OT_BANK)[:, k * P:(k + 1) * P], ot_sb[:, k * P:(k + 1) * P], ident[:, :])
                ins.then_inc(o_full, 1)

            ROUNDS = 2 + CT
            NG = NHEAD // QUAD
            pe.wait_ge(ones_in, 16 * PAR)
            pe.wait_ge(consts, N_CONSTS)
            pe.wait_ge(o_clear, 1)
            done = 0
            for u in range(3 * QUAD * (NG + 1)):
                n, k = u // (3 * QUAD), u % (3 * QUAD)
                if u % 3 == 0:
                    while done < pass1_before(u // 3):
                        pass1_unit(done)
                        done += 1
                if n < NG:
                    scores2(u // 3, u % 3)
                if n >= 2 and k == 3:
                    turn_values(n - 2)
                if n >= 1 and k % 2 == 1:
                    values(n - 1, k // 2)
            turn_values(NG - 1)

            pe.wait_ge(s1_free, len(pass1))
            for s in range(NHT):
                for t in range(TPH):
                    pe.wait_ge(y_in, H // QUAD * ((s * TPH + t) // QT + 1))
                    ins = pe.transpose(bank(s)[:, t * P:(t + 1) * P], y_sb[:, s * TPH + t, :], ident[:, :])
                ins.then_inc(yt_full, 1)
            for s in range(NHT):
                pe.wait_ge([yt_act, yt_dve][s], 1)
                for t in range(TPH):
                    tok = (s * TPH + t) * P
                    ins = pe.matmul(bank(2 + s)[:, t * P:(t + 1) * P], y_t[:, tok:tok + P], w_p[:, :],
                                    start=True, stop=True)
                ins.then_inc(proj_full, 1)

            def transpose_h(i):
                for s in range(NHT):
                    for t in range(TPH):
                        pe.wait_ge(h_in[i], s * TPH + t + 1)
                        ins = pe.transpose(bank(s)[:, t * P:(t + 1) * P], h_sb[:, s * TPH + t, :], ident[:, :])
                    ins.then_inc(ht_full[i], 1)
                pe.wait_ge(ht_act[i], 1)
                pe.wait_ge(ht_dve[i], 1)

            def experts(layer):
                units, down_after, trans_after, nj = ORDER[layer]
                nf = nf_of(layer)
                transpose_h(1 + 2 * layer)
                for t in range(NT):
                    ins = pe.matmul(bank(6)[:, t * E:(t + 1) * E], h_t[:, t * P:(t + 1) * P], gw_t[:, layer, :],
                                    start=True, stop=True)
                ins.then_inc(lg_full[layer], 1)

                def transpose_weights(e, j):
                    k = nj * e + j
                    if j == 0:
                        pe.wait_ge(raw_in[layer][e % NRAW], 48 * (e // NRAW + 1))
                    if k >= 2:
                        pe.wait_ge(wt_in[layer], k - 1)
                    for c, (m, f) in enumerate(tr_jobs(layer)[j]):
                        ins = pe.transpose(bank(k % 2)[:, c * P:(c + 1) * P], raw[:, e % NRAW, m, f, :], ident[:, :])
                    ins.then_inc(tr_full[layer], 1)

                def go_down(n):
                    e, s = n // NHT, n % NHT
                    pe.wait_ge(wt_in[layer], nj * (e + 1))
                    pe.wait_ge(hh_in[layer], nf * (n + 1))
                    if n >= 2:
                        pe.wait_ge(dn_taken[layer], n - 1)
                    for t in range(TPH):
                        for f in range(nf):
                            ins = pe.matmul(bank(6 + n % 2)[:, t * P:(t + 1) * P], hh[:, n % 2, f, t * P:(t + 1) * P],
                                            w_t[:, e % 2, 2, f * P:(f + 1) * P], start=(f == 0), stop=(f == nf - 1))
                    ins.then_inc(dn_full[layer], 1)

                for j in range(nj):
                    transpose_weights(0, j)
                for i, (e, s, f) in enumerate(units):
                    if s == 0 and f == 0:
                        pe.wait_ge(wt_in[layer], nj * e + (2 if layer == 0 else 1))
                    if i >= 2:
                        pe.wait_ge(hh_in[layer], i - 1)
                    for m in range(2):
                        ins = pe.matmul(bank(2 + 2 * (i % 2) + m), w_t[:, e % 2, m, f * P:(f + 1) * P],
                                        h_t[:, s * BANK:(s + 1) * BANK], start=True, stop=True)
                    ins.then_inc(gu_full[layer], 1)
                    if i == COUNT_AFTER and layer == 0:
                        pe.wait_ge(pick_in, 1)
                        dst = bank(7)[:, 0:2 * NT * E].rearrange("p (k t e) -> p k t e", k=2, t=NT)
                        pe.matmul(dst, upto_b[:, :], pick_b[:, :, :, :], start=True, stop=False, skip_group_check=True)
                        for d in range(1, NT):
                            ins = pe.matmul(dst[:, :, d:NT, :], ones_b[:, 0:P], pick_b[:, :, 0:NT - d, :],
                                            start=False, stop=(d == NT - 1), skip_group_check=True)
                        ins.then_inc(count_full, 1)
                    for n in down_after.get(i, ()):
                        go_down(n)
                    for w in trans_after.get(i, ()):
                        transpose_weights(*w)

            experts(0)

            for j in range(2 * B):
                if KV1_BANK[j] in (6, 7):
                    pe.wait_ge(dn_taken[0], NHT * E)
                if j in (6, 7):
                    pe.wait_ge(kv1_act, j - 5)
                if j == 0:
                    pe.wait_ge(hh_in[0], len(ORDER[0][0]))
                dst = bank(KV1_BANK[j])
                if j < B:
                    ins = pe.matmul(dst, w1_k[:, :], c_t[:, j * SC:(j + 1) * SC], start=True, stop=True)
                else:
                    for c in range(CT):
                        tok = (CT * (j - B) + c) * P
                        ins = pe.matmul(dst[:, c * P:(c + 1) * P], c_t[:, tok:tok + P], w1_v[:, :],
                                        start=True, stop=True)
                ins.then_inc(kv1_full, 1)
            transpose_h(2)
            pe.wait_ge(kv1_act, 2 * B)
            for s in range(NHT):
                pe.matmul(bank(4 + s), w1_q[:, :], h_t[:, s * BANK:(s + 1) * BANK],
                          start=True, stop=True).then_inc(q1_full, 1)
            pe.wait_ge(q1_act, NHT)

            def scores1(t):
                if t >= 2:
                    pe.wait_ge(p1_in, t - 1)
                b = t // QT
                pe.matmul(bank(t % 2), q1_t[:, t * P:(t + 1) * P], k1_t[:, b * SC:(b + 1) * SC],
                          start=True, stop=True).then_inc(sc1_full, 1)

            scores1(0)
            for t in range(NT):
                if t + 1 < NT:
                    scores1(t + 1)
                pe.wait_ge(p1_in, t + 1)
                if t >= 2:
                    pe.wait_ge(p1t_in, t - 1)
                for c in range(CT):
                    ins = pe.transpose(bank(2 + t % 2)[:, c * P:(c + 1) * P], p1[:, t % 2, c * P:(c + 1) * P], ident[:, :])
                ins.then_inc(p1t_full, 1)
                pe.wait_ge(p1t_in, t + 1)
                if t >= 2:
                    pe.wait_ge(x3_in, t - 1)
                for c in range(CT):
                    ins = pe.matmul(bank(4 + t % 2)[:, 0:D], p1_t[:, t % 2, c * P:(c + 1) * P], v1[:, CT * (t // QT) + c, :],
                                    start=(c == 0), stop=(c == CT - 1))
                ins.then_inc(o1_full, 1)
            experts(1)


_INS = ['x', 'ctx_512', 'g_xattn', 'g_ffn', 'L0_xattn_Wk', 'L0_xattn_bk', 'L0_xattn_Wq', 'L0_xattn_bq', 'L0_xattn_Wv',
        'L0_xattn_bv', 'L0_xattn_Wck', 'L0_xattn_bck', 'L0_xattn_Wcq', 'L0_xattn_bcq', 'L0_xattn_Wcv', 'L0_xattn_bcv',
        'L0_xattn_Wp', 'L0_xattn_bp', 'L0_ffn_gate_w', 'L0_ffn_wi_gate', 'L0_ffn_wi_up', 'L0_ffn_wo', 'L1_xattn_Wq',
        'L1_xattn_bq', 'L1_xattn_Wk', 'L1_xattn_bk', 'L1_xattn_Wv', 'L1_xattn_bv', 'L1_ffn_Wg', 'L1_ffn_bg',
        'L1_ffn_w1', 'L1_ffn_w2']


def kernel(**inputs):
    import numpy as _np
    import concourse.bacc as _bacc
    from concourse import mybir as _mybir
    from concourse.bass_utils import run_bass_kernel_spmd as _run

    nc = _bacc.Bacc("TRN2", target_bir_lowering=False, num_devices=1)
    arrays, aps = {}, {}
    for name in _INS:
        arr = _np.ascontiguousarray(inputs[name])
        arrays[f"in_{name}_dram"] = arr
        aps[name] = nc.dram_tensor(f"in_{name}_dram", arr.shape, _mybir.dt.from_np(arr.dtype),
                                   kind="ExternalInput").ap()
    out = nc.dram_tensor("out_0_dram", inputs["x"].shape, _mybir.dt.float32, kind="ExternalOutput").ap()
    flamingo_gated_kernel(nc, aps, out)
    r = _run(nc, [arrays], core_ids=[0])
    return r.results[0]["out_0_dram"]
```

```python
from contextlib import ExitStack

import concourse.bass as bass
from concourse import mybir

F32 = mybir.dt.float32
BF16 = mybir.dt.bfloat16
U32 = mybir.dt.uint32
ALU = mybir.AluOpType
ACT = mybir.ActivationFunctionType
AX = mybir.AxisListType

P = 128
BANK = 512
EPS = 1e-5
CAPACITY_FACTOR = 1.25
NEG = -1.0e30

Q_PART = (0, 0, 0, 1, 1, 2)
K_PART = (0, 1, 2, 0, 1, 0)
B_Q, B_CQ, B_K = range(3)


def flamingo_gated_kernel(nc, a, out):
    B, S, D = a["x"].shape
    SC, DC = a["ctx_512"].shape[1:]
    H = 16
    HD = D // H
    SCALE = float(HD) ** -0.5
    NT = B * S // P
    QT = S // P
    NC = B * SC // P
    CT = SC // P
    TOK = B * S
    E = a["L0_ffn_gate_w"].shape[0]
    NF0 = a["L0_ffn_wi_gate"].shape[1] // P
    NF1 = a["L1_ffn_w1"].shape[1] // 2 // P
    CAPACITY = max(int(TOK / E * CAPACITY_FACTOR), 1)
    assert D == P and QT == 2 and CT == 4 and NF1 == 1 and NF0 == 4 and E == 8 and HD == 8

    PAIR, PAR = H // 2, 2
    ROWS = HD * len(Q_PART)
    ROWS_M = ROWS + 3
    QW = 2 * S
    KW = S + SC
    XW = QW + KW
    HA = HD + 1
    QUAD = 4
    NPT = 2 * 3 * QUAD
    RING = 3

    ctx = ExitStack()
    with ctx:
        def sb(name, shape, dt=F32):
            return ctx.enter_context(nc.sbuf_tensor(name, shape, dt))

        def sem(name):
            return ctx.enter_context(nc.semaphore(name))

        x_sb = sb("x_sb", [P, NT, D])
        w_q = sb("w_q", [P, D])
        w_k = sb("w_k", [P, D])
        w_cq = sb("w_cq", [P, D])
        w_v = sb("w_v", [P, D])
        w_p = sb("w_p", [P, D])
        w_ck = sb("w_ck", [DC + 1, D])
        w_cv = sb("w_cv", [DC + 1, D])
        w1_q = sb("w1_q", [P, D])
        w1_k = sb("w1_k", [DC + 1, D])
        w1_v = sb("w1_v", [DC + 1, D])
        w_perm = sb("w_perm", [P, 4, D])
        b_perm = sb("b_perm", [3, D])
        b_rows = sb("b_rows", [3, D])
        b1_row = sb("b1_row", [1, D])
        b_col = sb("b_col", [P, 3])
        b1_col = sb("b1_col", [P, 1])
        b_v = sb("b_v", [DC + 1, D])
        b_p = sb("b_p", [P, D])
        b_g = sb("b_g", [P, E])
        gates = sb("gates", [P, 4])
        tanh_g = sb("tanh_g", [P, 4])
        gw_rows = sb("gw_rows", [E, 2, D])
        gw_t = sb("gw_t", [P, 2, E])

        ident = sb("ident", [P, P])
        ident_b = sb("ident_b", [P, P], BF16)
        mask_b = sb("mask_b", [P, P], BF16)
        upto_b = sb("upto_b", [P, P], BF16)
        ones_b = sb("ones_b", [P, KW], BF16)
        iota_e = sb("iota_e", [P, E])
        half_neg = sb("half_neg", [P, NT])
        table = sb("table", [P, 1])
        bp_g = sb("bp_g", [P, D])

        ln_stats = sb("ln_stats", [P, NT, 6])
        ln_mv = sb("ln_mv", [P, NT, 2])
        ln_rstd = sb("ln_rstd", [P, NT])
        h_rows = sb("h_rows", [P, NT, D + 1])
        h_sb = h_rows[:, :, 0:D]
        h_t = sb("h_t", [P, TOK])
        c_t = sb("c_t", [DC + 1, NC * P])

        qk = sb("qk", [P, 2, XW])
        qk_r = sb("qk_r", [P, 2, XW])
        parts = sb("parts", [P, B, 3, XW], BF16)
        qcat = sb("qcat", [P, RING, PAR, PAIR, QW], BF16)
        kcat = sb("kcat", [P, RING, PAIR, KW], BF16)
        v_aug = sb("v_aug", [P, NT + NC, H, HA])

        N_P_PARTS = RING * 3 * XW // (2 * BANK)
        N_P_MORE = NPT - 2 * (2 * XW // BANK) - N_P_PARTS
        p_more = sb("p_more", [P, N_P_MORE * BANK])
        p_slots = [x.rearrange("p (s n) -> p s n", n=BANK)[:, i, :]
                   for x, m in ((qk[:, :, :].rearrange("p s n -> p (s n)"), 2 * XW // BANK),
                                (qk_r[:, :, :].rearrange("p s n -> p (s n)"), 2 * XW // BANK),
                                (parts[:, 0:RING].rearrange("p b c n -> p (b c n)")[:, 0:N_P_PARTS * 2 * BANK]
                                 .bitcast(F32), N_P_PARTS),
                                (p_more[:, :], N_P_MORE)) for i in range(m)]
        ot_sb = sb("ot_sb", [P, BANK])
        nmax = sb("nmax", [P, 2, QT, 2, H // 2])
        nmax_r = sb("nmax_r", [P, QT, 2 * PAR, PAIR // 2])
        nmax_p = sb("nmax_p", [P, 2, QT, 2 * PAR, 3, PAIR // 2], BF16)
        nmax_t = sb("nmax_t", [2 * PAR * 3 * PAIR // 2, 2, S], BF16)
        o_sb = sb("o_sb", [P, 2, 2 * QT, QUAD, HA])
        o_rec = sb("o_rec", [P, 2, 2 * QT, QUAD])
        o_n = sb("o_n", [P, 2, 2 * QT, QUAD, HD])
        y_sb, y_t = h_sb, h_t
        x1_sb = sb("x1_sb", [P, NT, D])
        c_sb = x1_sb[:, :, :].rearrange("p t (u d) -> p (t u) d", d=DC)

        lg = sb("lg", [P, NT, E])
        top = sb("top", [P, NT, 8])
        top_i = sb("top_i", [P, NT, 8], U32)
        top_f = sb("top_f", [P, 2, NT])
        gap = sb("gap", [P, NT])
        e_gap = sb("e_gap", [P, NT])
        w_top = sb("w_top", [P, 2, NT])
        pick = sb("pick", [P, 2, NT, E])
        pick_b = sb("pick_b", [P, 2, NT, E], BF16)
        comb = sb("comb", [P, NT, E])
        NRAW = 2

        def q_place(slot, first, n):
            return qcat[:, slot].rearrange("p a b n -> p (a b n)").bitcast(F32)[:, first:first + n]

        def k_place(slot, first, n):
            return kcat[:, slot].rearrange("p b n -> p (b n)").bitcast(F32)[:, first:first + n]

        raw = k_place(1, 0, NRAW * 3 * NF0 * P).rearrange("p (s m n d) -> p s m n d", s=NRAW, m=3, n=NF0)
        w_t = k_place(2, 0, 2 * 3 * NF0 * P).rearrange("p (s m f) -> p s m f", s=2, m=3)
        hh = q_place(0, 0, 2 * NF0 * BANK).rearrange("p (s f k) -> p s f k", s=2, f=NF0)
        MT = -(-2 * CAPACITY // 3)
        SLOTS = 3 * MT
        ZROWS = 64 * -(-E * SLOTS // 64)
        rows_in = nc.dram_tensor("rows_in", [ZROWS, D + 1], F32, kind="Internal").ap()
        rows_back = nc.dram_tensor("rows_back", [2 * TOK, D], F32, kind="Internal").ap()
        slot_base = sb("slot_base", [P, 2, NT])
        cnt = sb("cnt", [P, 2, NT])
        chosen = sb("chosen", [P, 2, NT, E])
        valid = sb("valid", [P, 2, NT])
        slot = sb("slot", [P, 2, NT])
        put_f = sb("put_f", [P, 2, NT])
        put_at = sb("put_at", [P, 2, NT], U32)
        rank_off = sb("rank_off", [P, 3])
        back_f = sb("back_f", [P, E, 3])
        back_at = sb("back_at", [P, E, 3], U32)
        spare = parts[:, :, :, :].rearrange("p b c n -> p (b c n)").bitcast(F32)
        xs = spare[:, 0:E * 3 * (D + 1)].rearrange("p (e t d) -> p e t d", e=E, t=3)
        xs_t = p_more[:, 0:2 * SLOTS].rearrange("p (s k) -> p s k", s=2)
        eo = q_place(1, NC * P + 2 * BANK, 2 * 3 * D).rearrange("p (s t d) -> p s t d", s=2, t=3)
        got = q_place(2, NC * D, 2 * NT * D).rearrange("p (k t d) -> p k t d", k=2, t=NT)
        k1_t = q_place(1, 0, NC * P)
        sg = q_place(1, NC * P, 2 * BANK).rearrange("p (s k) -> p s k", s=2)
        acc = q_place(1, NC * P + 2 * BANK, NT * D).rearrange("p (t d) -> p t d", t=NT)
        v1 = q_place(2, 0, NC * D).rearrange("p (t d) -> p t d", t=NC)

        q1_t = qk[:, :, SC:SC + BANK]
        raw1 = spare[:, E * 3 * (D + 1):E * 3 * (D + 1) + E * 3 * P].rearrange("p (e m d) -> p e m d", e=E, m=3)
        w1_t = k_place(0, 0, E * 3 * P).rearrange("p (e m f) -> p e m f", e=E, m=3)
        p1 = qk[:, :, 0:SC]
        p1_t = qk_r[:, :, 0:SC]
        s1_nmax = sb("s1_nmax", [P, NT])
        s1_sum = sb("s1_sum", [P, NT])
        s1_rec = sb("s1_rec", [P, NT])

        psum = ctx.enter_context(nc.psum_tensor("psum", [P, 8 * BANK], F32))

        def bank(i, n=1):
            return psum[:, i * BANK:(i + n) * BANK]

        in_x = sem("in_x")
        in_ctx = sem("in_ctx")
        in_w = sem("in_w")
        in_late = sem("in_late")
        consts = sem("consts")
        zero_in = [sem(f"zero_in{n}") for n in range(RING)]
        ones_in = [sem(f"ones_in{n}") for n in range(RING)]
        perm_in = sem("perm_in")
        tanh_in = sem("tanh_in")
        stats_in = [sem(f"stats_in{i}") for i in range(4)]
        rstd_in = [sem(f"rstd_in{i}") for i in range(4)]
        h_in = [sem(f"h_in{i}") for i in range(4)]
        job_done = sem("job_done")
        job_act = sem("job_act")
        high_act = sem("high_act")
        rest_in = sem("rest_in")
        mid_in = sem("mid_in")
        parts_in = sem("parts_in")
        cat_in = [sem(f"cat_in{n}") for n in range(B)]
        cat_pool = sem("cat_pool")
        s1_full = sem("s1_full")
        s1_free = sem("s1_free")
        split_in = sem("split_in")
        mrow_in = [sem(f"mrow_in{n}") for n in range(2 * B)]
        s2_full = sem("s2_full")
        p_in = sem("p_in")
        masked = sem("masked")
        pv_done = sem("pv_done")
        ot_in = sem("ot_in")
        o_full = sem("o_full")
        o_clear = sem("o_clear")
        o_taken = sem("o_taken")
        rec_in = sem("rec_in")
        y_in = sem("y_in")
        xb_in = sem("xb_in")
        yt_full = sem("yt_full")
        yt_act = sem("yt_act")
        yt_dve = sem("yt_dve")
        gw_full = sem("gw_full")
        gw_in = sem("gw_in")
        proj_full = sem("proj_full")
        x1_in = sem("x1_in")
        x3_in = sem("x3_in")
        x4_in = sem("x4_in")
        ht_full = [sem(f"ht_full{i}") for i in range(4)]
        ht_act = [sem(f"ht_act{i}") for i in range(4)]
        ht_dve = [sem(f"ht_dve{i}") for i in range(4)]
        lg_full = [sem(f"lg_full{i}") for i in range(2)]
        gap_in = [sem(f"gap_in{i}") for i in range(2)]
        e_gap_in = [sem(f"e_gap_in{i}") for i in range(2)]
        pick_in = sem("pick_in")
        zeroed = sem("zeroed")
        put_in = sem("put_in")
        back_in = sem("back_in")
        put_out = sem("put_out")
        xs_in = [sem(f"xs_in{e}") for e in range(E)]
        xt_full = sem("xt_full")
        xt_in = sem("xt_in")
        eo_out = [sem(f"eo_out{i}") for i in range(2)]
        got_in = [sem(f"got_in{s}") for s in range(2)]
        count_full = sem("count_full")
        raw_in = [sem(f"raw_in{r}") for r in range(NRAW)]
        raw1_in = sem("raw1_in")
        tr_full = [sem(f"tr_full{i}") for i in range(2)]
        wt_in = [sem(f"wt_in{i}") for i in range(2)]
        gu_full = [sem(f"gu_full{i}") for i in range(2)]
        sg_in = [sem(f"sg_in{i}") for i in range(2)]
        hh_in = [sem(f"hh_in{i}") for i in range(2)]
        dn_full = [sem(f"dn_full{i}") for i in range(2)]
        dn_taken = [sem(f"dn_taken{i}") for i in range(2)]
        kv1_full = sem("kv1_full")
        kv1_act = sem("kv1_act")
        q1_full = sem("q1_full")
        q1_act = sem("q1_act")
        sc1_full = sem("sc1_full")
        nm1_in = sem("nm1_in")
        p1_in = sem("p1_in")
        p1t_full = sem("p1t_full")
        p1t_in = sem("p1t_in")
        o1_full = sem("o1_full")
        stored = sem("stored")
        dve_step = sem("dve_step")
        act_step = sem("act_step")
        pool_step = sem("pool_step")

        def linker(eng, s):
            count = [0]

            def link(ins):
                count[0] += 1
                ins.then_inc(s, 1)
                eng.wait_ge(s, count[0])
            return link

        jobs = [("ct", i, "act") for i in range(NC // 4)] + [("bias", 0, "act")]
        jobs += [("ck", 0, "act"), ("xt", 0, "act")]
        for b in range(B):
            jobs += [("q", b, "act"), ("k", b, "act")] + [("ck", b, "act")] * (b > 0)
            jobs += [("v", b, "act"), ("cv", b, "act")] + [("xt", 1, "act")] * (b == 0)

        def job_at(kind, index):
            return [j for j, (k, i, _) in enumerate(jobs) if (k, i) == (kind, index)][0]

        def taken_count(j):
            return sum(e == jobs[j][2] for _, _, e in jobs[:j + 1])

        def wait_taken(eng, j):
            eng.wait_ge(job_act, taken_count(j))

        NPART = 2 * B
        PP = PAIR // 2

        def units_of(part):
            first = PP * (part % 2)
            u = [("cross", part, t, pair) for t in range(QT) for pair in range(first, first + PP)]
            u += [("late", part, 1, g) for g in range(first // 2, (first + PP) // 2)]
            return u + [("early", part, 0, first // 4)]

        TURN_LAG = 2
        N1 = len(units_of(0))
        pass1 = []
        for n in range(NPART):
            u = units_of(n)
            if n:
                u.insert(TURN_LAG, ("turn", n - 1))
            pass1 += u
        pass1.append(("turn", NPART - 1))
        turn_at = {u[1]: i for i, u in enumerate(pass1) if u[0] == "turn"}
        split_after = {b: max(i for i, u in enumerate(pass1) if u[0] != "turn" and u[1] == b)
                       for b in range(NPART)}
        LEAD = N1 + 10

        def pass1_before(u):
            return min(len(pass1), LEAD + -(-u * (N1 + 1) // (3 * H // 2)))

        NHEAD = B * H

        def q_cols(kind):
            return kind * S

        def k_cols(kind):
            return kind * S

        NHT = TOK // BANK
        TPH = BANK // P

        def expert_weights(e):
            return [a["L0_ffn_wi_gate"][e].rearrange("(n f) d -> f n d", f=P),
                    a["L0_ffn_wi_up"][e].rearrange("(n f) d -> f n d", f=P),
                    a["L0_ffn_wo"][e].rearrange("d (n f) -> d n f", f=P)]

        block = ctx.enter_context(nc.Block())

        O_BANK, OT_BANK = 6, 7
        TAKE_AT = 0
        N_ZERO = 5
        FAR = 1.0e6
        N_CONSTS = 13
        DOWN_AFTER = 1
        KV1_BANK = [2, 3, 4, 5] * 2
        N_IN_LATE = 11
        N_IN_W = 14

        UNITS1 = [(s, e) for s in range(NHT) for e in range(E)]
        CHOOSE_AFTER, WEIGH_AFTER = 2, 3
        HALF_AFTER = 1
        DN_BANK = [6, 7, 1, 0]

        def taken_after(i):
            return 0 if i < WEIGH_AFTER else min(i, 2 * (i - WEIGH_AFTER) + 1)
        LG_BANK = [6, 0]

        def lay_out(eng, b, groups, laid):
            for par, r in groups:
                half = slice(64 * par, 64 * par + 64)
                rows = slice(64 * par + HD * r, 64 * par + HD * (r + 1))
                eng.dma_start(qcat[rows, b % RING, par], parts[half, b, Q_PART[r], 0:QW]).then_inc(laid, 16)
                eng.dma_start(kcat[rows, b % RING], parts[half, b, K_PART[r], QW:XW]).then_inc(laid, 16)
            if b >= RING:
                for par in range(PAR):
                    other = slice(64 * (1 - par), 64 * (1 - par) + 3)
                    eng.dma_start(qcat[64 * par + ROWS:64 * par + ROWS_M, b % RING, par],
                                  qcat[other, b % RING, par]).then_inc(laid, 16)

        GROUPS = [(par, r) for par in range(PAR) for r in range(len(Q_PART))]
        SPLIT_DVE = 2
        N_POOL = 4

        def wait_laid(eng, b):
            if b == 0:
                eng.wait_ge(cat_pool, 32 * N_POOL)
            eng.wait_ge(cat_in[b], 32 * (len(GROUPS) - (N_POOL if b == 0 else 0)) + (16 * PAR if b >= RING else 0))

        @block.sync
        def _(sp):
            sp.dma_start(x_sb[:, :, :], a["x"].rearrange("b (t p) d -> p (b t) d", p=P)).then_inc(in_x, 16)
            sp.dma_start(c_sb[:, :, :], a["ctx_512"].rearrange("b (t p) d -> p (b t) d", p=P)).then_inc(in_ctx, 16)

            def lay_out_first(b):
                sp.wait_ge(parts_in, b + 1)
                sp.wait_ge(zero_in[b], 2)
                lay_out(sp, b, GROUPS[:len(GROUPS) - N_POOL] if b == 0 else GROUPS, cat_in[b])

            count = [0]

            def load(dst, src):
                sp.dma_start(dst, src).then_inc(in_late, 16)
                count[0] += 1

            def load_late():
                load(w_p[:, :], a["L0_xattn_Wp"])
                load(b_p[:, :], a["L0_xattn_bp"].partition_broadcast(P))
                load(gw_rows[:, 0, :], a["L0_ffn_gate_w"])
                load(gw_rows[:, 1, :], a["L1_ffn_Wg"])
                load(b_g[:, :], a["L1_ffn_bg"].partition_broadcast(P))
                load(w1_q[:, :], a["L1_xattn_Wq"])
                load(b1_row[:, :], a["L1_xattn_bq"].unsqueeze(0))
                for w, n in ((w1_k, "k"), (w1_v, "v")):
                    load(w[0:DC, :], a["L1_xattn_W" + n])
                    load(w[DC:DC + 1, :], a["L1_xattn_b" + n].unsqueeze(0))
                assert count[0] == N_IN_LATE, count[0]

            lay_out_first(0)
            lay_out_first(1)
            for n in range(NPART):
                sp.wait_ge(s1_free, turn_at[n] + 1)
                for kind in range(2):
                    for par in range(PAR):
                        r = 3 * PP * (PAR * kind + par)
                        dst = qcat[64 * par + ROWS:64 * par + ROWS_M, n // 2 % RING, par]
                        sp.dma_start(dst[:, PP * (n % 2):PP * (n % 2 + 1), kind * S:kind * S + S],
                                     nmax_t[r:r + 3 * PP, n % 2, :]).then_inc(mrow_in[n], 16)
                if n == 0:
                    lay_out_first(2)
                if n == 1:
                    load_late()
                    zeros = qcat[64:P, 0, 0].rearrange("p b n -> p (b n)").bitcast(F32)
                    most = zeros.shape[1]
                    for rows in (rows_in, rows_back):
                        whole = rows.rearrange("r d -> (r d)")
                        n_each = rows.shape[0] * rows.shape[1] // 64
                        for first in range(0, n_each, most):
                            m = min(most, n_each - first)
                            sp.dma_start(whole[64 * first:64 * (first + m)].rearrange("(p m) -> p m", p=64),
                                         zeros[:, 0:m]).then_inc(zeroed, 16)
                if n == 2:
                    sp.wait_ge(s2_full, 3 * H)
                    sp.wait_ge(parts_in, B)
                    lay_out(sp, B - 1, GROUPS, cat_in[B - 1])
                if n == 4:
                    sp.wait_ge(s2_full, 3 * H * 2)
                    for e in range(NRAW):
                        for m, w in enumerate(expert_weights(e)):
                            sp.dma_start(raw[:, e, m, :, :], w).then_inc(raw_in[e], 16)
            sp.wait_ge(put_out, 16 * 2 * NT)
            for e in range(E):
                sp.dma_start(xs[0:MT, e], rows_in[e * SLOTS:(e + 1) * SLOTS, :].rearrange("(p t) d -> p t d", t=3))\
                    .then_inc(xs_in[e], 16)
            w1 = a["L1_ffn_w1"].rearrange("e (m p) d -> m p e d", m=2)
            for m in range(2):
                sp.dma_start(raw1[:, :, m, :], w1[m]).then_inc(raw1_in, 16)
            sp.dma_start(raw1[:, :, 2, :], a["L1_ffn_w2"].rearrange("e d f -> d e f")).then_inc(raw1_in, 16)
            for e in range(E):
                if e + NRAW < E:
                    sp.wait_ge(tr_full[0], 3 * (e + 1))
                    for m, w in enumerate(expert_weights(e + NRAW)):
                        sp.dma_start(raw[:, e % NRAW, m, :, :], w).then_inc(raw_in[e % NRAW], 16)
                if e == E - 1:
                    for i in range(2):
                        sp.wait_ge(eo_out[i], 16 * 3 * (E // 2))
                    back = rows_back.rearrange("(k t p) d -> k p t d", k=2, p=P)
                    for s in range(NHT):
                        half = slice(s * TPH, (s + 1) * TPH)
                        for k in range(2):
                            sp.dma_start(got[:, k, half, :], back[k, :, half, :]).then_inc(got_in[s], 16)
            out_v = out.rearrange("b (t p) d -> p (b t) d", p=P)
            for s in range(NHT):
                sp.wait_ge(x4_in, s + 1)
                sp.dma_start(out_v[:, s * TPH:(s + 1) * TPH, :], x_sb[:, s * TPH:(s + 1) * TPH, :]).then_inc(stored, 16)
            sp.wait_ge(stored, 16 * NHT)

        @block.gpsimd
        def _(pool):
            link = linker(pool, pool_step)
            made = [0]

            def const(ins):
                made[0] += 1
                ins.then_inc(consts, 1)
                pool.wait_ge(consts, made[0])

            const(pool.memset(ones_b[:, :], 1.0))
            link(pool.memset(ident[:, :], 0.0))
            link(pool.affine_select(out=ident[:, :], in_=ident[:, :], pattern=[[-1, P]], compare_op=ALU.not_equal,
                                    fill=1.0, base=0, channel_multiplier=1))
            const(pool.memset(half_neg[:, :], -0.5))
            const(pool.memset(c_t[DC:DC + 1, :], 1.0))
            const(pool.tensor_copy(ident_b[:, :], ident[:, :]))

            def lay_ones(slot):
                pool.wait_ge(zero_in[slot], 2)
                for par in range(PAR):
                    r = 64 * par + ROWS
                    pool.dma_start(kcat[r:r + 3, slot], ones_b[0:3 * PAIR, :]).then_inc(ones_in[slot], 16)

            pool.memset(kcat[:, 0], 0.0).then_inc(zero_in[0], 1)
            lay_ones(0)

            def rstd(i):
                for s in range(NHT):
                    half = slice(s * TPH, (s + 1) * TPH)
                    pool.wait_ge(stats_in[i], (s + 1) * TPH)
                    link(pool.tensor_scalar(ln_rstd[:, half], ln_mv[:, half, 1], EPS, None, ALU.add))
                    pool.tensor_tensor(ln_rstd[:, half], ln_rstd[:, half], half_neg[:, half],
                                       ALU.pow).then_inc(rstd_in[i], 1)

            rstd(0)
            link(pool.memset(mask_b[:, :], 0.0))
            const(pool.affine_select(out=mask_b[:, :], in_=mask_b[:, :], pattern=[[-1, P]], compare_op=ALU.is_ge,
                                     fill=NEG, base=0, channel_multiplier=1))
            const(pool.affine_select(out=upto_b[:, :], in_=ones_b[:, 0:P], pattern=[[1, P]], compare_op=ALU.is_ge,
                                     fill=0.0, base=0, channel_multiplier=-1))
            const(pool.iota(iota_e[:, :], pattern=[[1, E]], base=0, channel_multiplier=0,
                            allow_small_or_imprecise_dtypes=True))
            const(pool.iota(h_rows[:, :, D], pattern=[[P, NT]], base=1, channel_multiplier=1,
                            allow_small_or_imprecise_dtypes=True))
            const(pool.iota(rank_off[:, :], pattern=[[1, 3]], base=0, channel_multiplier=3,
                            allow_small_or_imprecise_dtypes=True))
            link(pool.tensor_scalar(rank_off[:, :], rank_off[:, :], CAPACITY - 0.5, float(TOK), ALU.is_ge, ALU.mult))
            const(pool.tensor_scalar(rank_off[:, :], rank_off[:, :], -1.0, None, ALU.add))
            for k in range(2):
                const(pool.memset(slot_base[:, k, :], float(k * CAPACITY - 1)))
            const(pool.memset(v_aug[:, :, :, HD:HA], 1.0))

            pool.memset(kcat[:, 1], 0.0).then_inc(zero_in[1], 1)
            pool.wait_ge(parts_in, 1)
            lay_out(pool, 0, GROUPS[len(GROUPS) - N_POOL:], cat_pool)
            pool.memset(qcat[:, 2], 0.0).then_inc(zero_in[2], 1)
            pool.memset(kcat[:, 2], 0.0).then_inc(zero_in[2], 1)
            for slot in range(1, RING):
                lay_ones(slot)
            for b in range(SPLIT_DVE, B):
                pool.wait_ge(high_act, b - SPLIT_DVE + 1)
                pool.wait_ge(rest_in, b)
                pool.wait_ge(parts_in, SPLIT_DVE)
                pool.tensor_tensor(qk_r[:, b % 2, :], qk[:, b % 2, :], parts[:, b, 0, :],
                                   ALU.subtract).then_inc(rest_in, 1)
            for b in range(SPLIT_DVE, B):
                pool.wait_ge(mid_in, b - SPLIT_DVE + 1)
                pool.tensor_tensor(parts[:, b, 2, :], qk_r[:, b % 2, :], parts[:, b, 1, :],
                                   ALU.subtract).then_inc(parts_in, 1)

            def normalise(n):
                pool.wait_ge(rec_in, n + 1)
                link(pool.tensor_tensor(o_n[:, n % 2].rearrange("p k h d -> p (k h) d"),
                                        o_sb[:, n % 2].rearrange("p k h d -> p (k h) d")[:, :, 0:HD],
                                        o_rec[:, n % 2].rearrange("p k h -> p (k h)").unsqueeze(2)
                                        .to_broadcast([P, 2 * QT * QUAD, HD]), ALU.mult))
                b, at = n // (H // QUAD), n % (H // QUAD) * QUAD * HD
                pool.tensor_tensor(y_sb[:, QT * b:QT * (b + 1), at:at + QUAD * HD],
                                   o_n[:, n % 2, 0:QT].rearrange("p t h d -> p t (h d)"),
                                   o_n[:, n % 2, QT:2 * QT].rearrange("p t h d -> p t (h d)"),
                                   ALU.add).then_inc(y_in, 1)

            def add_bias():
                pool.wait_ge(in_late, 16 * N_IN_LATE)
                pool.wait_ge(tanh_in, 1)
                link(pool.tensor_scalar(bp_g[:, :], b_p[:, :], tanh_g[:, 0:1], None, ALU.mult))
                pool.tensor_tensor(x1_sb[:, :, :], x_sb[:, :, :], bp_g[:, :].unsqueeze(1).to_broadcast([P, NT, D]),
                                   ALU.add).then_inc(xb_in, 1)

            for head in range(NHEAD):
                if head == 5 * QUAD:
                    add_bias()
                pool.wait_ge(p_in, 3 * head + 1)
                diag = p_slots[(3 * head) % NPT].rearrange("p (c q) -> p c q", q=P)[:, 0:3:2, :]
                pool.affine_select(out=diag, in_=diag, pattern=[[0, 2], [1, P]], compare_op=ALU.is_ge, fill=0.0,
                                   base=0, channel_multiplier=-1).then_inc(masked, 1)
                if head % QUAD == QUAD - 1 and head >= 3 * QUAD:
                    normalise(head // QUAD - 3)
            normalise(NHEAD // QUAD - 3)
            normalise(NHEAD // QUAD - 2)
            normalise(NHEAD // QUAD - 1)
            rstd(1)
            pool.wait_ge(zeroed, 16 * N_ZERO)
            pool.wait_ge(put_in, 1)
            for t in range(NT):
                for k in range(2):
                    pool.indirect_dma_start(out=rows_in[0:E * SLOTS, :],
                                            out_offset=bass.IndirectOffsetOnAxis(ap=put_at[:, k, t:t + 1], axis=0),
                                            in_=h_rows[:, t, :], in_offset=None, bounds_check=E * SLOTS - 1,
                                            oob_is_err=False).then_inc(put_out, 16)
            pool.wait_ge(back_in, 1)
            for e in range(E):
                pool.wait_ge(dn_taken[0], e + 1)
                for t in range(3):
                    pool.indirect_dma_start(out=rows_back[:, :],
                                            out_offset=bass.IndirectOffsetOnAxis(ap=back_at[0:MT, e, t:t + 1], axis=0),
                                            in_=eo[0:MT, e % 2, t, :], in_offset=None, bounds_check=2 * TOK - 1,
                                            oob_is_err=False).then_inc(eo_out[e % 2], 16)
            rstd(2)
            rstd(3)

        @block.scalar
        def _(act):
            link = linker(act, act_step)
            count = [0]

            def load(dst, src):
                act.dma_start(dst, src).then_inc(in_w, 16)
                count[0] += 1

            load(w_ck[0:DC, :], a["L0_xattn_Wck"])
            load(w_ck[DC:DC + 1, :], a["L0_xattn_bck"].unsqueeze(0))
            load(w_cv[0:DC, :], a["L0_xattn_Wcv"])
            load(w_cv[DC:DC + 1, :], a["L0_xattn_bcv"].unsqueeze(0))
            load(w_q[:, :], a["L0_xattn_Wq"])
            load(w_cq[:, :], a["L0_xattn_Wcq"])
            load(w_k[:, :], a["L0_xattn_Wk"])
            for c, name in ((B_Q, "bq"), (B_CQ, "bcq"), (B_K, "bk")):
                load(b_rows[c:c + 1, :], a["L0_xattn_" + name].unsqueeze(0))
            load(w_v[:, :], a["L0_xattn_Wv"])
            load(b_v[DC:DC + 1, :], a["L0_xattn_bv"].unsqueeze(0))
            load(gates[:, 0:2], a["g_xattn"].partition_broadcast(P))
            load(gates[:, 2:4], a["g_ffn"].partition_broadcast(P))
            assert count[0] == N_IN_W, count[0]
            act.wait_ge(in_w, 16 * N_IN_W)
            act.activation(tanh_g[:, :], gates[:, :], ACT.Tanh).then_inc(tanh_in, 1)

            for j, (kind, i, engine) in enumerate(jobs):
                if engine != "act":
                    continue
                act.wait_ge(job_done, j + 1)
                if kind in ("q", "k", "ck") and i >= 2:
                    act.wait_ge(rest_in, i - 1)
                src, dst = bank(j % 8), qk[:, i % 2, :]
                if kind == "ct":
                    act.activation(c_t[0:DC, i * BANK:(i + 1) * BANK], src[0:DC, :], ACT.Copy).then_inc(job_act, 1)
                elif kind == "xt":
                    act.activation(h_t[:, i * BANK:(i + 1) * BANK], src, ACT.Copy).then_inc(job_act, 1)
                elif kind == "bias":
                    act.activation(b_col[:, :], src[:, 0:3], ACT.Copy).then_inc(job_act, 1)
                elif kind == "q":
                    act.wait_ge(job_act, taken_count(job_at("bias", 0)))
                    act.activation(dst[:, 0:S], src[:, 0:S], ACT.Identity, bias=b_col[:, B_Q:B_Q + 1])
                    act.activation(dst[:, S:QW], src[:, S:QW], ACT.Identity,
                                   bias=b_col[:, B_CQ:B_CQ + 1]).then_inc(job_act, 1)
                elif kind == "k":
                    act.activation(dst[:, QW:QW + S], src[:, 0:S], ACT.Identity,
                                   bias=b_col[:, B_K:B_K + 1]).then_inc(job_act, 1)
                elif kind == "v":
                    act.activation(v_aug[:, QT * i:QT * (i + 1), :, 0:HD],
                                   src[:, 0:QT * D].rearrange("p (t h d) -> p t h d", t=QT, h=H),
                                   ACT.Copy).then_inc(job_act, 1)
                elif kind == "cv":
                    act.activation(v_aug[:, NT + CT * i:NT + CT * (i + 1), :, 0:HD],
                                   src.rearrange("p (t h d) -> p t h d", t=CT, h=H), ACT.Copy).then_inc(job_act, 1)
                else:
                    act.activation(dst[:, QW + S:XW], src[:, :], ACT.Copy).then_inc(job_act, 1)
                    if i >= SPLIT_DVE:
                        act.wait_ge(job_act, taken_count(j))
                        act.activation(parts[:, i, 0, :], dst, ACT.Copy).then_inc(high_act, 1)
            for b in range(SPLIT_DVE, B):
                act.wait_ge(rest_in, b + 1)
                act.activation(parts[:, b, 1, :], qk_r[:, b % 2, :], ACT.Copy).then_inc(mid_in, 1)

            def take_values(n):
                act.wait_ge(pv_done, n + 1)
                if n >= 1:
                    act.wait_ge(o_full, n)
                act.activation(ot_sb[:, :], bank(O_BANK), ACT.Copy).then_inc(ot_in, 1)

            act.wait_ge(parts_in, B)
            parts_under = {}
            for i in range(N_P_PARTS):
                for n in range(i * 2 * BANK // (3 * XW), ((i + 1) * 2 * BANK - 1) // (3 * XW) + 1):
                    if n not in parts_under.values():
                        parts_under[2 * (2 * XW // BANK) + i] = n
            for u in range(3 * NHEAD):
                head, w = u // 3, (S + P if u % 3 == 0 else BANK)
                if u in parts_under:
                    wait_laid(act, parts_under[u])
                act.wait_ge(s2_full, u + 1)
                if u >= NPT and u % (3 * QUAD) == 0:
                    act.wait_ge(pv_done, u // (3 * QUAD) - 1)
                act.activation(p_slots[u % NPT][:, 0:w], bank(4 + u % 2)[:, 0:w], ACT.Exp,
                               scale=SCALE).then_inc(p_in, 1)
                if u % (3 * QUAD) == TAKE_AT and u >= 2 * 3 * QUAD:
                    take_values(u // (3 * QUAD) - 2)
            take_values(NHEAD // QUAD - 2)
            take_values(NHEAD // QUAD - 1)

            act.wait_ge(yt_full, 1)
            act.activation(y_t[:, 0:BANK], bank(0), ACT.Copy).then_inc(yt_act, 1)

            def take_ht(i):
                act.wait_ge(ht_full[i], 1)
                act.activation(h_t[:, 0:BANK], bank(0), ACT.Copy).then_inc(ht_act[i], 1)

            def weigh(layer):
                act.wait_ge(gap_in[layer], 1)
                act.activation(e_gap[:, :], gap[:, :], ACT.Exp).then_inc(e_gap_in[layer], 1)

            def take_weights(e, j):
                k = 3 * e + j
                act.wait_ge(tr_full[0], k + 1)
                if e >= 2:
                    act.wait_ge(dn_full[0], e - 1)
                act.activation(w_t[:, e % 2, j, :], bank(k % 2), ACT.Copy).then_inc(wt_in[0], 1)

            def routed_experts():
                def take_down(e):
                    act.wait_ge(dn_full[0], e + 1)
                    if e >= 2:
                        act.wait_ge(eo_out[e % 2], 48 * (e // 2))
                    act.activation(eo[0:MT, e % 2], bank(6)[0:MT, 0:3 * D].rearrange("p (t d) -> p t d", t=3),
                                   ACT.Copy).then_inc(dn_taken[0], 1)

                for e in range(E):
                    for f in range(NF0):
                        i = NF0 * e + f
                        act.wait_ge(gu_full[0], i + 1)
                        if i >= 2:
                            act.wait_ge(hh_in[0], i - 1)
                        act.activation(sg[:, i % 2, 0:SLOTS], bank(2 + 2 * (i % 2))[:, 0:SLOTS],
                                       ACT.Silu).then_inc(sg_in[0], 1)
                        if f >= 1 and e + 1 < E:
                            take_weights(e + 1, f - 1)
                        if f == DOWN_AFTER + 1 and e > 0:
                            take_down(e - 1)
                take_down(E - 1)

            def dense_experts():
                take_ht(3)
                act.activation(table[:, :], half_neg[:, 0:1], ACT.Silu)
                for i in range(len(UNITS1)):
                    act.wait_ge(gu_full[1], i + 1)
                    if i >= 2:
                        act.wait_ge(hh_in[1], i - 1)
                    act.activation(sg[:, i % 2, :], bank(2 + 2 * (i % 2)), ACT.Silu).then_inc(sg_in[1], 1)
                    if i == WEIGH_AFTER:
                        weigh(1)

            take_ht(1)
            for j in range(3):
                take_weights(0, j)
            weigh(0)
            for j in range(2 * B):
                act.wait_ge(kv1_full, j + 1)
                src = bank(KV1_BANK[j])
                if j < B:
                    act.activation(k1_t[:, j * BANK:(j + 1) * BANK], src, ACT.Copy).then_inc(kv1_act, 1)
                else:
                    dst = v1[:, CT * (j - B):CT * (j - B + 1), :]
                    act.activation(dst, src.rearrange("p (t d) -> p t d", t=CT), ACT.Copy).then_inc(kv1_act, 1)
            routed_experts()
            act.activation(table[:, :], half_neg[:, 0:1], ACT.Exp)
            for e in range(E):
                act.wait_ge(tr_full[1], e + 1)
                act.activation(w1_t[:, e], bank(e % 2)[:, 0:3 * P].rearrange("p (m f) -> p m f", m=3),
                               ACT.Copy).then_inc(wt_in[1], 1)
            take_ht(2)
            for s in range(NHT):
                act.wait_ge(q1_full, s + 1)
                act.activation(q1_t[:, s, :], bank(4 + s), ACT.Identity,
                               bias=b1_col[:, :]).then_inc(q1_act, 1)
            for t in range(NT):
                act.wait_ge(nm1_in, t + 1)
                if t >= 2:
                    act.wait_ge(p1t_full, t - 1)
                act.activation(p1[:, t % 2, :], bank(t % 2), ACT.Exp, bias=s1_nmax[:, t:t + 1],
                               accum_out=s1_sum[:, t:t + 1]).then_inc(p1_in, 1)
            dense_experts()

        @block.vector
        def _(dve):
            link = linker(dve, dve_step)

            def permute_weights():
                dve.wait_ge(in_w, 16 * N_IN_W)
                for dst, src in ((w_perm[:, 0, :], w_q), (w_perm[:, 1, :], w_cq), (w_perm[:, 2, :], w_k),
                                 (w_perm[0:DC + 1, 3, :], w_ck), (b_perm[:, :], b_rows)):
                    dve.tensor_copy(dst.rearrange("k (par d pair) -> k par d pair", pair=PAIR, par=PAR),
                                    src[:, :].rearrange("k (pair par d) -> k par d pair", pair=PAIR, par=PAR))\
                       .then_inc(perm_in, 1)

            def halves(s):
                return range(s * TPH, (s + 1) * TPH)

            def statistics(i, s, x):
                for t in halves(s):
                    ins = dve.bn_stats(ln_stats[:, t, :], x[:, t, :])
                link(ins)
                for t in halves(s):
                    dve.bn_aggr(ln_mv[:, t, :], ln_stats[:, t, :]).then_inc(stats_in[i], 1)

            def normalise(i, s, x):
                dve.wait_ge(rstd_in[i], s + 1)
                for t in halves(s):
                    dve.tensor_scalar(h_sb[:, t, :], x[:, t, :], ln_mv[:, t, 0:1], ln_rstd[:, t:t + 1],
                                      ALU.subtract, ALU.mult).then_inc(h_in[i], 1)

            dve.memset(qcat[:, 0], 0.0).then_inc(zero_in[0], 1)
            dve.wait_ge(in_x, 16)
            for s in range(NHT):
                statistics(0, s, x_sb)
            permute_weights()
            for s in range(NHT):
                normalise(0, s, x_sb)

            def split(b, first, end, last):
                cols = slice(first, end)
                link(dve.tensor_copy(parts[:, b, 0, cols], qk[:, b, cols]))
                ins = dve.tensor_tensor(qk_r[:, b, cols], qk[:, b, cols], parts[:, b, 0, cols], ALU.subtract)
                if last:
                    ins.then_inc(rest_in, 1)
                    dve.wait_ge(rest_in, b + 1)
                else:
                    link(ins)
                link(dve.tensor_copy(parts[:, b, 1, cols], qk_r[:, b, cols]))
                ins = dve.tensor_tensor(parts[:, b, 2, cols], qk_r[:, b, cols], parts[:, b, 1, cols], ALU.subtract)
                if last:
                    ins.then_inc(parts_in, 1)

            dve.wait_ge(job_act, taken_count(job_at("ck", 0)))
            split(0, QW + S, XW, False)
            dve.wait_ge(job_act, taken_count(job_at("k", 0)))
            split(0, 0, QW + S, True)
            dve.memset(qcat[:, 1], 0.0).then_inc(zero_in[1], 1)
            for b in range(1, SPLIT_DVE):
                dve.wait_ge(job_act, taken_count(job_at("ck", b)))
                split(b, 0, XW, True)

            def split_max(n):
                dve.wait_ge(s1_free, split_after[n] + 1)
                whole = nmax[:, n % 2].rearrange("p t k (r q) -> p t (k r) q", q=PP)
                part = [nmax_p[:, n % 2, :, :, i, :] for i in range(3)]
                link(dve.tensor_copy(part[0], whole))
                link(dve.tensor_tensor(nmax_r[:, :, :, :], whole, part[0], ALU.subtract))
                link(dve.tensor_copy(part[1], nmax_r[:, :, :, :]))
                dve.tensor_tensor(part[2], nmax_r[:, :, :, :], part[1], ALU.subtract).then_inc(split_in, 1)

            def take_sums(n):
                dve.wait_ge(o_full, n + 1)
                if n >= 2:
                    dve.wait_ge(y_in, n - 1)
                dve.tensor_copy(o_sb[:, n % 2], bank(OT_BANK).rearrange("p (k h c) -> p k h c", k=2 * QT, h=QUAD)
                                [:, :, :, 0:HA]).then_inc(o_taken, 1)
                dve.wait_ge(o_taken, n + 1)
                dve.reciprocal(o_rec[:, n % 2].rearrange("p k h -> p (k h)"),
                               o_sb[:, n % 2].rearrange("p k h d -> p (k h) d")[:, :, HD]).then_inc(rec_in, 1)

            sums_after = {}
            for n in range(NHEAD // QUAD):
                at = min(pass1_before(3 * QUAD * (n + 2) + 3) + 1, len(pass1) - 1)
                sums_after.setdefault(at, []).append(n)
            for i, u in enumerate(pass1):
                dve.wait_ge(s1_full, i + 1)
                src = bank(2 * (i % 2), 2)
                if u[0] == "turn":
                    if u[1] >= 2:
                        dve.wait_ge(mrow_in[u[1] - 2], 16 * 2 * PAR)
                    dve.tensor_copy(nmax_t[:, u[1] % 2, :],
                                    src[0:2 * PAR * 3 * PP, 0:S // 2].bitcast(BF16)).then_inc(s1_free, 1)
                else:
                    kind, b, t, g = u
                    n = {"cross": 1, "late": 2, "early": 4}[kind]
                    g %= PP // n
                    dst = nmax[:, b % 2, t, int(kind == "cross"), :].rearrange("p (r q) -> p r q", r=PAR)
                    dve.tensor_reduce(dst[:, :, n * g:n * (g + 1)],
                                      src.rearrange("p (r q k) -> p r q k", r=PAR, q=n),
                                      AX.X, ALU.max, negate=True).then_inc(s1_free, 1)
                    if i == split_after[b]:
                        split_max(b)
                if i == 1:
                    dve.memset(bank(O_BANK), 0.0).then_inc(o_clear, 1)
                for n in sums_after.get(i, ()):
                    take_sums(n)

            dve.wait_ge(yt_full, 2)
            dve.tensor_copy(y_t[:, BANK:TOK], bank(1)).then_inc(yt_dve, 1)
            dve.wait_ge(gw_full, 1)
            dve.tensor_copy(gw_t[:, :, :], bank(4)[:, 0:2 * E].rearrange("p (l e) -> p l e", l=2))
            dve.tensor_copy(b1_col[:, :], bank(4)[:, 2 * E:2 * E + 1]).then_inc(gw_in, 1)
            dve.wait_ge(xb_in, 1)
            for s in range(NHT):
                half = x1_sb[:, s * TPH:(s + 1) * TPH, :].rearrange("p t d -> p (t d)")
                dve.wait_ge(proj_full, s + 1)
                dve.scalar_tensor_tensor(out=half, in0=bank(2 + s), scalar=tanh_g[:, 0:1], in1=half,
                                         op0=ALU.mult, op1=ALU.add).then_inc(x1_in, 1)

            def take_ht(i):
                dve.wait_ge(ht_full[i], 2)
                dve.tensor_copy(h_t[:, BANK:TOK], bank(1)).then_inc(ht_dve[i], 1)

            def choose(layer):
                dve.wait_ge(lg_full[layer], 1)
                src = bank(LG_BANK[layer])[:, 0:NT * E].rearrange("p (t e) -> p t e", t=NT)
                if layer == 0:
                    link(dve.tensor_copy(lg[:, :, :], src))
                else:
                    link(dve.tensor_tensor(lg[:, :, :], src, b_g[:, :].unsqueeze(1).to_broadcast([P, NT, E]), ALU.add))
                for t in range(NT):
                    ins = dve.max(top[:, t, :], lg[:, t, :])
                link(ins)
                dve.tensor_tensor(gap[:, :], top[:, :, 1], top[:, :, 0], ALU.subtract).then_inc(gap_in[layer], 1)
                for t in range(NT):
                    ins = dve.max_index(top_i[:, t, :], top[:, t, :], lg[:, t, :])
                link(ins)
                link(dve.tensor_copy(top_f[:, :, :], top_i[:, :, 0:2].rearrange("p t k -> p k t")))
                link(dve.tensor_tensor(pick[:, :, :, :].rearrange("p k t e -> p (k t) e"),
                                       iota_e[:, :].unsqueeze(1).to_broadcast([P, 2 * NT, E]),
                                       top_f[:, :, :].rearrange("p k t -> p (k t)").unsqueeze(2)
                                       .to_broadcast([P, 2 * NT, E]), ALU.is_equal))
                if layer == 0:
                    dve.tensor_copy(pick_b[:, :, :, :], pick[:, :, :, :]).then_inc(pick_in, 1)
            def weigh(layer):
                dve.wait_ge(e_gap_in[layer], 1)
                link(dve.tensor_scalar(w_top[:, 1, :], e_gap[:, :], 1.0, None, ALU.add))
                link(dve.reciprocal(w_top[:, 0, :], w_top[:, 1, :]))
                link(dve.tensor_tensor(w_top[:, 1, :], w_top[:, 0, :], e_gap[:, :], ALU.mult))

            def combine():
                link(dve.tensor_tensor(pick[:, :, :, :].rearrange("p k t e -> p (k t) e"),
                                       pick[:, :, :, :].rearrange("p k t e -> p (k t) e"),
                                       w_top[:, :, :].rearrange("p k t -> p (k t)").unsqueeze(2)
                                       .to_broadcast([P, 2 * NT, E]), ALU.mult))
                link(dve.tensor_tensor(comb[:, :, :], pick[:, 0, :, :], pick[:, 1, :, :], ALU.add))

            def flat(x):
                return x[:, :, :].rearrange("p k t -> p (k t)")

            def route():
                link(dve.scalar_tensor_tensor(out=flat(slot_base), in0=flat(top_f), scalar=float(SLOTS),
                                              in1=flat(slot_base), op0=ALU.mult, op1=ALU.add))
                dve.wait_ge(count_full, 1)
                link(dve.tensor_tensor(chosen[:, :, :, :].rearrange("p k t e -> p (k t e)"),
                                       bank(7)[:, 0:2 * NT * E],
                                       pick[:, :, :, :].rearrange("p k t e -> p (k t e)"), ALU.mult))
                link(dve.tensor_reduce(flat(cnt), chosen[:, :, :, :].rearrange("p k t e -> p (k t) e"),
                                       AX.X, ALU.add))
                dve.tensor_scalar(flat(valid), flat(cnt), float(CAPACITY) + 0.5, None, ALU.is_le)
                link(dve.tensor_tensor(flat(slot), flat(slot_base), flat(cnt), ALU.add))
                link(dve.scalar_tensor_tensor(out=flat(put_f), in0=flat(valid), scalar=-FAR, in1=flat(slot),
                                              op0=ALU.mult, op1=ALU.add))
                link(dve.tensor_scalar(flat(put_f), flat(put_f), FAR, None, ALU.add))
                dve.tensor_copy(flat(put_at), flat(put_f)).then_inc(put_in, 1)
                weigh(0)
                link(dve.tensor_tensor(flat(w_top), flat(w_top), flat(valid), ALU.mult))
                link(dve.tensor_scalar(flat(w_top), flat(w_top), tanh_g[:, 2:3], None, ALU.mult))

            def ways_back():
                for e in range(E):
                    dve.wait_ge(xs_in[e], 16)
                number = xs[0:MT, :, :, D]
                link(dve.tensor_scalar(back_f[0:MT], number, 0.0, FAR, ALU.is_equal, ALU.mult))
                link(dve.tensor_tensor(back_f[0:MT], back_f[0:MT], number, ALU.add))
                link(dve.tensor_tensor(back_f[0:MT], back_f[0:MT],
                                       rank_off[0:MT, :].unsqueeze(1).to_broadcast([MT, E, 3]), ALU.add))
                dve.tensor_copy(back_at[0:MT], back_f[0:MT]).then_inc(back_in, 1)

            def routed_experts():
                def take_rows(e):
                    dve.wait_ge(xt_full, e + 1)
                    dve.tensor_copy(xs_t[:, e % 2, :], bank(7)[:, 0:SLOTS]).then_inc(xt_in, 1)

                take_rows(0)
                for e in range(E):
                    for f in range(NF0):
                        i = NF0 * e + f
                        dve.wait_ge(sg_in[0], i + 1)
                        if f == 0 and e >= 2:
                            dve.wait_ge(dn_full[0], e - 1)
                        dve.tensor_tensor(hh[:, e % 2, f, 0:SLOTS], bank(3 + 2 * (i % 2))[:, 0:SLOTS],
                                          sg[:, i % 2, 0:SLOTS], ALU.mult).then_inc(hh_in[0], 1)
                        if f == 2 and e + 1 < E:
                            take_rows(e + 1)
                    if e == 0:
                        ways_back()
                for s in range(NHT):
                    dve.wait_ge(got_in[s], 16 * 2)
                    for t in halves(s):
                        ins = dve.scalar_tensor_tensor(out=x_sb[:, t, :], in0=got[:, 0, t, :],
                                                       scalar=w_top[:, 0, t:t + 1], in1=x1_sb[:, t, :],
                                                       op0=ALU.mult, op1=ALU.add)
                    link(ins)
                    for t in halves(s):
                        ins = dve.scalar_tensor_tensor(out=x_sb[:, t, :], in0=got[:, 1, t, :],
                                                       scalar=w_top[:, 1, t:t + 1], in1=x_sb[:, t, :],
                                                       op0=ALU.mult, op1=ALU.add)
                    link(ins)
                    statistics(2, s, x_sb)

            def dense_experts():
                def take_down(n):
                    s, e = UNITS1[n]
                    dve.wait_ge(dn_full[1], n + 1)
                    if e > 0:
                        dve.wait_ge(dn_taken[1], n)
                    for t in range(TPH):
                        src, dst = bank(DN_BANK[n % 4])[:, t * P:(t + 1) * P], acc[:, s * TPH + t, :]
                        weight = comb[:, s * TPH + t, e:e + 1]
                        if e == 0:
                            ins = dve.tensor_scalar(dst, src, weight, None, ALU.mult)
                        else:
                            ins = dve.scalar_tensor_tensor(out=dst, in0=src, scalar=weight, in1=dst,
                                                           op0=ALU.mult, op1=ALU.add)
                    ins.then_inc(dn_taken[1], 1)
                    if e == E - 1:
                        dve.wait_ge(dn_taken[1], n + 1)
                        half = slice(s * TPH, (s + 1) * TPH)
                        whole = "p t d -> p (t d)"
                        dve.scalar_tensor_tensor(out=x_sb[:, half, :].rearrange(whole),
                                                 in0=acc[:, half, :].rearrange(whole), scalar=tanh_g[:, 3:4],
                                                 in1=x1_sb[:, half, :].rearrange(whole),
                                                 op0=ALU.mult, op1=ALU.add).then_inc(x4_in, 1)

                for i in range(len(UNITS1)):
                    dve.wait_ge(sg_in[1], i + 1)
                    if i >= 2:
                        dve.wait_ge(dn_full[1], i - 1)
                    dve.tensor_tensor(hh[:, i % 2, 0, :], bank(3 + 2 * (i % 2)), sg[:, i % 2, :],
                                      ALU.mult).then_inc(hh_in[1], 1)
                    if i == HALF_AFTER - 1:
                        normalise(3, 1, x1_sb)
                    if i == HALF_AFTER:
                        take_ht(3)
                    if i == CHOOSE_AFTER:
                        choose(1)
                    if i == WEIGH_AFTER:
                        weigh(1)
                        combine()
                    for n in range(taken_after(i - 1), taken_after(i)):
                        take_down(n)
                take_down(len(UNITS1) - 1)

            for s in range(NHT):
                dve.wait_ge(x1_in, s + 1)
                statistics(1, s, x1_sb)
            for s in range(NHT):
                normalise(1, s, x1_sb)
            take_ht(1)
            choose(0)
            route()
            routed_experts()

            for s in range(NHT):
                normalise(2, s, x_sb)
            take_ht(2)

            def max1(t):
                dve.wait_ge(sc1_full, t + 1)
                dve.tensor_reduce(s1_nmax[:, t:t + 1], bank(t % 2), AX.X, ALU.max, negate=True).then_inc(nm1_in, 1)

            def add_values(t):
                dve.wait_ge(o1_full, t + 1)
                dve.scalar_tensor_tensor(out=x1_sb[:, t, :], in0=bank(4 + t % 2)[:, 0:D], scalar=s1_rec[:, t:t + 1],
                                         in1=x_sb[:, t, :], op0=ALU.mult, op1=ALU.add).then_inc(x3_in, 1)
                if t % TPH == TPH - 1:
                    dve.wait_ge(x3_in, t + 1)
                    statistics(3, t // TPH, x1_sb)

            max1(0)
            for t in range(NT):
                if t + 1 < NT:
                    max1(t + 1)
                dve.wait_ge(p1t_full, t + 1)
                if t >= 2:
                    dve.wait_ge(o1_full, t - 1)
                dve.tensor_copy(p1_t[:, t % 2, :], bank(2 + t % 2)).then_inc(p1t_in, 1)
                link(dve.reciprocal(s1_rec[:, t:t + 1], s1_sum[:, t:t + 1]))
                link(dve.tensor_tensor(s1_rec[:, t:t + 1], s1_rec[:, t:t + 1], tanh_g[:, 1:2], ALU.mult))
                if t >= 1:
                    add_values(t - 1)
                if t == NT - 2:
                    normalise(3, 0, x1_sb)
            add_values(NT - 1)

            dense_experts()

        @block.tensor
        def _(pe):
            pe.wait_ge(consts, 4)
            for j, (kind, i, engine) in enumerate(jobs):
                if j >= 8:
                    wait_taken(pe, j - 8)
                dst = bank(j % 8)
                if kind == "xt":
                    for t in range(4 * i, 4 * i + 4):
                        pe.wait_ge(h_in[0], t + 1)
                        ins = pe.transpose(dst[:, (t % 4) * P:(t % 4 + 1) * P], h_sb[:, t, :], ident[:, :])
                elif kind == "ct":
                    pe.wait_ge(in_ctx, 16)
                    for t in range(4 * i, 4 * i + 4):
                        ins = pe.transpose(dst[0:DC, (t % 4) * P:(t % 4 + 1) * P], c_sb[:, t, :], ident[:, :])
                elif kind == "bias":
                    pe.wait_ge(in_w, 16 * N_IN_W)
                    pe.wait_ge(perm_in, 5)
                    ins = pe.transpose(dst[:, 0:3], b_perm[:, :], ident[0:3, 0:3])
                elif kind == "q":
                    if i % 2 == 0:
                        wait_taken(pe, job_at("xt", i // 2))
                    for c in range(2):
                        ins = pe.matmul(dst[:, c * S:(c + 1) * S], w_perm[:, c, :],
                                        h_t[:, i * S:(i + 1) * S], start=True, stop=True)
                elif kind == "k":
                    ins = pe.matmul(dst[:, 0:S], w_perm[:, 2, :],
                                    h_t[:, i * S:(i + 1) * S], start=True, stop=True)
                elif kind == "ck":
                    if i == 0:
                        for k in range(NC // 4):
                            wait_taken(pe, job_at("ct", k))
                    ins = pe.matmul(dst, w_perm[0:DC + 1, 3, :],
                                    c_t[:, i * SC:(i + 1) * SC], start=True, stop=True)
                elif kind == "v":
                    for t in range(QT):
                        tok = (QT * i + t) * P
                        pe.matmul(dst[:, t * P:(t + 1) * P], h_t[:, tok:tok + P], w_v[:, :],
                                  start=True, stop=False)
                        ins = pe.matmul(dst[:, t * P:(t + 1) * P], c_t[DC:DC + 1, 0:P], b_v[DC:DC + 1, :],
                                        start=False, stop=True)
                else:
                    for t in range(CT):
                        tok = (CT * i + t) * P
                        ins = pe.matmul(dst[:, t * P:(t + 1) * P], c_t[:, tok:tok + P], w_cv[:, :],
                                        start=True, stop=True)
                ins.then_inc(job_done, 1)
            for j in range(len(jobs) - 8, len(jobs)):
                wait_taken(pe, j)

            def masked_scores(dst, q, k, width):
                pe.matmul(dst, q, k, start=True, stop=False, skip_group_check=True)
                return pe.matmul(dst[:, width - P:width], ident_b[:, :], mask_b[:, :], start=False, stop=True,
                                 skip_group_check=True)

            def pass1_unit(i):
                u = pass1[i]
                if i >= 2:
                    pe.wait_ge(s1_free, i - 1)
                first = 2 * (i % 2)
                if u[0] == "turn":
                    pe.wait_ge(split_in, u[1] + 1)
                    for t in range(QT):
                        dst = bank(first)[0:2 * PAR * 3 * PP, t * P // 2:(t + 1) * P // 2].bitcast(BF16)
                        src = nmax_p[:, u[1] % 2, t].rearrange("p k c q -> p (k c q)")
                        ins = pe.transpose(dst, src, ident_b[:, :])
                    ins.then_inc(s1_full, 1)
                    return
                kind, part, t, g = u
                b = part // 2
                if kind == "cross" and t == 0 and g == 0:
                    wait_laid(pe, b)
                    if b < RING:
                        pe.wait_ge(ones_in[b], 16 * PAR)
                for par in range(PAR):
                    q, k = qcat[:, b % RING, par], kcat[:, b % RING]
                    dst = bank(first + par)
                    if kind == "cross":
                        ins = pe.matmul(dst, q[:, g, S + t * P:S + (t + 1) * P], k[:, g, S:KW],
                                        start=True, stop=True)
                    elif kind == "late":
                        for n in range(2):
                            ins = masked_scores(dst[:, n * S:(n + 1) * S], q[:, 2 * g + n, P:S],
                                                k[:, 2 * g + n, 0:S], S)
                    else:
                        for n in range(4):
                            ins = masked_scores(dst[:, n * P:(n + 1) * P], q[:, 4 * g + n, 0:P],
                                                k[:, 4 * g + n, 0:P], P)
                ins.then_inc(s1_full, 1)

            def scores2(head, part):
                b, h = head // H, head % H
                u = 3 * head + part
                if u >= 2:
                    pe.wait_ge(p_in, u - 1)
                if head % (H // 2) == 0 and part == 0:
                    pe.wait_ge(mrow_in[head // (H // 2)], 16 * 2 * PAR)
                dst, q, k = bank(4 + u % 2), qcat[:, b % RING, h % 2, h // 2, :], kcat[:, b % RING, h // 2, :]
                if part == 0:
                    pe.matmul(dst[:, 0:S], k[:, 0:P], q[:, 0:S], start=True, stop=True)
                    ins = pe.matmul(dst[:, S:S + P], k[:, P:S], q[:, P:S], start=True, stop=True)
                else:
                    for c in range(2):
                        key = S + (2 * (part - 1) + c) * P
                        ins = pe.matmul(dst[:, c * S:(c + 1) * S], k[:, key:key + P], q[:, S:QW],
                                        start=True, stop=True)
                ins.then_inc(s2_full, 1)

            def values(n, r):
                if r == 0:
                    if n >= 1:
                        pe.wait_ge(ot_in, n)
                    else:
                        pe.wait_ge(o_clear, 1)
                    pe.wait_ge(masked, QUAD * (n + 1))
                if r == 2:
                    pe.wait_ge(p_in, 3 * QUAD * (n + 1))
                for j in range(QUAD):
                    head = QUAD * n + j
                    b, h = head // H, head % H
                    if r < 2:
                        p = p_slots[(3 * head) % NPT][:, (0 if r == 0 else S):(S if r == 0 else S + P)]
                        cols, v = slice(r * P, S), QT * b + r
                    else:
                        c = r - 2
                        p = p_slots[(3 * head + 1 + c // 2) % NPT][:, (c % 2) * S:(c % 2 + 1) * S]
                        cols, v = slice(S, 2 * S), NT + CT * b + c
                    ins = pe.matmul(bank(O_BANK)[32 * j:32 * j + HA, cols], v_aug[:, v, h, :], p,
                                    start=r in (0, 2), stop=r in (1, ROUNDS - 1), skip_group_check=True)
                if r == ROUNDS - 1:
                    ins.then_inc(pv_done, 1)

            def turn_values(n):
                pe.wait_ge(ot_in, n + 1)
                if n >= 1:
                    pe.wait_ge(o_taken, n)
                for k in range(2 * QT):
                    ins = pe.transpose(bank(OT_BANK)[:, k * P:(k + 1) * P], ot_sb[:, k * P:(k + 1) * P], ident[:, :])
                ins.then_inc(o_full, 1)

            ROUNDS = 2 + CT
            ROUND_AT = (2, 4, 6, 8, 10, 11)
            NG = NHEAD // QUAD
            pe.wait_ge(consts, N_CONSTS)
            done = 0
            for u in range(3 * QUAD * (NG + 1)):
                n, k = u // (3 * QUAD), u % (3 * QUAD)
                while done < pass1_before(u):
                    pass1_unit(done)
                    done += 1
                if n < NG:
                    scores2(u // 3, u % 3)
                if n >= 2 and k == 3:
                    turn_values(n - 2)
                if n >= 1 and k in ROUND_AT:
                    values(n - 1, ROUND_AT.index(k))
            turn_values(NG - 1)

            pe.wait_ge(in_late, 16 * N_IN_LATE)
            pe.wait_ge(p_in, 3 * NHEAD)
            for layer in range(2):
                pe.transpose(bank(4)[:, layer * E:(layer + 1) * E], gw_rows[:, layer, :], ident[0:E, 0:E])
            pe.transpose(bank(4)[:, 2 * E:2 * E + 1], b1_row[:, :], ident[0:1, 0:1]).then_inc(gw_full, 1)

            pe.wait_ge(s1_free, len(pass1))
            for s in range(NHT):
                for t in range(TPH):
                    pe.wait_ge(y_in, H // QUAD * ((s * TPH + t) // QT + 1))
                    ins = pe.transpose(bank(s)[:, t * P:(t + 1) * P], y_sb[:, s * TPH + t, :], ident[:, :])
                ins.then_inc(yt_full, 1)
            for s in range(NHT):
                pe.wait_ge([yt_act, yt_dve][s], 1)
                for t in range(TPH):
                    tok = (s * TPH + t) * P
                    ins = pe.matmul(bank(2 + s)[:, t * P:(t + 1) * P], y_t[:, tok:tok + P], w_p[:, :],
                                    start=True, stop=True)
                ins.then_inc(proj_full, 1)

            def transpose_half(i, s):
                for t in range(TPH):
                    pe.wait_ge(h_in[i], s * TPH + t + 1)
                    ins = pe.transpose(bank(s)[:, t * P:(t + 1) * P], h_sb[:, s * TPH + t, :], ident[:, :])
                ins.then_inc(ht_full[i], 1)

            def transpose_h(i):
                for s in range(NHT):
                    transpose_half(i, s)

            def router(layer):
                pe.wait_ge(gw_in, 1)
                for t in range(NT):
                    pe.wait_ge((ht_act if t < TPH else ht_dve)[1 + 2 * layer], 1)
                    ins = pe.matmul(bank(LG_BANK[layer])[:, t * E:(t + 1) * E], h_t[:, t * P:(t + 1) * P], gw_t[:, layer, :],
                                    start=True, stop=True)
                ins.then_inc(lg_full[layer], 1)

            def transpose_weights(e, j):
                k = 3 * e + j
                if j == 0:
                    pe.wait_ge(raw_in[e % NRAW], 48 * (e // NRAW + 1))
                if k >= 2:
                    pe.wait_ge(wt_in[0], k - 1)
                for f in range(NF0):
                    ins = pe.transpose(bank(k % 2)[:, f * P:(f + 1) * P], raw[:, e % NRAW, j, f, :], ident[:, :])
                ins.then_inc(tr_full[0], 1)

            def routed_experts():
                def transpose_rows(e):
                    pe.wait_ge(xs_in[e], 16)
                    if e > 0:
                        pe.wait_ge(xt_in, e)
                    for t in range(3):
                        ins = pe.transpose(bank(7)[:, t * MT:(t + 1) * MT], xs[0:MT, e, t, 0:D], ident[0:MT, 0:MT])
                    ins.then_inc(xt_full, 1)

                def go_down(e):
                    pe.wait_ge(wt_in[0], 3 * (e + 1))
                    pe.wait_ge(hh_in[0], NF0 * (e + 1))
                    if e > 0:
                        pe.wait_ge(dn_taken[0], e)
                    for t in range(3):
                        for f in range(NF0):
                            ins = pe.matmul(bank(6)[0:MT, t * D:(t + 1) * D], hh[:, e % 2, f, t * MT:(t + 1) * MT],
                                            w_t[:, e % 2, 2, f * P:(f + 1) * P], start=(f == 0), stop=(f == NF0 - 1))
                    ins.then_inc(dn_full[0], 1)

                transpose_rows(0)
                for e in range(E):
                    for f in range(NF0):
                        i = NF0 * e + f
                        if f == 0:
                            pe.wait_ge(wt_in[0], 3 * e + 2)
                            pe.wait_ge(xt_in, e + 1)
                        if i >= 2:
                            pe.wait_ge(hh_in[0], i - 1)
                        for m in range(2):
                            ins = pe.matmul(bank(2 + 2 * (i % 2) + m)[:, 0:SLOTS], w_t[:, e % 2, m, f * P:(f + 1) * P],
                                            xs_t[:, e % 2, :], start=True, stop=True)
                        ins.then_inc(gu_full[0], 1)
                        if f == DOWN_AFTER and e > 0:
                            go_down(e - 1)
                        if f == 2 and e + 1 < E:
                            transpose_rows(e + 1)
                        if f >= 1 and e + 1 < E:
                            transpose_weights(e + 1, f - 1)
                go_down(E - 1)

            def dense_experts():
                transpose_half(3, 0)

                def go_down(n):
                    s, e = UNITS1[n]
                    pe.wait_ge(hh_in[1], n + 1)
                    if n >= 4:
                        pe.wait_ge(dn_taken[1], n - 3)
                    for t in range(TPH):
                        ins = pe.matmul(bank(DN_BANK[n % 4])[:, t * P:(t + 1) * P], hh[:, n % 2, 0, t * P:(t + 1) * P],
                                        w1_t[:, e, 2, :], start=True, stop=True)
                    ins.then_inc(dn_full[1], 1)

                for i, (s, e) in enumerate(UNITS1):
                    if e == 0:
                        pe.wait_ge([ht_act, ht_dve][s][3], 1)
                    if i == 1:
                        pe.wait_ge(x3_in, NT)
                    if i >= 2:
                        pe.wait_ge(hh_in[1], i - 1)
                    for m in range(2):
                        ins = pe.matmul(bank(2 + 2 * (i % 2) + m), w1_t[:, e, m, :],
                                        h_t[:, s * BANK:(s + 1) * BANK], start=True, stop=True)
                    ins.then_inc(gu_full[1], 1)
                    if i == HALF_AFTER:
                        transpose_half(3, 1)
                        router(1)
                    elif i == HALF_AFTER + 1:
                        for n in range(i):
                            go_down(n)
                    elif i > HALF_AFTER + 1:
                        go_down(i - 1)
                go_down(len(UNITS1) - 1)

            transpose_h(1)
            router(0)
            for j in range(3):
                transpose_weights(0, j)

            def context(j):
                if j >= 4:
                    pe.wait_ge(kv1_act, j - 3)
                dst = bank(KV1_BANK[j])
                if j < B:
                    ins = pe.matmul(dst, w1_k[:, :], c_t[:, j * SC:(j + 1) * SC], start=True, stop=True)
                else:
                    for c in range(CT):
                        tok = (CT * (j - B) + c) * P
                        ins = pe.matmul(dst[:, c * P:(c + 1) * P], c_t[:, tok:tok + P], w1_v[:, :],
                                        start=True, stop=True)
                ins.then_inc(kv1_full, 1)

            pe.wait_ge(pick_in, 1)
            dst = bank(7)[:, 0:2 * NT * E].rearrange("p (k t e) -> p k t e", k=2, t=NT)
            pe.matmul(dst, upto_b[:, :], pick_b[:, :, :, :], start=True, stop=False, skip_group_check=True)
            for d in range(1, NT):
                ins = pe.matmul(dst[:, :, d:NT, :], ones_b[:, 0:P], pick_b[:, :, 0:NT - d, :],
                                start=False, stop=(d == NT - 1), skip_group_check=True)
            ins.then_inc(count_full, 1)
            for j in range(2 * B):
                context(j)
            pe.wait_ge(kv1_act, 2 * B)
            routed_experts()

            pe.wait_ge(raw1_in, 16 * 3)
            for e in range(E):
                if e >= 2:
                    pe.wait_ge(wt_in[1], e - 1)
                for m in range(3):
                    ins = pe.transpose(bank(e % 2)[:, m * P:(m + 1) * P], raw1[:, e, m, :], ident[:, :])
                ins.then_inc(tr_full[1], 1)
            pe.wait_ge(wt_in[1], E)
            transpose_h(2)
            pe.wait_ge(kv1_act, 2 * B)
            for s in range(NHT):
                pe.wait_ge([ht_act, ht_dve][s][2], 1)
                pe.matmul(bank(4 + s), w1_q[:, :], h_t[:, s * BANK:(s + 1) * BANK],
                          start=True, stop=True).then_inc(q1_full, 1)

            def scores1(t):
                pe.wait_ge(q1_act, t // TPH + 1)
                if t >= 2:
                    pe.wait_ge(p1_in, t - 1)
                b = t // QT
                pe.matmul(bank(t % 2), q1_t[:, t // TPH, t % TPH * P:(t % TPH + 1) * P], k1_t[:, b * SC:(b + 1) * SC],
                          start=True, stop=True).then_inc(sc1_full, 1)

            def values1(t):
                pe.wait_ge(p1t_in, t + 1)
                if t < NHT:
                    pe.wait_ge(q1_act, t + 1)
                if t >= 2:
                    pe.wait_ge(x3_in, t - 1)
                for c in range(CT):
                    ins = pe.matmul(bank(4 + t % 2)[:, 0:D], p1_t[:, t % 2, c * P:(c + 1) * P], v1[:, CT * (t // QT) + c, :],
                                    start=(c == 0), stop=(c == CT - 1))
                ins.then_inc(o1_full, 1)

            scores1(0)
            for t in range(NT):
                if t + 1 < NT:
                    scores1(t + 1)
                pe.wait_ge(p1_in, t + 1)
                if t >= 2:
                    pe.wait_ge(p1t_in, t - 1)
                for c in range(CT):
                    ins = pe.transpose(bank(2 + t % 2)[:, c * P:(c + 1) * P], p1[:, t % 2, c * P:(c + 1) * P], ident[:, :])
                ins.then_inc(p1t_full, 1)
                if t >= 1:
                    values1(t - 1)
            values1(NT - 1)
            dense_experts()


_INS = ['x', 'ctx_512', 'g_xattn', 'g_ffn', 'L0_xattn_Wk', 'L0_xattn_bk', 'L0_xattn_Wq', 'L0_xattn_bq', 'L0_xattn_Wv',
        'L0_xattn_bv', 'L0_xattn_Wck', 'L0_xattn_bck', 'L0_xattn_Wcq', 'L0_xattn_bcq', 'L0_xattn_Wcv', 'L0_xattn_bcv',
        'L0_xattn_Wp', 'L0_xattn_bp', 'L0_ffn_gate_w', 'L0_ffn_wi_gate', 'L0_ffn_wi_up', 'L0_ffn_wo', 'L1_xattn_Wq',
        'L1_xattn_bq', 'L1_xattn_Wk', 'L1_xattn_bk', 'L1_xattn_Wv', 'L1_xattn_bv', 'L1_ffn_Wg', 'L1_ffn_bg',
        'L1_ffn_w1', 'L1_ffn_w2']


def kernel(**inputs):
    import numpy as _np
    import concourse.bacc as _bacc
    from concourse import mybir as _mybir
    from concourse.bass_utils import run_bass_kernel_spmd as _run

    nc = _bacc.Bacc("TRN2", target_bir_lowering=False, num_devices=1)
    arrays, aps = {}, {}
    for name in _INS:
        arr = _np.ascontiguousarray(inputs[name])
        arrays[f"in_{name}_dram"] = arr
        aps[name] = nc.dram_tensor(f"in_{name}_dram", arr.shape, _mybir.dt.from_np(arr.dtype),
                                   kind="ExternalInput").ap()
    out = nc.dram_tensor("out_0_dram", inputs["x"].shape, _mybir.dt.float32, kind="ExternalOutput").ap()
    flamingo_gated_kernel(nc, aps, out)
    r = _run(nc, [arrays], core_ids=[0])
    return r.results[0]["out_0_dram"]
```
